# Optimizing a Trainium2 kernel written in Bass

```python
import numpy as np
import jax
import jax.numpy as jnp

def _softmax(x, axis=-1):
    return jax.nn.softmax(x, axis=axis)

def _gelu(x):
    return jax.nn.gelu(x, approximate=True)

def _silu(x):
    return jax.nn.silu(x)

def _sigmoid(x):
    return jax.nn.sigmoid(x)

def _layernorm(x, axis=-1, eps=1e-05):
    m = jnp.mean(x, axis=axis, keepdims=True)
    v = jnp.var(x, axis=axis, keepdims=True)
    return (x - m) / jnp.sqrt(v + eps)

def _scatter_add(tgt, idx, src, axis=0):
    return tgt.at[idx].add(src)

def _segment_sum(src, seg, n):
    return jax.ops.segment_sum(src, seg, n)
kernel_name = 'mk_cond_seq_d2_seqx_r4_5d115a'

def setup_inputs(seed: int=0):
    np.random.seed(seed)
    _w = jnp.asarray

    def _rec_inputs():
        import jax
        import jax.numpy as jnp
        _rk = jax.random.key(seed)
        x = -0.0002928 + 1 * jax.random.normal(jax.random.fold_in(_rk, 1), (8, 256, 256), jnp.float32)
        _lenS = 256 - jax.random.randint(jax.random.fold_in(_rk, 7), (8,), 0, max(1, 256 // 4) + 1, jnp.int32)
        _lenS2 = 256 - jax.random.randint(jax.random.fold_in(_rk, 8), (8,), 0, max(1, 256 // 4) + 1, jnp.int32)
        cond_1024 = 0.000887014 + 1.03683 * jax.random.normal(jax.random.fold_in(_rk, 11), (8, 256), jnp.float32)
        fside_BxSx3_0 = jax.random.uniform(jax.random.fold_in(_rk, 12), (8, 256, 3), jnp.float32, 0.0, 0.999943)
        return (x, cond_1024, fside_BxSx3_0)
    x, cond_1024, fside_BxSx3_0 = _rec_inputs()

    def _L0_cond_setup():
        import jax, jax.numpy as jnp
        import numpy as np
        HID = 256
        HEADS = 16
        HEAD_DIM = HID // HEADS
        ROPE_DIM = HEAD_DIM // 6 * 6
        HALF = ROPE_DIM // 3 // 2
        SWIGLU_HID = int(2 * (HID * 4) / 3)
        EPS = 1e-06
        THETA = 10000.0

        def rmsnorm(x, w, eps=EPS):
            xf = x.astype(jnp.float32)
            v = jnp.mean(xf * xf, axis=-1, keepdims=True)
            return w * (xf * jax.lax.rsqrt(v + eps)).astype(x.dtype)

        def modulate(x, shift, scale):
            return x * (1.0 + scale) + shift

        def rope_freqs():
            return 1.0 / THETA ** (jnp.arange(HALF, dtype=jnp.float32) / HALF)

        def apply_rope3d(q, k, positions):
            freqs = rope_freqs()
            ang = positions[..., :, None] * freqs
            ang = ang.reshape(ang.shape[0], ang.shape[1], -1)
            cos = jnp.cos(ang)[:, :, None, :]
            sin = jnp.sin(ang)[:, :, None, :]

            def rot(t):
                B, N, H, D = t.shape
                tr = t.reshape(B, N, H, D // 2, 2)
                t0, t1 = (tr[..., 0], tr[..., 1])
                out = jnp.stack([t0 * cos - t1 * sin, t0 * sin + t1 * cos], axis=-1)
                return out.reshape(B, N, H, D)
            return (rot(q), rot(k))
        key = jax.random.key(seed)
        ks = jax.random.split(key, 12)
        B, N = (2, 512)
        s = 0.02
        return {'x': jax.random.normal(ks[0], (B, N, HID), jnp.float32), 'c': jax.random.normal(ks[1], (B, HID), jnp.float32), 'positions': jax.random.uniform(ks[2], (B, N, 3), jnp.float32), 'norm1_w': jnp.ones((HID,), jnp.float32), 'qkv_w': jax.random.normal(ks[3], (3 * HID, HID), jnp.float32) * s, 'q_norm_w': jnp.ones((HEAD_DIM,), jnp.float32), 'k_norm_w': jnp.ones((HEAD_DIM,), jnp.float32), 'proj_w': jax.random.normal(ks[4], (HID, HID), jnp.float32) * s, 'proj_b': jnp.zeros((HID,), jnp.float32), 'norm2_w': jnp.ones((HID,), jnp.float32), 'w1': jax.random.normal(ks[5], (SWIGLU_HID, HID), jnp.float32) * s, 'w3': jax.random.normal(ks[6], (SWIGLU_HID, HID), jnp.float32) * s, 'w2': jax.random.normal(ks[7], (HID, SWIGLU_HID), jnp.float32) * s, 'ada_w': jax.random.normal(ks[8], (6 * HID, HID), jnp.float32) * s, 'ada_b': jnp.zeros((6 * HID,), jnp.float32)}
    _L0_cond_all = _L0_cond_setup()
    _L0_cond_in = {k: v for k, v in _L0_cond_all.items() if k in ('norm1_w', 'qkv_w', 'q_norm_w', 'k_norm_w', 'proj_w', 'proj_b', 'norm2_w', 'w1', 'w3', 'w2', 'ada_w', 'ada_b')}
    del _L0_cond_all

    def _L1_cond_setup():
        import jax, jax.numpy as jnp
        import numpy as np
        B, T, DIM = (4, 256, 256)
        COND = 256
        HEADS, DH = (16, 64)
        INNER = HEADS * DH
        MLP = 1024
        EPS = 1e-05

        def _layernorm(x):
            mu = jnp.mean(x, axis=-1, keepdims=True)
            var = jnp.mean(jnp.square(x - mu), axis=-1, keepdims=True)
            return (x - mu) * jax.lax.rsqrt(var + EPS)

        def _modulate(x, shift, scale):
            return x * (1.0 + scale) + shift

        def _attention(x, W_qkv, W_out, b_out):
            Bq, Tq, _ = x.shape
            qkv = x @ W_qkv
            q, k, v = jnp.split(qkv, 3, axis=-1)
            q = q.reshape(Bq, Tq, HEADS, DH)
            k = k.reshape(Bq, Tq, HEADS, DH)
            v = v.reshape(Bq, Tq, HEADS, DH)
            scale = DH ** (-0.5)
            attn = jnp.einsum('bqhd,bkhd->bhqk', q, k) * scale
            attn = jax.nn.softmax(attn, axis=-1)
            out = jnp.einsum('bhqk,bkhd->bqhd', attn, v).reshape(Bq, Tq, INNER)
            return out @ W_out + b_out

        def _ff(x, W1, b1, W2, b2):
            return jax.nn.gelu(x @ W1 + b1, approximate=False) @ W2 + b2
        key = jax.random.key(seed)
        ks = jax.random.split(key, 12)
        s = 0.02
        return {'x': jax.random.normal(ks[0], (B, T, DIM), jnp.float32), 'c': jax.random.normal(ks[1], (B, 1, COND), jnp.float32), 'W_mod': jax.random.normal(ks[2], (COND, 6 * DIM), jnp.float32) * s, 'b_mod': jax.random.normal(ks[3], (6 * DIM,), jnp.float32) * s, 'W_qkv': jax.random.normal(ks[4], (DIM, 3 * INNER), jnp.float32) * s, 'W_out': jax.random.normal(ks[5], (INNER, DIM), jnp.float32) * s, 'b_out': jax.random.normal(ks[6], (DIM,), jnp.float32) * s, 'W1': jax.random.normal(ks[7], (DIM, MLP), jnp.float32) * s, 'b1': jax.random.normal(ks[8], (MLP,), jnp.float32) * s, 'W2': jax.random.normal(ks[9], (MLP, DIM), jnp.float32) * s, 'b2': jax.random.normal(ks[10], (DIM,), jnp.float32) * s}
    _L1_cond_all = _L1_cond_setup()
    _L1_cond_in = {k: v for k, v in _L1_cond_all.items() if k in ('W_mod', 'b_mod', 'W_qkv', 'W_out', 'b_out', 'W1', 'b1', 'W2', 'b2')}
    del _L1_cond_all
    return {'x': x, 'cond_1024': cond_1024, 'fside_BxSx3_0': fside_BxSx3_0, 'L0_cond_norm1_w': _L0_cond_in['norm1_w'], 'L0_cond_qkv_w': _L0_cond_in['qkv_w'], 'L0_cond_q_norm_w': _L0_cond_in['q_norm_w'], 'L0_cond_k_norm_w': _L0_cond_in['k_norm_w'], 'L0_cond_proj_w': _L0_cond_in['proj_w'], 'L0_cond_proj_b': _L0_cond_in['proj_b'], 'L0_cond_norm2_w': _L0_cond_in['norm2_w'], 'L0_cond_w1': _L0_cond_in['w1'], 'L0_cond_w3': _L0_cond_in['w3'], 'L0_cond_w2': _L0_cond_in['w2'], 'L0_cond_ada_w': _L0_cond_in['ada_w'], 'L0_cond_ada_b': _L0_cond_in['ada_b'], 'L1_cond_W_mod': _L1_cond_in['W_mod'], 'L1_cond_b_mod': _L1_cond_in['b_mod'], 'L1_cond_W_qkv': _L1_cond_in['W_qkv'], 'L1_cond_W_out': _L1_cond_in['W_out'], 'L1_cond_b_out': _L1_cond_in['b_out'], 'L1_cond_W1': _L1_cond_in['W1'], 'L1_cond_b1': _L1_cond_in['b1'], 'L1_cond_W2': _L1_cond_in['W2'], 'L1_cond_b2': _L1_cond_in['b2']}

def reference(x, cond_1024, fside_BxSx3_0, L0_cond_norm1_w, L0_cond_qkv_w, L0_cond_q_norm_w, L0_cond_k_norm_w, L0_cond_proj_w, L0_cond_proj_b, L0_cond_norm2_w, L0_cond_w1, L0_cond_w3, L0_cond_w2, L0_cond_ada_w, L0_cond_ada_b, L1_cond_W_mod, L1_cond_b_mod, L1_cond_W_qkv, L1_cond_W_out, L1_cond_b_out, L1_cond_W1, L1_cond_b1, L1_cond_W2, L1_cond_b2):
    import jax
    import jax.numpy as jnp

    def _L0_cond_ref(x, c, positions, norm1_w, qkv_w, q_norm_w, k_norm_w, proj_w, proj_b, norm2_w, w1, w3, w2, ada_w, ada_b):
        import jax, jax.numpy as jnp
        import numpy as np
        HID = 256
        HEADS = 16
        HEAD_DIM = HID // HEADS
        ROPE_DIM = HEAD_DIM // 6 * 6
        HALF = ROPE_DIM // 3 // 2
        SWIGLU_HID = int(2 * (HID * 4) / 3)
        EPS = 1e-06
        THETA = 10000.0

        def rmsnorm(x, w, eps=EPS):
            xf = x.astype(jnp.float32)
            v = jnp.mean(xf * xf, axis=-1, keepdims=True)
            return w * (xf * jax.lax.rsqrt(v + eps)).astype(x.dtype)

        def modulate(x, shift, scale):
            return x * (1.0 + scale) + shift

        def rope_freqs():
            return 1.0 / THETA ** (jnp.arange(HALF, dtype=jnp.float32) / HALF)

        def apply_rope3d(q, k, positions):
            freqs = rope_freqs()
            ang = positions[..., :, None] * freqs
            ang = ang.reshape(ang.shape[0], ang.shape[1], -1)
            cos = jnp.cos(ang)[:, :, None, :]
            sin = jnp.sin(ang)[:, :, None, :]

            def rot(t):
                B, N, H, D = t.shape
                tr = t.reshape(B, N, H, D // 2, 2)
                t0, t1 = (tr[..., 0], tr[..., 1])
                out = jnp.stack([t0 * cos - t1 * sin, t0 * sin + t1 * cos], axis=-1)
                return out.reshape(B, N, H, D)
            return (rot(q), rot(k))
        B, N, C = x.shape
        H, D = (HEADS, HEAD_DIM)
        mod = (c @ ada_w.T + ada_b)[:, None, :]
        sh_msa, sc_msa, g_msa, sh_mlp, sc_mlp, g_mlp = jnp.split(mod, 6, axis=-1)
        h = modulate(rmsnorm(x, norm1_w), sh_msa, sc_msa)
        qkv = (h @ qkv_w.T).reshape(B, N, 3, H, D)
        q, k, v = (qkv[:, :, 0], qkv[:, :, 1], qkv[:, :, 2])
        q = rmsnorm(q, q_norm_w)
        k = rmsnorm(k, k_norm_w)
        q_r, k_r = apply_rope3d(q[..., :ROPE_DIM], k[..., :ROPE_DIM], positions)
        q = jnp.concatenate([q_r, q[..., ROPE_DIM:]], axis=-1)
        k = jnp.concatenate([k_r, k[..., ROPE_DIM:]], axis=-1)
        scale = D ** (-0.5)
        attn = jnp.einsum('bnhd,bmhd->bhnm', q, k) * scale
        attn = jax.nn.softmax(attn, axis=-1)
        o = jnp.einsum('bhnm,bmhd->bnhd', attn, v).reshape(B, N, C)
        o = o @ proj_w.T + proj_b
        x = x + g_msa * o
        h2 = modulate(rmsnorm(x, norm2_w), sh_mlp, sc_mlp)
        ff = jax.nn.silu(h2 @ w1.T) * (h2 @ w3.T) @ w2.T
        x = x + g_mlp * ff
        return x

    def _L1_cond_ref(x, c, W_mod, b_mod, W_qkv, W_out, b_out, W1, b1, W2, b2):
        import jax, jax.numpy as jnp
        import numpy as np
        B, T, DIM = (4, 256, 256)
        COND = 256
        HEADS, DH = (16, 64)
        INNER = HEADS * DH
        MLP = 1024
        EPS = 1e-05

        def _layernorm(x):
            mu = jnp.mean(x, axis=-1, keepdims=True)
            var = jnp.mean(jnp.square(x - mu), axis=-1, keepdims=True)
            return (x - mu) * jax.lax.rsqrt(var + EPS)

        def _modulate(x, shift, scale):
            return x * (1.0 + scale) + shift

        def _attention(x, W_qkv, W_out, b_out):
            Bq, Tq, _ = x.shape
            qkv = x @ W_qkv
            q, k, v = jnp.split(qkv, 3, axis=-1)
            q = q.reshape(Bq, Tq, HEADS, DH)
            k = k.reshape(Bq, Tq, HEADS, DH)
            v = v.reshape(Bq, Tq, HEADS, DH)
            scale = DH ** (-0.5)
            attn = jnp.einsum('bqhd,bkhd->bhqk', q, k) * scale
            attn = jax.nn.softmax(attn, axis=-1)
            out = jnp.einsum('bhqk,bkhd->bqhd', attn, v).reshape(Bq, Tq, INNER)
            return out @ W_out + b_out

        def _ff(x, W1, b1, W2, b2):
            return jax.nn.gelu(x @ W1 + b1, approximate=False) @ W2 + b2
        mod = jax.nn.silu(c) @ W_mod + b_mod
        sh_msa, sc_msa, g_msa, sh_mlp, sc_mlp, g_mlp = jnp.split(mod, 6, axis=-1)
        x = x + g_msa * _attention(_modulate(_layernorm(x), sh_msa, sc_msa), W_qkv, W_out, b_out)
        x = x + g_mlp * _ff(_modulate(_layernorm(x), sh_mlp, sc_mlp), W1, b1, W2, b2)
        return x
    x = _L0_cond_ref(x, cond_1024, fside_BxSx3_0, L0_cond_norm1_w, L0_cond_qkv_w, L0_cond_q_norm_w, L0_cond_k_norm_w, L0_cond_proj_w, L0_cond_proj_b, L0_cond_norm2_w, L0_cond_w1, L0_cond_w3, L0_cond_w2, L0_cond_ada_w, L0_cond_ada_b)
    x = _L1_cond_ref(x, cond_1024[:, None, :], L1_cond_W_mod, L1_cond_b_mod, L1_cond_W_qkv, L1_cond_W_out, L1_cond_b_out, L1_cond_W1, L1_cond_b1, L1_cond_W2, L1_cond_b2)
    return x

_drawn_inputs = setup_inputs


def setup_inputs(seed=0):
    import zlib

    import numpy as np

    out = dict(_drawn_inputs(seed))
    spreads = {'L0_cond_norm1_w': (1.0, 0.6),
     'L0_cond_q_norm_w': (1.0, 0.6),
     'L0_cond_k_norm_w': (1.0, 0.6),
     'L0_cond_proj_b': (0.0, 0.1),
     'L0_cond_norm2_w': (1.0, 0.6),
     'L0_cond_ada_b': (0.0, 0.568)}
    factors = {'fside_BxSx3_0': 8.0,
     'L0_cond_qkv_w': 4.542,
     'L0_cond_proj_w': 4.574,
     'L0_cond_w1': 4.383,
     'L0_cond_w3': 4.3,
     'L0_cond_w2': 4.324,
     'L1_cond_b_mod': 8.0,
     'L1_cond_W_qkv': 6.908,
     'L1_cond_W_out': 6.703,
     'L1_cond_b_out': 64.0,
     'L1_cond_b1': 64.0,
     'L1_cond_b2': 64.0,
     'L1_cond_W1': 8.0,
     'L1_cond_W2': 8.0}
    for name, (base, spread) in spreads.items():
        noise = np.random.default_rng([zlib.crc32(name.encode()), seed]).standard_normal(out[name].shape)
        drawn = base * np.exp(spread * noise) if base else spread * noise
        out[name] = jnp.asarray(drawn.astype(out[name].dtype))
    for name, factor in factors.items():
        out[name] = (out[name] * factor).astype(out[name].dtype)
    return out
```

```python
from contextlib import ExitStack
import math

import numpy as np
import concourse.bass as bass
from concourse import mybir

F32 = mybir.dt.float32
F32R = mybir.dt.float32r
ALU = mybir.AluOpType
ACT = mybir.ActivationFunctionType
AX = mybir.AxisListType

P = 128
NB = 8
NTOK = 256
TT = NTOK // P
D = 256
FT = D // P
HEADS = 16
UNITS = HEADS // 2
FF0 = 682
FF0P = 768
QK_ROWS = 48

LAYERS = [
    dict(dh=16, eps=1e-6, hid=FF0P // P, inner=256, qkv=768, scale=16 ** -0.5),
    dict(dh=64, eps=1e-5, hid=1024 // P, inner=1024, qkv=3072, scale=64 ** -0.5),
]


class Signal:

    def __init__(self, sem, per):
        self.sem, self.per = sem, per

    def wait(self, eng, b, k):
        v = b * self.per + k
        if isinstance(v, int) and v <= 0:
            return
        eng.wait_ge(self.sem, v)


class Chain:

    def __init__(self, sem, per):
        self.sem, self.per, self.k, self.b = sem, per, 0, 0

    def start(self, b):
        self.b, self.k = b, 0

    def link(self, ins):
        self.k += 1
        ins.then_inc(self.sem, 1)

    def wait(self, eng):
        eng.wait_ge(self.sem, self.b * self.per + self.k)

    def end(self):
        assert self.k == self.per, (self.k, self.per)


def bcast(ap, axis, n):
    a = ap.unsqueeze(axis)
    shape = list(a.shape)
    shape[axis] = n
    return a.to_broadcast(shape)


def t_orders(L):
    if L == 0:
        a1, a2 = ["xnT0", "xnT1"], ["qk0", "v0"]
        m1 = ["oT0", "oT1"]
        first = a1 + a2 + ["qk1", "v1"] + [f"qkT{i}" for i in range(8)]
        mid = (m1 + a1 + a2 + ["pj0", "pj1", "qk1", "v1", "h2T0", "h2T1"]
               + [f"hid{i}" for i in range(6)] + [f"qkT{i}" for i in range(4)]
               + ["w20", "w21"] + [f"qkT{i}" for i in range(4, 8)])
        last = m1 + ["pj0", "pj1", "h2T0", "h2T1"] + [f"hid{i}" for i in range(6)] + ["w20", "w21"]
    else:
        a1 = ["xnT0", "xnT1"] + [f"v{i}" for i in range(4)]
        m1 = [f"oT{i}" for i in range(4)]
        m2 = ["h2T0", "h2T1"] + [f"hid{i}" for i in range(4)] + ["w20", "w21"]
        q = [f"qk{u}" for u in range(UNITS)]
        first = a1 + q
        mid = m1 + a1 + ["pj0", "pj1"] + q[:2] + m2 + q[2:]
        last = m1 + ["pj0", "pj1"] + m2
    return dict(first=first, mid=mid, last=last)


def build_layer(nc, L, x_src, y_dst, w, scratch):
    cfg = LAYERS[L]
    DH, HID, INNER, QKV = cfg["dh"], cfg["hid"], cfg["inner"], cfg["qkv"]
    KO = INNER // P
    DHA = DH + 1
    ORD = t_orders(L)
    NF, NM = len(ORD["first"]), len(ORD["mid"])
    assert NF % 2 == 0 and NM % 2 == 0
    NMOD = 6 * D

    ctx = ExitStack()
    with ctx:
        def sb(name, shape, dt=F32):
            return ctx.enter_context(nc.sbuf_tensor(f"{name}_{L}", shape, dt))

        def ps(name):
            return ctx.enter_context(nc.psum_tensor(f"{name}_{L}", [P, 512], F32))

        def sem(name):
            return ctx.enter_context(nc.semaphore(f"{name}_{L}"))

        shapes = dict(wqkv=[P, FT, QKV], wo=[P, KO, D], w1=[P, FT, HID * P], w2=[P, HID, D])
        if L == 0:
            shapes["w3"] = [P, FT, HID * P]
        hi = {k: sb(f"{k}_hi", s, F32R) for k, s in shapes.items()}
        lo = {k: sb(f"{k}_lo", s, F32R) for k, s in shapes.items()}
        CH = 1536
        raw = sb("raw", [P, 2, CH])
        chunks = []
        for k in ["wqkv", "wo", "w1", "w3", "w2"]:
            if k in shapes:
                n = shapes[k][1] * shapes[k][2]
                chunks += [(k, c, min(CH, n - c)) for c in range(0, n, CH)]

        ident = sb("ident", [P, P])
        x_in = sb("x_in", [P, TT, D])
        xr = sb("xr", [P, TT, D])
        x2 = sb("x2", [P, TT, D])
        yo = sb("yo", [P, TT, D])
        xn = sb("xn", [P, TT, D])
        xn2 = sb("xn2", [P, TT, D])
        hfull = sb("hfull", [P, FT, NTOK])
        hhi = sb("hhi", [P, FT, NTOK], F32R)
        hlo = sb("hlo", [P, FT, NTOK], F32R)
        h2hi = sb("h2hi", [P, FT, NTOK], F32R)
        h2lo = sb("h2lo", [P, FT, NTOK], F32R)
        h2full = sb("h2full", [P, FT, NTOK])
        ab1 = sb("ab1", [P, 4])
        gb1 = sb("gb1", [P, D])
        ab2 = sb("ab2", [P, 4])
        g12 = sb("g12", [P, 3, D])
        held = sb("held", [P, 1])
        stat = sb("stat", [P, TT, 6])
        aggr = sb("aggr", [P, TT, 2])
        msq = sb("msq", [P, TT])
        rstd = sb("rstd", [P, TT])
        stat2 = sb("stat2", [P, TT, 6])
        aggr2 = sb("aggr2", [P, TT, 2])
        msq2 = sb("msq2", [P, TT])
        rstd2 = sb("rstd2", [P, TT])
        mhalf = sb("mhalf", [P, 32])
        vaug = sb("vaug", [P, TT, HEADS, DHA])
        negm = sb("negm", [P, 2, TT])
        mhi = sb("mhi", [P, 2, TT], F32R)
        mcols = sb("mcols", [P, TT, 2, 2])
        mT = sb("mT", [P, NTOK], F32R)
        sel = sb("sel", [P, 2, P], F32R)
        pt = sb("pt", [P, 4, 512])
        rden = sb("rden", [P, TT, 2])
        o_tok = sb("o_tok", [P, TT, INNER])
        ahi = sb("ahi", [P, HID, NTOK], F32R)
        alo = sb("alo", [P, HID, NTOK], F32R)
        othi, otlo = ahi[:, 0:KO, :], alo[:, 0:KO, :]
        if L == 0:
            cs = sb("cs", [P, TT, 2, 2, 16])
            qraw = sb("qraw", [P, TT, 512])
            sq = sb("sq", [P, 512])
            hss = sb("hss", [P, TT, 32])
            hr = sb("hr", [P, TT, 32])
            qn = sb("qn", [P, TT, 512])
            m1 = sb("m1", [P, TT, 512])
            m2 = sb("m2", [P, 32, 12])
            stack = sb("stack", [P, 2, HEADS, 64], F32R)
            qkT = sb("qkT", [P, 2, UNITS, NTOK], F32R)
            th = sb("th", [P, 2, NTOK])
            t1 = sb("t1", [P, 2, NTOK])
            afull = sb("afull", [P, 2, NTOK])
        else:
            qkhi = sb("qkhi", [P, 2, 512], F32R)
            qklo = sb("qklo", [P, 2, 512], F32R)
            afull = sb("afull", [P, 2, 512])
            b1c = sb("b1c", [P, HID])

        T = [ps("T0"), ps("T1")]
        S = [ps("S0"), ps("S1")]
        PB = [ps("P0"), ps("P1")]
        V = [ps("V0"), ps("V1")]

        raw_in, raw_hi, raw_lo = [sem("raw_in0"), sem("raw_in1")], sem("raw_hi"), sem("raw_lo")
        const_in, mod_in, s_init, s_ident, s_sel = sem("const_in"), [sem("mod_in0"), sem("mod_in1")], sem("init"), sem("ident_m"), sem("selm")
        mod_mm, mod_row, mod_T, mod_ab, mod_silu, gates_out, mod_chain = (
            sem("mod_mm"), sem("mod_row"), sem("mod_T"), sem("mod_ab"), sem("mod_silu"), sem("gates_out"), sem("mod_chain"))
        trig_in, trig_red, trig_sin, trig_done = sem("trig_in"), sem("trig_red"), sem("trig_sin"), sem("trig_done")
        chain_a = Chain(sem("chain_a"), 3 + 3 * TT + UNITS if L == 0 else 2 + UNITS)
        chain_m = Chain(sem("chain_m"), 3)
        t_full = [sem("t_full0"), sem("t_full1")]

        def sig(name, per):
            return Signal(sem(name), per)

        x_loaded = sig("x_loaded", 16)
        par1, par2 = sig("par1", 48 if L == 0 else 32), sig("par2", 32)
        ms1, rstd1, xn_ok = sig("ms1", 1), sig("rstd1", 1), sig("xn_ok", TT)
        ms2, rs2, xn2_ok = sig("ms2", 1), sig("rs2", 1), sig("xn2_ok", TT)
        h_full, h_hi, h_lo = sig("h_full", FT), sig("h_hi", FT), sig("h_lo", FT)
        h2_full, h2_hi, h2_lo = sig("h2_full", FT), sig("h2_hi", FT), sig("h2_lo", FT)
        xr_ok, x2_ok, y_ok, y_stored = sig("xr_ok", 1), sig("x2_ok", TT), sig("y_ok", TT), sig("y_stored", 16)
        w2_gated = sig("w2_gated", TT)
        v_ok = sig("v_ok", 2 if L == 0 else 4)
        s_full, m_ok, mT_full, mT_ok = sig("s_full", 16), sig("m_ok", 8), sig("mT_full", 8), sig("mT_ok", 8)
        p_full, p_ok, av_full, o_ok = sig("p_full", 16), sig("p_ok", 16), sig("av_full", 16), sig("o_ok", 8)
        mh_ok, rd_ok, sw_ok = sig("mh_ok", 16), sig("rd_ok", 8), sig("sw_ok", HID)
        ot_hi, ot_lo = sig("ot_hi", 2 if L == 0 else 4), sig("ot_lo", 2 if L == 0 else 4)
        pj_gated = sig("pj_gated", TT)
        a_full, a_hi, a_lo = sig("a_full", HID), sig("a_hi", HID), sig("a_lo", HID)
        if L == 0:
            qraw_ok, hss_ok, hr_ok, qn_ok, m1_ok, qf_ok = (
                sig("qraw_ok", TT), sig("hss_ok", TT), sig("hr_ok", TT), sig("qn_ok", TT), sig("m1_ok", TT), sig("qf_ok", TT))
            st_hi, st_lo, qkT_ok, tanh_ok = (
                sig("st_hi", 2 * TT), sig("st_lo", 2 * TT), sig("qkT_ok", 8), sig("tanh_ok", HID))
        else:
            qk_hi, qk_lo = sig("qk_hi", 8), sig("qk_lo", 8)

        last_read = {f"xnT{i}": (h_full, True, i + 1) for i in range(FT)}
        last_read |= {f"h2T{i}": (h2_full, False, i + 1) for i in range(FT)}
        last_read |= {f"v{i}": (v_ok, True, i + 1) for i in range(v_ok.per)}
        last_read |= {f"oT{i}": (ot_lo, False, i + 1) for i in range(ot_lo.per)}
        last_read |= {f"pj{i}": (pj_gated, False, i + 1) for i in range(TT)}
        last_read |= {f"w2{i}": (w2_gated, False, i + 1) for i in range(TT)}
        if L == 0:
            last_read |= {f"qk{i}": (qraw_ok, True, i + 1) for i in range(TT)}
            last_read |= {f"qkT{i}": (qkT_ok, True, i + 1) for i in range(8)}
            last_read |= {f"hid{i}": (a_full, False, i + 1) for i in range(HID)}
            hh_read = (v_ok, v_ok.per)
        else:
            last_read |= {f"qk{i}": (qk_lo, True, i + 1) for i in range(UNITS)}
            last_read |= {f"hid{i}": (a_full, False, 2 * i + 2) for i in range(HID // 2)}
            hh_read = (qk_lo, 8)

        def t_claim(eng, kind, n, name):
            order, pos = ORD[kind], ORD[kind].index(name)
            if pos >= 2:
                s_, attn, k = last_read[order[pos - 2]]
                s_.wait(eng, n if attn else n - 1, k)
            elif kind != "first":
                former = ORD["first" if isinstance(n, int) and n == 1 else "mid"]
                s_, attn, k = last_read[former[pos - 2]]
                s_.wait(eng, n - 1 if attn else n - 2, k)
            return T[pos % 2], t_full[pos % 2]

        def t_read(eng, kind, n, name):
            pos = ORD[kind].index(name)
            before = 0 if kind == "first" else NF // 2 + (n - 1) * (NM // 2)
            eng.wait_ge(t_full[pos % 2], before + pos // 2 + 1)
            return T[pos % 2]

        cT = sb("cT", [P, FT, NB])
        cact = sb("cact", [P, FT, NB])
        modr = sb("modr", [NB, NMOD]) if L == 0 else o_tok[0:NB, :, :].rearrange("p t c -> p (t c)")
        bmod = pt[0:NB, :, :].rearrange("p s c -> p (s c)")[:, 0:NMOD]
        grow = (qn if L == 0 else afull)[0:NB, :, :].rearrange("p a (b c) -> p (a b) c", b=2)
        bo8 = sb("bo8", [NB, 2, D])
        wn = sb("wn", [P, 4])
        abT = sb("abT", [P, 8, NB])
        ab_all = sb("ab_all", [P, NB, 8])
        if L == 0:
            pos = sb("pos", [P, NB * TT, 3])
            ang = sb("ang", [P, 2, NB * TT, 6])
            kk = sb("kk", [P, 2, NB * TT, 6])
            trig = sb("trig", [P, 2, NB * TT, 6])
            wqk = sb("wqk", [P, 2, 16])
            cs_all = sb("cs_all", [P, NB * TT, 2, 2, 16])

        block = ctx.enter_context(nc.Block())

        def bodies(eng, body):
            body("first", 0)
            body("mid", 1)
            with eng.Fori(2, NB) as n:
                body("mid", n)
            body("last", NB)

        @block.sync
        def _(sp):
            sp.dma_start(cT[:, :, :], w["cT"]).then_inc(const_in, 16)
            sp.dma_start(bmod[:, :], w["bmod"].partition_broadcast(NB)).then_inc(const_in, 16)
            sp.dma_start(bo8[:, 0, :], w["bo"].partition_broadcast(NB)).then_inc(const_in, 16)
            if L == 0:
                sp.dma_start(wn[:, 0:2], w["n1"]).then_inc(const_in, 16)
                sp.dma_start(wn[:, 2:4], w["n2"]).then_inc(const_in, 16)
                sp.dma_start(pos[:, :, :], w["pos"]).then_inc(trig_in, 16)
                sp.dma_start(wqk[:, 0, :], w["qn"].partition_broadcast(P)).then_inc(trig_in, 16)
                sp.dma_start(wqk[:, 1, :], w["kn"].partition_broadcast(P)).then_inc(trig_in, 16)
            else:
                sp.dma_start(bo8[:, 1, :], w["b2"].partition_broadcast(NB)).then_inc(const_in, 16)
                sp.dma_start(b1c[:, :], w["b1"]).then_inc(const_in, 16)
            for h in range(2):
                sp.dma_start(raw[:, h, :].rearrange("p (k n) -> p k n", k=FT), w["wmod"].rearrange("p (k n) -> p k n", k=FT)[:, :, h * 768:(h + 1) * 768]).then_inc(mod_in[h], 16)
            for n, (k, c, m) in enumerate(chunks):
                if n >= 2:
                    sp.wait_ge(raw_lo, n - 1)
                else:
                    sp.wait_ge(mod_mm, n + 1)
                src = w[k][:, c:c + m]
                sp.dma_start(raw[:, n % 2, 0:m], src).then_inc(raw_in[n % 2], 16)
            sp.wait_ge(mod_row, 1)
            sp.dma_start(scratch["gates"], grow[:, :, :].rearrange("b g d -> b (g d)")).then_inc(gates_out, 16)
            sp.wait_ge(gates_out, 16)
            sp.wait_ge(mod_ab, 1)
            if L == 0:
                sp.wait_ge(trig_done, 1)

            def load_attn(n):
                xn_ok.wait(sp, n, 0)
                xr_ok.wait(sp, n, 0)
                sp.dma_start(x_in[:, :, :], x_src[n]).then_inc(x_loaded.sem, 16)
                h_full.wait(sp, n, 0)
                if L == 0:
                    qf_ok.wait(sp, n, 0)
                sp.dma_start(ab1[:, :], ab_all[:, n, 0:4]).then_inc(par1.sem, 16)
                sp.dma_start(gb1[:, :], scratch["gates"][n, 0:D].partition_broadcast(P)).then_inc(par1.sem, 16)
                if L == 0:
                    sp.dma_start(cs[:, :, :, :, :].rearrange("p t c q d -> p t (c q d)"), cs_all[:, :, :, :, :].rearrange("p (n t) c q d -> p n t (c q d)", t=TT)[:, n]).then_inc(par1.sem, 16)

            def load_mlp(b):
                h2_full.wait(sp, b, 0)
                y_ok.wait(sp, b, 0)
                sp.dma_start(ab2[:, :], ab_all[:, b, 4:8]).then_inc(par2.sem, 16)
                sp.dma_start(g12[:, :, :], scratch["g3"][b].partition_broadcast(P)).then_inc(par2.sem, 16)

            def store(b):
                y_ok.wait(sp, b, TT)
                sp.dma_start(y_dst[b], yo[:, :, :]).then_inc(y_stored.sem, 16)

            def body(kind, n):
                if kind != "last":
                    load_attn(n)
                if kind != "first":
                    load_mlp(n - 1)
                    store(n - 1)

            bodies(sp, body)
            y_stored.wait(sp, NB, 0)

        @block.gpsimd
        def _(pool):
            g = nc.gpsimd
            g.memset(ident[:, :], 0.0).then_inc(s_ident, 1)
            pool.wait_ge(s_ident, 1)
            g.affine_select(out=ident[:, :], in_=ident[:, :], compare_op=ALU.not_equal, fill=1.0,
                            base=0, pattern=[[-1, P]], channel_multiplier=1).then_inc(s_ident, 1)
            g.memset(mhalf[:, :], -0.5).then_inc(s_init, 1)
            g.memset(vaug[:, :, :, DH:DHA], 1.0).then_inc(s_init, 1)
            g.memset(negm[:, :, :], 0.0).then_inc(s_init, 1)
            if L == 0:
                g.memset(stack[:, :, :, 48:64].bitcast(F32), 0.0).then_inc(s_init, 1)
            else:
                g.memset(rden[:, :, :], 0.0).then_inc(s_init, 1)
            pool.wait_ge(s_init, 4)

            def power(out, in_, ok, ms, b, k):
                ms.wait(pool, b, k)
                g.tensor_tensor(out, in_, mhalf[:, 0:in_.shape[-1]], ALU.pow).then_inc(ok.sem, 1)

            def low(out, full, hi_, ok, hi_ok, b, k, read, rk):
                read.wait(pool, b, rk)
                hi_ok.wait(pool, b, k)
                g.tensor_tensor(out, full, hi_.bitcast(F32), ALU.subtract).then_inc(ok.sem, 1)

            def residual(n):
                x_loaded.wait(pool, n, 16)
                par1.wait(pool, n, par1.per)
                x2_ok.wait(pool, n, 0)
                g.tensor_tensor(xr[:, :, :], x_in[:, :, :], bcast(gb1[:, :], 1, TT), ALU.add).then_inc(xr_ok.sem, 1)

            def h_low(n):
                for ft in range(FT):
                    low(hlo[:, ft, :], hfull[:, ft, :], hhi[:, ft, :], h_lo, h_hi, n, ft + 1, hh_read[0], 0)

            def h2_low(b):
                for ft in range(FT):
                    low(h2lo[:, ft, :], h2full[:, ft, :], h2hi[:, ft, :], h2_lo, h2_hi, b, ft + 1, a_full, 0)

            def head_norm(n, t):
                power(hr[:, t, :], hss[:, t, :], hr_ok, hss_ok, n, t + 1)

            def cos_part(n, t):
                st_lo.wait(pool, n - 1, 2 * t + 2)
                qn_ok.wait(pool, n, t + 1)
                o4 = m1[:, t, :].rearrange("p (q h d) -> p q h d", q=2, h=HEADS)
                i4 = qn[:, t, :].rearrange("p (q h d) -> p q h d", q=2, h=HEADS)
                g.tensor_tensor(o4, i4, bcast(cs[:, t, 0, :, :], 2, HEADS), ALU.mult).then_inc(m1_ok.sem, 1)

            def a_low(b, i):
                if L == 0:
                    low(alo[:, i, :], afull[:, i % 2, :], ahi[:, i, :], a_lo, a_hi, b, i + 1, pj_gated, TT)
                else:
                    j = i // 2
                    if i % 2 == 0:
                        low(alo[:, i, :], afull[:, j % 2, 0:256], ahi[:, i, :], a_lo, a_hi, b, i + 1, pj_gated, TT)
                    else:
                        low(alo[:, i, :], afull[:, j % 2, 256:512], ahi[:, i, :], a_lo, a_hi, b, i + 1, pj_gated, TT)

            def body(kind, n):
                A, M = kind != "last", kind != "first"
                b = n - 1
                if A:
                    norm1_n(n)
                    h_low(n)
                    if L == 0:
                        head_norm(n, 0)
                if M:
                    power(rstd2[:, :], msq2[:, :], rs2, ms2, b, 1)
                if A:
                    if L == 0:
                        cos_part(n, 0)
                        head_norm(n, 1)
                    residual(n)
                if M:
                    h2_low(b)
                if A and L == 0:
                    cos_part(n, 1)
                if M:
                    for i in range(HID):
                        a_low(b, i)

            def norm1_n(n):
                power(rstd[:, :], msq[:, :], rstd1, ms1, n, 1)

            bodies(pool, body)

        @block.scalar
        def _(act):
            a = nc.scalar
            if L == 0:
                act.wait_ge(trig_red, 1)
                a.activation(trig[:, :, :, :], ang[:, :, :, :], ACT.Sin).then_inc(trig_sin, 1)
            else:
                act.wait_ge(const_in, 16 * 5)
                a.activation(cact[:, :, :], cT[:, :, :], ACT.Tanh, scale=0.5).then_inc(mod_silu, 1)
            for n, (k, c, m) in enumerate(chunks):
                act.wait_ge(raw_in[n % 2], 16 * (n // 2 + 1))
                dst = hi[k][:, :, :].rearrange("p a b -> p (a b)")[:, c:c + m]
                a.copy(dst, raw[:, n % 2, 0:m]).then_inc(raw_hi, 1)

            def high(out, full, ok, full_ok, b, k, read, rk):
                read.wait(act, b, rk)
                full_ok.wait(act, b, k)
                a.copy(out, full).then_inc(ok.sem, 1)

            def h_high(n):
                for ft in range(FT):
                    high(hhi[:, ft, :], hfull[:, ft, :], h_hi, h_full, n, ft + 1, hh_read[0], 0)

            def h2_high(b):
                for ft in range(FT):
                    high(h2hi[:, ft, :], h2full[:, ft, :], h2_hi, h2_full, b, ft + 1, a_full, 0)

            def ot_high(kind, n, b):
                for i in range(ot_hi.per):
                    bank = t_read(act, kind, n, f"oT{i}")
                    w2_gated.wait(act, b, 0)
                    a.copy(othi[:, 2 * i:2 * i + 2, :].rearrange("p a b -> p (a b)") if L else othi[:, i, :],
                           bank[:, 0:512] if L else bank[:, 0:256]).then_inc(ot_hi.sem, 1)

            def qkv_raw(kind, n, t):
                bank = t_read(act, kind, n, f"qk{t}")
                qn_ok.wait(act, n - 1, t + 1)
                a.copy(qraw[:, t, :], bank[:, :]).then_inc(qraw_ok.sem, 1)

            def v_evac(kind, n, i):
                bank = t_read(act, kind, n, f"v{i}")
                av_full.wait(act, n, 0)
                if L == 0:
                    out = vaug[:, i, :, 0:DH]
                    src = bank[:, 0:256].rearrange("p (h d) -> p h d", d=DH)
                else:
                    out = vaug[:, i // 2, (i % 2) * 8:(i % 2) * 8 + 8, 0:DH]
                    src = bank[:, :].rearrange("p (h d) -> p h d", d=DH)
                a.copy(out, src).then_inc(v_ok.sem, 1)

            def stack_high(n, t):
                qkT_ok.wait(act, n, 4 * t)
                qf_ok.wait(act, n, t + 1)
                f = m1[:, t, :].rearrange("p (q h d) -> p q h d", q=2, h=HEADS)
                a.copy(stack[:, 0, :, 0:32].rearrange("p h (r d) -> p h r d", r=2),
                       bcast(f[:, 0], 2, 2)).then_inc(st_hi.sem, 1)
                a.copy(stack[:, 1, :, 0:64].rearrange("p h (r d) -> p h r d", r=2)[:, :, :, 0:16],
                       bcast(f[:, 1], 2, 2)).then_inc(st_hi.sem, 1)

            def qkT_evac(kind, n, i):
                t, q, half = i // 4, (i // 2) % 2, i % 2
                bank = t_read(act, kind, n, f"qkT{i}")
                p_full.wait(act, n, 0)
                a.copy(qkT[:, q, 4 * half:4 * half + 4, t * P:(t + 1) * P],
                       bank[:, :].rearrange("p (u c) -> p u c", u=4)).then_inc(qkT_ok.sem, 1)

            def qk_high(kind, n, u):
                bank = t_read(act, kind, n, f"qk{u}")
                p_full.wait(act, n, 2 * (u - 1))
                a.copy(qkhi[:, u % 2, :], bank[:, :]).then_inc(qk_hi.sem, 1)

            def m_evac(n, u):
                mT_full.wait(act, n, u + 1)
                p_full.wait(act, n, 2 * u)
                a.copy(mT[0:4, :], S[0][0:4, 0:NTOK]).then_inc(mT_ok.sem, 1)

            def exps(n, u):
                for hh in range(2):
                    k = 2 * u + hh
                    p_full.wait(act, n, k + 1)
                    av_full.wait(act, n, k - 3)
                    a.activation(pt[:, k % 4, :], PB[hh][:, :], ACT.Exp, scale=cfg["scale"]).then_inc(p_ok.sem, 1)

            def hid_act(kind, n, b, i):
                if L == 0:
                    bank = t_read(act, kind, n, f"hid{i}")
                    a_full.wait(act, b, i - 1)
                    a.activation(th[:, i % 2, :], bank[:, 0:256], ACT.Tanh, scale=0.5).then_inc(tanh_ok.sem, 1)
                else:
                    bank = t_read(act, kind, n, f"hid{i}")
                    a_lo.wait(act, b, 2 * i - 2)
                    for j in range(2):
                        ins = a.activation(afull[:, i % 2, 256 * j:256 * j + 256], bank[:, 256 * j:256 * j + 256],
                                           ACT.Gelu, bias=b1c[:, 2 * i + j:2 * i + j + 1])
                        ins.then_inc(a_full.sem, 1)
                    a_full.wait(act, b, 2 * i + 2)
                    pj_gated.wait(act, b, TT)
                    for j in range(2):
                        ins = a.copy(ahi[:, 2 * i + j, :], afull[:, i % 2, 256 * j:256 * j + 256])
                        ins.then_inc(a_hi.sem, 1)

            def a_high(b, i):
                high(ahi[:, i, :], afull[:, i % 2, :], a_hi, a_full, b, i + 1, pj_gated, TT)

            def body(kind, n):
                A, M = kind != "last", kind != "first"
                b = n - 1
                if M:
                    ot_high(kind, n, b)
                if A:
                    h_high(n)
                if L == 0:
                    if A:
                        qkv_raw(kind, n, 0)
                        v_evac(kind, n, 0)
                        qkv_raw(kind, n, 1)
                        v_evac(kind, n, 1)
                    if M:
                        h2_high(b)
                    if A:
                        stack_high(n, 0)
                    if M:
                        for i in range(HID):
                            hid_act(kind, n, b, i)
                            a_high(b, i)
                    if A:
                        for i in range(4):
                            qkT_evac(kind, n, i)
                        stack_high(n, 1)
                        for i in range(4, 8):
                            qkT_evac(kind, n, i)
                        for u in range(UNITS):
                            m_evac(n, u)
                            exps(n, u)
                else:
                    if A:
                        for i in range(4):
                            v_evac(kind, n, i)
                        qk_high(kind, n, 0)
                        qk_high(kind, n, 1)
                    if M:
                        h2_high(b)
                        for i in range(4):
                            hid_act(kind, n, b, i)
                    if A:
                        for u in range(UNITS):
                            m_evac(n, u)
                            exps(n, u)
                            if u + 2 < UNITS:
                                qk_high(kind, n, u + 2)

            bodies(act, body)

        @block.vector
        def _(dve):
            v = nc.vector
            pre = Chain(mod_chain, 0)

            def done(ins):
                pre.link(ins)
                pre.wait(dve)

            dve.wait_ge(s_ident, 2)
            for hh in range(2):
                v.tensor_tensor(sel[:, hh, :], ident[:, 2 * hh:2 * hh + 1].to_broadcast([P, P]),
                                ident[:, 2 * hh + 1:2 * hh + 2].to_broadcast([P, P]), ALU.add).then_inc(s_sel, 1)
            if L == 0:
                dve.wait_ge(trig_in, 48)
                freq = [1.0, 0.01]
                a_v = ang[:, 1, :, :].rearrange("p n (a h) -> p n a h", h=2)
                for h in range(2):
                    done(v.tensor_scalar(a_v[:, :, :, h], pos[:, :, :], freq[h], None, ALU.mult))
                magic = 1.5 * 2 ** 23
                c1 = 6.28125
                c2 = round((2 * math.pi - c1) * 2 ** 21) / 2 ** 21
                c3 = 2 * math.pi - c1 - c2
                sa, ca, kt = ang[:, 1, :, :], ang[:, 0, :, :], kk[:, 0, :, :]
                done(v.tensor_scalar(kt, sa, 1 / (2 * math.pi), magic, ALU.mult, ALU.add))
                done(v.tensor_scalar(kt, kt, magic, None, ALU.subtract))
                for c in (c1, c2, c3):
                    done(v.scalar_tensor_tensor(out=sa, in0=kt, scalar=-c, in1=sa, op0=ALU.mult, op1=ALU.add))
                pi = 3.1415925
                done(v.tensor_scalar(sa, sa, pi, -pi, ALU.min, ALU.max))
                done(v.tensor_scalar(ca, sa, math.pi / 2, None, ALU.add))
                done(v.tensor_scalar(kt, ca, pi, -2 * math.pi, ALU.is_gt, ALU.mult))
                done(v.tensor_tensor(ca, ca, kt, ALU.add))
                v.tensor_scalar(ca, ca, pi, -pi, ALU.min, ALU.max).then_inc(trig_red, 1)
                dve.wait_ge(trig_sin, 1)
                done(v.tensor_scalar(kk[:, 1, :, :], trig[:, 1, :, :], -1.0, None, ALU.mult))
                N16 = NB * TT
                for q in range(2):
                    w2_ = wqk[:, q, 0:12].rearrange("p (j e) -> p j e", e=2)
                    c_o = cs_all[:, :, 0, q, 0:12].rearrange("p n (j e) -> p n j e", e=2)
                    s_o = cs_all[:, :, 1, q, 0:12].rearrange("p n (j e) -> p n j e", e=2)
                    done(v.tensor_tensor(c_o, bcast(trig[:, 0, :, :], 3, 2), bcast(w2_, 1, N16), ALU.mult))
                    done(v.tensor_copy(cs_all[:, :, 0, q, 12:16], bcast(wqk[:, q, 12:16], 1, N16)))
                    done(v.tensor_tensor(s_o[:, :, :, 0], kk[:, 1, :, :], bcast(w2_[:, :, 1], 1, N16), ALU.mult))
                    done(v.tensor_tensor(s_o[:, :, :, 1], trig[:, 1, :, :], bcast(w2_[:, :, 0], 1, N16), ALU.mult))
                    done(v.memset(cs_all[:, :, 1, q, 12:16], 0.0))
                v.memset(grow[:, 3, :], 0.0).then_inc(trig_done, 1)
                dve.wait_ge(trig_done, 1)
            dve.wait_ge(s_init, 4)
            dve.wait_ge(const_in, 16 * 5)
            if L == 1:
                dve.wait_ge(mod_silu, 1)
                done(v.scalar_tensor_tensor(out=cact[:, :, :], in0=cact[:, :, :], scalar=1.0, in1=cT[:, :, :], op0=ALU.add, op1=ALU.mult))
                v.tensor_scalar(cact[:, :, :], cact[:, :, :], 0.5, None, ALU.mult).then_inc(mod_silu, 1)
            else:
                v.tensor_copy(cact[:, :, :], cT[:, :, :]).then_inc(mod_silu, 2)
            for q in range(4):
                dve.wait_ge(mod_mm, 1 + q // 2)
                src = [T[0], T[1], S[0], S[1]][q]
                done(v.tensor_tensor(modr[:, 384 * q:384 * q + 384], src[0:NB, 0:384], bmod[:, 384 * q:384 * q + 384], ALU.add))
            done(v.tensor_copy(grow[:, 1, :], modr[:, 512:768]))
            done(v.tensor_tensor(grow[:, 0, :], modr[:, 512:768], bo8[:, 0, :], ALU.mult))
            if L == 1:
                done(v.tensor_tensor(grow[:, 3, :], modr[:, 1280:1536], bo8[:, 1, :], ALU.mult))
            v.tensor_copy(grow[:, 2, :], modr[:, 1280:1536]).then_inc(mod_row, 1)
            dve.wait_ge(mod_T, 1)
            for j in range(8):
                src = V[0][:, 8 * j:8 * j + 8]
                out = ab_all[:, :, j]
                if j % 4 < 2:
                    if L == 0:
                        k = (j // 4) * 2 + j % 2
                        ins = v.tensor_scalar(out, src, 1.0, wn[:, k:k + 1], ALU.add, ALU.mult)
                    else:
                        ins = v.tensor_scalar(out, src, 1.0, None, ALU.add)
                else:
                    ins = v.tensor_copy(out, src)
            ins.then_inc(mod_ab, 1)
            for n, (k, c, m) in enumerate(chunks):
                dve.wait_ge(raw_hi, n + 1)
                cols = [x[k][:, :, :].rearrange("p a b -> p (a b)")[:, c:c + m] for x in (hi, lo)]
                v.tensor_tensor(cols[1], raw[:, n % 2, 0:m], cols[0].bitcast(F32), ALU.subtract).then_inc(raw_lo, 1)

            def norm_stats(ch, x, st, ag, ms, ms_ok):
                for t in range(TT):
                    ins = v.bn_stats(st[:, t, :], x[:, t, :])
                ch.link(ins)
                ch.wait(dve)
                v.tensor_copy(held[:, :], mhalf[:, 0:1])
                for t in range(TT):
                    ins = v.bn_aggr(ag[:, t, :], st[:, t, :])
                ch.link(ins)
                ch.wait(dve)
                if L == 0:
                    ch.link(v.tensor_tensor(ms, ag[:, :, 0], ag[:, :, 0], ALU.mult))
                    ch.wait(dve)
                    v.scalar_tensor_tensor(out=ms, in0=ms, scalar=cfg["eps"], in1=ag[:, :, 1], op0=ALU.add, op1=ALU.add).then_inc(ms_ok.sem, 1)
                else:
                    v.tensor_scalar(ms, ag[:, :, 1], cfg["eps"], None, ALU.add).then_inc(ms_ok.sem, 1)

            def normed(out, x, ag, rs, out_ok):
                for t in range(TT):
                    if L == 0:
                        ins = v.tensor_scalar(out[:, t, :], x[:, t, :], rs[:, t:t + 1], None, ALU.mult)
                    else:
                        ins = v.tensor_scalar(out[:, t, :], x[:, t, :], ag[:, t, 0:1], rs[:, t:t + 1], ALU.subtract, ALU.mult)
                    ins.then_inc(out_ok.sem, 1)

            def norm1(n):
                x_loaded.wait(dve, n, 16)
                norm_stats(chain_a, x_in, stat, aggr, msq[:, :], ms1)
                rstd1.wait(dve, n, 1)
                h_full.wait(dve, n, 0)
                normed(xn, x_in, aggr, rstd, xn_ok)

            def norm2(b):
                x2_ok.wait(dve, b, TT)
                norm_stats(chain_m, x2, stat2, aggr2, msq2[:, :], ms2)
                rs2.wait(dve, b, 1)
                normed(xn2, x2, aggr2, rstd2, xn2_ok)

            def modulated(kind, n, b, name, out, ab, ok, hi_read, lo_read):
                for ft in range(FT):
                    bank = t_read(dve, kind, n, f"{name}{ft}")
                    hi_read.wait(dve, b, 0)
                    lo_read.wait(dve, b, 0)
                    v.tensor_scalar(out[:, ft, :], bank[:, 0:NTOK], ab[:, ft:ft + 1], ab[:, 2 + ft:3 + ft],
                                    ALU.mult, ALU.add).then_inc(ok.sem, 1)

            def ot_low(kind, n, b):
                for i in range(ot_lo.per):
                    bank = T[ORD[kind].index(f"oT{i}") % 2]
                    ot_hi.wait(dve, b, i + 1)
                    w2_gated.wait(dve, b, 0)
                    sl = slice(2 * i, 2 * i + 2) if L else slice(i, i + 1)
                    flat = lambda x: x[:, sl, :].rearrange("p a b -> p (a b)")
                    v.tensor_tensor(flat(otlo), bank[:, 0:512 if L else 256], flat(othi).bitcast(F32), ALU.subtract).then_inc(ot_lo.sem, 1)

            def residual1(kind, n, b):
                par2.wait(dve, b, 32)
                xr_ok.wait(dve, b, 1)
                for t in range(TT):
                    bank = t_read(dve, kind, n, f"pj{t}")
                    v.tensor_tensor(x2[:, t, :], bank[:, 0:D], g12[:, 0, :], ALU.mult).then_inc(pj_gated.sem, 1)
                    pj_gated.wait(dve, b, t + 1)
                    v.tensor_tensor(x2[:, t, :], x2[:, t, :], xr[:, t, :], ALU.add).then_inc(x2_ok.sem, 1)

            def residual2(kind, n, b):
                if L == 1:
                    chain_m.link(v.tensor_tensor(x2[:, :, :], x2[:, :, :], bcast(g12[:, 2, :], 1, TT), ALU.add))
                y_stored.wait(dve, b, 0)
                for t in range(TT):
                    bank = t_read(dve, kind, n, f"w2{t}")
                    v.tensor_tensor(yo[:, t, :], bank[:, 0:D], g12[:, 1, :], ALU.mult).then_inc(w2_gated.sem, 1)
                    w2_gated.wait(dve, b, t + 1)
                    v.tensor_tensor(yo[:, t, :], yo[:, t, :], x2[:, t, :], ALU.add).then_inc(y_ok.sem, 1)

            def head_squares(n, t):
                qraw_ok.wait(dve, n, t + 1)
                chain_a.link(v.tensor_tensor(sq[:, :], qraw[:, t, :], qraw[:, t, :], ALU.mult))
                chain_a.wait(dve)
                chain_a.link(v.tensor_reduce(hss[:, t, :], sq[:, :].rearrange("p (h d) -> p h d", d=16), AX.X, ALU.add))
                chain_a.wait(dve)
                v.tensor_scalar(hss[:, t, :], hss[:, t, :], 1.0 / 16, cfg["eps"], ALU.mult, ALU.add).then_inc(hss_ok.sem, 1)

            def head_rotate(n, t):
                hr_ok.wait(dve, n, t + 1)
                m1_ok.wait(dve, n - 1, t + 1)
                i3 = qraw[:, t, :].rearrange("p (h d) -> p h d", d=16)
                n3 = qn[:, t, :].rearrange("p (h d) -> p h d", d=16)
                v.tensor_tensor(n3, i3, bcast(hr[:, t, :], 2, 16), ALU.mult).then_inc(qn_ok.sem, 1)
                qn_ok.wait(dve, n, t + 1)
                par1.wait(dve, n, par1.per)
                n5 = qn[:, t, :].rearrange("p (q h j e) -> p q h j e", q=2, h=HEADS, e=2)
                m5 = m2[:, :, :].rearrange("p (q h) (j e) -> p q h j e", q=2, e=2)
                s5 = cs[:, t, 1, :, :].rearrange("p q (j e) -> p q j e", e=2)
                for e in range(2):
                    for q in range(2):
                        ins = v.tensor_tensor(m5[:, q, :, :, e], n5[:, q, :, 0:6, 1 - e],
                                              bcast(s5[:, q, 0:6, e], 1, HEADS), ALU.mult)
                chain_a.link(ins)
                chain_a.wait(dve)
                m1_ok.wait(dve, n, t + 1)
                f3 = m1[:, t, :].rearrange("p (h d) -> p h d", d=16)[:, :, 0:12]
                v.tensor_tensor(f3, f3, m2[:, :, :], ALU.add).then_inc(qf_ok.sem, 1)

            def stack_low(n, t):
                qf_ok.wait(dve, n, t + 1)
                f = m1[:, t, :].rearrange("p (q h d) -> p q h d", q=2, h=HEADS)
                for q in range(2):
                    st_hi.wait(dve, n, 2 * t + q + 1)
                    at = 32 if q == 0 else 16
                    v.tensor_tensor(stack[:, q, :, at:at + 16], f[:, q], stack[:, q, :, 0:16].bitcast(F32), ALU.subtract).then_inc(st_lo.sem, 1)

            def qk_low(kind, n, u):
                bank = T[ORD[kind].index(f"qk{u}") % 2]
                qk_hi.wait(dve, n, u + 1)
                p_full.wait(dve, n, 2 * (u - 1))
                v.tensor_tensor(qklo[:, u % 2, :], bank[:, :], qkhi[:, u % 2, :].bitcast(F32), ALU.subtract).then_inc(qk_lo.sem, 1)

            def maxima(n, u):
                for hh in range(2):
                    s_full.wait(dve, n, 2 * u + hh + 1)
                    ins = v.tensor_reduce(negm[:, hh, :], S[hh][:, :].rearrange("p (t k) -> p t k", t=TT), AX.X, ALU.max, negate=True)
                chain_a.link(ins)
                chain_a.wait(dve)
                mT_full.wait(dve, n, u)
                m_src = negm[:, :, :].rearrange("p h t -> p t h")
                m_hi = mcols[:, :, :, 0]
                neg_hi = mhi[:, :, :].rearrange("p h t -> p t h")
                v.tensor_copy(mhi[:, :, :], negm[:, :, :]).then_inc(mh_ok.sem, 1)
                mh_ok.wait(dve, n, 2 * u + 1)
                v.tensor_copy(m_hi, neg_hi.bitcast(F32)).then_inc(mh_ok.sem, 1)
                v.tensor_tensor(mcols[:, :, :, 1], m_src, neg_hi.bitcast(F32), ALU.subtract).then_inc(m_ok.sem, 1)

            def outputs(n, u):
                av_full.wait(dve, n, 2 * u + 2)
                ot_lo.wait(dve, n, 0)
                o_ok.wait(dve, n, u)
                vb = V[u % 2][:, 0:4 * DHA].rearrange("p (t h d) -> p t h d", t=TT, d=DHA)
                v.reciprocal(rden[:, :, :], vb[:, :, :, DH]).then_inc(rd_ok.sem, 1)
                rd_ok.wait(dve, n, u + 1)
                out = o_tok[:, :, 2 * u * DH:(2 * u + 2) * DH].rearrange("p t (h d) -> p t h d", h=2)
                v.tensor_tensor(out, vb[:, :, :, 0:DH], bcast(rden[:, :, :], 3, DH), ALU.mult).then_inc(o_ok.sem, 1)

            def body(kind, n):
                A, M = kind != "last", kind != "first"
                b = n - 1
                if A:
                    chain_a.start(n)
                if M:
                    chain_m.start(b)
                    ot_low(kind, n, b)
                if A:
                    norm1(n)
                    par1.wait(dve, n, par1.per)
                    modulated(kind, n, n, "xnT", hfull, ab1, h_full, h_hi, h_lo)
                if A and L == 0:
                    head_squares(n, 0)
                if M:
                    residual1(kind, n, b)
                    norm2(b)
                if A and L == 0:
                    head_rotate(n, 0)
                    head_squares(n, 1)
                if A and L == 1:
                    qk_low(kind, n, 0)
                    qk_low(kind, n, 1)
                if M:
                    modulated(kind, n, b, "h2T", h2full, ab2, h2_full, h2_hi, h2_lo)
                if A and L == 0:
                    stack_low(n, 0)
                    head_rotate(n, 1)
                if M and L == 0:
                    for i in range(HID):
                        swiglu(kind, n, b, i)
                if M:
                    residual2(kind, n, b)
                    chain_m.end()
                if A:
                    if L == 0:
                        stack_low(n, 1)
                    for u in range(UNITS):
                        maxima(n, u)
                        if L == 1 and u + 2 < UNITS:
                            qk_low(kind, n, u + 2)
                        if u >= 1:
                            outputs(n, u - 1)
                    outputs(n, UNITS - 1)
                    chain_a.end()

            def swiglu(kind, n, b, i):
                bank = T[ORD[kind].index(f"hid{i}") % 2]
                tanh_ok.wait(dve, b, i + 1)
                v.scalar_tensor_tensor(out=t1[:, i % 2, :], in0=th[:, i % 2, :], scalar=1.0, in1=bank[:, 0:256],
                                       op0=ALU.add, op1=ALU.mult).then_inc(sw_ok.sem, 1)
                sw_ok.wait(dve, b, i + 1)
                a_lo.wait(dve, b, i - 1)
                v.scalar_tensor_tensor(out=afull[:, i % 2, :], in0=bank[:, 256:512], scalar=0.5, in1=t1[:, i % 2, :],
                                       op0=ALU.mult, op1=ALU.mult).then_inc(a_full.sem, 1)

            bodies(dve, body)

        @block.tensor
        def _(pe):
            mm = nc.tensor.matmul
            pe.wait_ge(mod_silu, 2)
            pe.wait_ge(s_ident, 2)
            for h in range(2):
                pe.wait_ge(mod_in[h], 16)
                for j in range(2):
                    bank = (T, S)[h][j]
                    modw = raw[:, h, :].rearrange("p (k n) -> p k n", k=FT)
                    for k in range(FT):
                        ins = mm(bank[0:NB, 0:384], cact[:, k, :], modw[:, k, j * 384:(j + 1) * 384], start=(k == 0), stop=(k == FT - 1))
                ins.then_inc(mod_mm, 1)
            pe.wait_ge(mod_row, 1)
            comps = [256, 384, 0, 128, 1024, 1152, 768, 896]
            for j, c in enumerate(comps):
                ins = nc.tensor.transpose(V[0][:, 8 * j:8 * j + 8], modr[:, c:c + P], ident[0:NB, 0:NB])
            ins.then_inc(mod_T, 1)
            pe.wait_ge(mod_ab, 1)
            pe.wait_ge(s_init, 4)
            pe.wait_ge(s_sel, 2)
            pe.wait_ge(raw_lo, len(chunks))

            def split_mm(out, wts, mov, first, last):
                parts = [(0, 0), (1, 0), (0, 1)]
                for j, (a_, b_) in enumerate(parts):
                    ins = mm(out, wts[a_], mov[b_], start=first and j == 0, stop=last and j == 2)
                return ins

            def xnT(kind, n, name, src, ok, b):
                ok.wait(pe, b, TT)
                for ft in range(FT):
                    bank, full = t_claim(pe, kind, n, f"{name}{ft}")
                    for t in range(TT):
                        ins = nc.tensor.transpose(bank[:, t * P:(t + 1) * P], src[:, t, ft * P:(ft + 1) * P], ident[:, :])
                    ins.then_inc(full, 1)

            def tok_major(bank, xs, ws, t, c0, c1, kt):
                for k in range(kt):
                    ins = split_mm(bank[:, 0:c1 - c0], [x[:, k, t * P:(t + 1) * P] for x in xs],
                                   [y[:, k, c0:c1] for y in ws], k == 0, k == kt - 1)
                return ins

            wp = {k: (hi[k], lo[k]) for k in shapes}

            def qkv0(kind, n, t):
                h_lo.wait(pe, n, FT)
                h_hi.wait(pe, n, FT)
                bank, full = t_claim(pe, kind, n, f"qk{t}")
                tok_major(bank, (hhi, hlo), wp["wqkv"], t, 0, 512, FT).then_inc(full, 1)
                bank, full = t_claim(pe, kind, n, f"v{t}")
                tok_major(bank, (hhi, hlo), wp["wqkv"], t, 512, 768, FT).then_inc(full, 1)

            def v1_(kind, n):
                h_lo.wait(pe, n, FT)
                h_hi.wait(pe, n, FT)
                for i in range(4):
                    bank, full = t_claim(pe, kind, n, f"v{i}")
                    c = 2048 + 512 * (i % 2)
                    tok_major(bank, (hhi, hlo), wp["wqkv"], i // 2, c, c + 512, FT).then_inc(full, 1)

            def qk1(kind, n, u):
                bank, full = t_claim(pe, kind, n, f"qk{u}")
                for q in range(2):
                    c = q * 1024 + u * P
                    for k in range(FT):
                        ins = split_mm(bank[:, q * 256:(q + 1) * 256], [x[:, k, c:c + P] for x in wp["wqkv"]],
                                       [x[:, k, :] for x in (hhi, hlo)], k == 0, k == FT - 1)
                ins.then_inc(full, 1)

            def oT(kind, n, b):
                o_ok.wait(pe, b, UNITS)
                per = INNER // P // ot_lo.per
                for i in range(ot_lo.per):
                    bank, full = t_claim(pe, kind, n, f"oT{i}")
                    for j in range(per):
                        for t in range(TT):
                            c = (i * per + j) * P
                            ins = nc.tensor.transpose(bank[:, j * 256 + t * P:j * 256 + (t + 1) * P], o_tok[:, t, c:c + P], ident[:, :])
                    ins.then_inc(full, 1)

            def project(kind, n, b):
                ot_lo.wait(pe, b, ot_lo.per)
                ot_hi.wait(pe, b, ot_hi.per)
                for t in range(TT):
                    bank, full = t_claim(pe, kind, n, f"pj{t}")
                    tok_major(bank, (othi, otlo), wp["wo"], t, 0, D, KO).then_inc(full, 1)

            def hidden(kind, n, b):
                h2_lo.wait(pe, b, FT)
                h2_hi.wait(pe, b, FT)
                for i in range(HID if L == 0 else HID // 2):
                    bank, full = t_claim(pe, kind, n, f"hid{i}")
                    for j in range(2):
                        ws, c = (wp["w3" if j else "w1"], i * P) if L == 0 else (wp["w1"], (2 * i + j) * P)
                        for k in range(FT):
                            ins = split_mm(bank[:, j * 256:(j + 1) * 256], [x[:, k, c:c + P] for x in ws],
                                           [x[:, k, :] for x in (h2hi, h2lo)], k == 0, k == FT - 1)
                    ins.then_inc(full, 1)

            def down(kind, n, b):
                a_lo.wait(pe, b, HID)
                a_hi.wait(pe, b, HID)
                for t in range(TT):
                    bank, full = t_claim(pe, kind, n, f"w2{t}")
                    tok_major(bank, (ahi, alo), wp["w2"], t, 0, D, HID).then_inc(full, 1)

            def qkT0(kind, n, i):
                t, q, half = i // 4, (i // 2) % 2, i % 2
                st_lo.wait(pe, n, 2 * t + 2)
                bank, full = t_claim(pe, kind, n, f"qkT{i}")
                for j in range(4):
                    u = 4 * half + j
                    ins = nc.tensor.transpose(bank[:, j * P:(j + 1) * P],
                                              stack[:, q, 2 * u:2 * u + 2, :].rearrange("p h r -> p (h r)").bitcast(F32), ident[:, :])
                ins.then_inc(full, 1)

            def head_rows(n, u, hh):
                if L == 0:
                    r = slice(64 * hh, 64 * hh + QK_ROWS)
                    return [(qkT[r, 0, u, :], qkT[r, 1, u, :])]
                r = slice(64 * hh, 64 * hh + 64)
                q = [x[r, u % 2, 0:256] for x in (qkhi, qklo)]
                k = [x[r, u % 2, 256:512] for x in (qkhi, qklo)]
                return [(q[0], k[0]), (q[1], k[0]), (q[0], k[1])]

            def scores(n, u):
                if L == 0:
                    qkT_ok.wait(pe, n, 8)
                else:
                    qk_lo.wait(pe, n, u + 1)
                mT_ok.wait(pe, n, u)
                for hh in range(2):
                    prods = head_rows(n, u, hh)
                    for t in range(TT):
                        for j, (q, k) in enumerate(prods):
                            ins = mm(S[hh][:, t * 256:(t + 1) * 256], q[:, t * P:(t + 1) * P], k, start=(j == 0), stop=(j == len(prods) - 1))
                    ins.then_inc(s_full.sem, 1)

            def maxT(n, u):
                m_ok.wait(pe, n, u + 1)
                for t in range(TT):
                    ins = nc.tensor.transpose(S[0][0:4, t * P:(t + 1) * P], mcols[:, t, :, :].rearrange("p h s -> p (h s)"), ident[:, :])
                ins.then_inc(mT_full.sem, 1)

            def scores_T(n, u):
                mT_ok.wait(pe, n, u + 1)
                for hh in range(2):
                    p_ok.wait(pe, n, 2 * u + hh - 1)
                    prods = head_rows(n, u, hh)
                    for kt in range(TT):
                        out = PB[hh][:, kt * 256:(kt + 1) * 256]
                        mm(out, sel[0:4, hh, :], mT[0:4, :], start=True, stop=False)
                        for j, (q, k) in enumerate(prods):
                            ins = mm(out, k[:, kt * P:(kt + 1) * P], q, start=False, stop=(j == len(prods) - 1))
                    ins.then_inc(p_full.sem, 1)

            def weigh(n, u, hh):
                if hh == 0:
                    v_ok.wait(pe, n, v_ok.per)
                    o_ok.wait(pe, n, u - 1)
                p_ok.wait(pe, n, 2 * u + hh + 1)
                for t in range(TT):
                    c = (2 * t + hh) * DHA
                    for kt in range(TT):
                        ins = mm(V[u % 2][:, c:c + DHA], pt[:, (2 * u + hh) % 4, kt * 256 + t * P:kt * 256 + (t + 1) * P],
                                 vaug[:, kt, 2 * u + hh, :], start=(kt == 0), stop=(kt == 1))
                ins.then_inc(av_full.sem, 1)

            def body(kind, n):
                A, M = kind != "last", kind != "first"
                b = n - 1
                if M:
                    oT(kind, n, b)
                if A:
                    xnT(kind, n, "xnT", xn, xn_ok, n)
                    if L == 0:
                        qkv0(kind, n, 0)
                    else:
                        v1_(kind, n)
                if M:
                    project(kind, n, b)
                if A:
                    if L == 0:
                        qkv0(kind, n, 1)
                    else:
                        qk1(kind, n, 0)
                        qk1(kind, n, 1)
                if M:
                    xnT(kind, n, "h2T", xn2, xn2_ok, b)
                    hidden(kind, n, b)
                if L == 0:
                    if A:
                        for i in range(4):
                            qkT0(kind, n, i)
                    if M:
                        down(kind, n, b)
                    if A:
                        for i in range(4, 8):
                            qkT0(kind, n, i)
                elif M:
                    down(kind, n, b)
                if A:
                    for u in range(UNITS):
                        scores(n, u)
                        if u >= 1:
                            weigh(n, u - 1, 0)
                        maxT(n, u)
                        if u >= 1:
                            weigh(n, u - 1, 1)
                        if L == 1 and u + 2 < UNITS:
                            qk1(kind, n, u + 2)
                        scores_T(n, u)
                    weigh(n, UNITS - 1, 0)
                    weigh(n, UNITS - 1, 1)

            bodies(pe, body)


def build(nc, ins, out):
    x = ins["x"].rearrange("b (t p) d -> b p t d", p=P)
    y = out.rearrange("b (t p) d -> b p t d", p=P)
    mid = nc.dram_tensor("tokens_between", [NB, NTOK, D], F32, kind="Internal").ap().rearrange("b (t p) d -> b p t d", p=P)
    layers = []
    for L, names in enumerate([
        dict(wqkv="qkvT0", wo="projT0", w1="w1T0", w3="w3T0", w2="w2T0", wmod="adaT0"),
        dict(wqkv="W_qkv", wo="W_out", w1="W1", w2="W2", wmod="W_mod"),
    ]):
        w = {k: ins[v] for k, v in names.items()}
        w["cT"] = ins["cT"].rearrange("p (k b) -> p k b", k=FT)
        layers.append(w)
    layers[0] |= dict(bmod=ins["ada_b"], bo=ins["proj_b"], n1=ins["norm1"], n2=ins["norm2"], pos=ins["pos"],
                      qn=ins["q_norm"], kn=ins["k_norm"])
    layers[1] |= dict(bmod=ins["b_mod"], bo=ins["b_out"], b2=ins["b2"], b1=ins["b1"])
    for L in range(2):
        gates = nc.dram_tensor(f"gates{L}", [NB, 4 * D], F32, kind="Internal").ap()
        scratch = dict(gates=gates, g3=gates[:, D:4 * D])
        build_layer(nc, L, (x, mid)[L], (mid, y)[L], layers[L], scratch)


def kernel(**inputs):
    import numpy as _np
    import concourse.bacc as _bacc
    from concourse import mybir as _mybir
    from concourse.bass_utils import run_bass_kernel_spmd as _run

    def arr(name):
        return _np.asarray(inputs[name])

    def tiles(a):
        return a.reshape(-1, P, a.shape[1]).transpose(1, 0, 2).reshape(P, -1)

    def pad(a, n, axis):
        w = [(0, 0)] * a.ndim
        w[axis] = (0, n - a.shape[axis])
        return _np.pad(a, w)

    L0, L1 = "L0_cond_", "L1_cond_"
    host = dict(
        x=arr("x"),
        cT=tiles(arr("cond_1024").T),
        pos=arr("fside_BxSx3_0").reshape(NB * TT, P, 3).transpose(1, 0, 2),
        qkvT0=tiles(arr(L0 + "qkv_w").T), projT0=tiles(arr(L0 + "proj_w").T),
        w1T0=tiles(pad(arr(L0 + "w1").T, FF0P, 1)), w3T0=tiles(pad(arr(L0 + "w3").T, FF0P, 1)),
        w2T0=tiles(pad(arr(L0 + "w2").T, FF0P, 0)), adaT0=tiles(arr(L0 + "ada_w").T),
        ada_b=arr(L0 + "ada_b"), proj_b=arr(L0 + "proj_b"),
        norm1=arr(L0 + "norm1_w").reshape(FT, P).T, norm2=arr(L0 + "norm2_w").reshape(FT, P).T,
        q_norm=arr(L0 + "q_norm_w"), k_norm=arr(L0 + "k_norm_w"),
        W_mod=tiles(arr(L1 + "W_mod")), b_mod=arr(L1 + "b_mod"), W_qkv=tiles(arr(L1 + "W_qkv")), W_out=tiles(arr(L1 + "W_out")),
        b_out=arr(L1 + "b_out"), W1=tiles(arr(L1 + "W1")), b1=arr(L1 + "b1").reshape(8, P).T, W2=tiles(arr(L1 + "W2")), b2=arr(L1 + "b2"),
    )
    nc = _bacc.Bacc("TRN2", target_bir_lowering=False, num_devices=1)
    arrays, ins = {}, {}
    for name, a in host.items():
        a = _np.ascontiguousarray(a)
        arrays[f"in_{name}"] = a
        ins[name] = nc.dram_tensor(f"in_{name}", a.shape, _mybir.dt.from_np(a.dtype), kind="ExternalInput").ap()
    out = nc.dram_tensor("out", (NB, NTOK, D), F32, kind="ExternalOutput").ap()
    build(nc, ins, out)
    r = _run(nc, [arrays], core_ids=[0])
    return r.results[0]["out"]
```

```python
from contextlib import ExitStack
import math

import numpy as np
import concourse.bass as bass
from concourse import mybir

F32 = mybir.dt.float32
F32R = mybir.dt.float32r
ALU = mybir.AluOpType
ACT = mybir.ActivationFunctionType
AX = mybir.AxisListType

P = 128
NB = 8
NTOK = 256
TT = NTOK // P
D = 256
FT = D // P
HEADS = 16
UNITS = HEADS // 2
FF0 = 682
FF0P = 768
QK_ROWS = 48

LAYERS = [
    dict(dh=16, eps=1e-6, hid=FF0P // P, inner=256, qkv=768, scale=16 ** -0.5),
    dict(dh=64, eps=1e-5, hid=1024 // P, inner=1024, qkv=3072, scale=64 ** -0.5),
]


class Signal:

    def __init__(self, sem, per):
        self.sem, self.per = sem, per

    def wait(self, eng, b, k):
        v = b * self.per + k
        if isinstance(v, int) and v <= 0:
            return
        eng.wait_ge(self.sem, v)


def bcast(ap, axis, n):
    a = ap.unsqueeze(axis)
    shape = list(a.shape)
    shape[axis] = n
    return a.to_broadcast(shape)


def dense_uses(L, U, F, B):
    steps = {
        0: [["v0U", "v1U", "qkT4U", "qkT5U", "qkT6U", "qkT7U"],
            ["xnT0F", "xnT1F", "oT0B", "oT1B"],
            ["qk0F", "qk1F", "pj0B", "pj1B"],
            [],
            ["h2T0B", "h2T1B"],
            ["hid0B", "hid1B"],
            ["hid2B", "hid3B"],
            ["hid4B", "hid5B", "w20B", "w21B"]],
        1: [["qk3U"],
            ["v1U", "qk4U", "oT0B", "oT1B", "oT2B", "oT3B"],
            ["v3U", "qk5U"],
            ["qk6U", "pj0B", "pj1B"],
            ["qk7U", "xnT0F", "xnT1F", "h2T0B", "h2T1B"],
            ["qk0F", "hid0B", "hid1B", "hid2B", "hid3B"],
            ["qk1F", "v0F", "w20B"],
            ["qk2F", "v2F", "w21B"]],
    }[L]
    has = dict(U=U, F=F, B=B)
    out = []
    for u, names in enumerate(steps):
        if L == 0 and u == 6:
            out += [(f"qkT{i}", "F") for i in range(4) if F]
        if u < 7 and U:
            out.append((f"m{u + 1}", "U"))
        if u == 7 and F:
            out.append(("m0", "F"))
        out += [(x[:-1], x[-1]) for x in names if has[x[-1]]]
    return out


def parts_of(n):
    if isinstance(n, int):
        return 0 <= n < NB, n + 1 < NB, n >= 1
    return True, True, True


def build_layer(nc, L, x_src, y_dst, w, scratch):
    cfg = LAYERS[L]
    DH, HID, INNER, QKV = cfg["dh"], cfg["hid"], cfg["inner"], cfg["qkv"]
    KO = INNER // P
    QS = 4
    DHA = DH + 1
    NMOD = 6 * D

    ctx = ExitStack()
    with ctx:
        def sb(name, shape, dt=F32):
            return ctx.enter_context(nc.sbuf_tensor(f"{name}_{L}", shape, dt))

        def ps(name):
            return ctx.enter_context(nc.psum_tensor(f"{name}_{L}", [P, 512], F32))

        def sem(name):
            return ctx.enter_context(nc.semaphore(f"{name}_{L}"))

        shapes = dict(wqkv=[P, FT, QKV], wo=[P, KO, D], w1=[P, FT, HID * P], w2=[P, HID, D])
        if L == 0:
            shapes["w3"] = [P, FT, HID * P]
        hi = {k: sb(f"{k}_hi", s, F32R) for k, s in shapes.items()}
        lo = {k: sb(f"{k}_lo", s, F32R) for k, s in shapes.items()}
        CH = 1536
        raw = sb("raw", [P, 2, CH])
        chunks = []
        for k in ["wqkv", "wo", "w1", "w3", "w2"]:
            if k in shapes:
                n = shapes[k][1] * shapes[k][2]
                chunks += [(k, c, min(CH, n - c)) for c in range(0, n, CH)]

        ident = sb("ident", [P, P])
        x_in = sb("x_in", [P, TT, D])
        x_back = sb("x_back", [P, TT, D])
        xr = sb("xr", [P, TT, D])
        x2 = sb("x2", [P, TT, D])
        yo = sb("yo", [P, TT, D])
        xn = sb("xn", [P, TT, D])
        xn2 = sb("xn2", [P, TT, D])
        hfull = sb("hfull", [P, FT, NTOK])
        hhi = sb("hhi", [P, FT, NTOK], F32R)
        hlo = sb("hlo", [P, FT, NTOK], F32R)
        h2hi = sb("h2hi", [P, FT, NTOK], F32R)
        h2lo = sb("h2lo", [P, FT, NTOK], F32R)
        h2full = sb("h2full", [P, FT, NTOK])
        ab1 = sb("ab1", [P, 4])
        ab2 = sb("ab2", [P, 4])
        gates = sb("gates", [P, 4, D])
        held = sb("held", [P, 1])
        stat = sb("stat", [P, TT, 6])
        aggr = sb("aggr", [P, TT, 2])
        msq = sb("msq", [P, TT])
        rstd = sb("rstd", [P, TT])
        stat2 = sb("stat2", [P, TT, 6])
        aggr2 = sb("aggr2", [P, TT, 2])
        msq2 = sb("msq2", [P, TT])
        rstd2 = sb("rstd2", [P, TT])
        mhalf = sb("mhalf", [P, 32])
        vaug = sb("vaug", [P, TT, HEADS, DHA])
        negm = sb("negm", [P, 2, TT])
        mhi = sb("mhi", [P, 2, TT], F32R)
        mcols = sb("mcols", [P, TT, 2, 2])
        mT = sb("mT", [P, 2, NTOK], F32R)
        sel = sb("sel", [P, 2, P], F32R)
        pt = sb("pt", [P, 4, 512])
        rden = sb("rden", [P, TT, 2])
        o_tok = sb("o_tok", [P, TT, INNER])
        ahi = sb("ahi", [P, HID, NTOK], F32R)
        alo = sb("alo", [P, HID, NTOK], F32R)
        othi, otlo = ahi[:, 0:KO, :], alo[:, 0:KO, :]
        if L == 0:
            cs = sb("cs", [P, TT, 2, 2, 16])
            qraw = sb("qraw", [P, TT, 512])
            sq = sb("sq", [P, 512])
            hss = sb("hss", [P, TT, 32])
            hr = sb("hr", [P, TT, 32])
            qn = sb("qn", [P, TT, 512])
            m1 = sb("m1", [P, TT, 512])
            m2 = sb("m2", [P, 32, 12])
            stack = sb("stack", [P, TT, 2, HEADS, 64], F32R)
            qkT = sb("qkT", [P, 2, UNITS, NTOK], F32R)
            th = sb("th", [P, 2, NTOK])
            t1 = sb("t1", [P, 2, NTOK])
            afull = sb("afull", [P, 2, NTOK])
        else:
            qkhi = sb("qkhi", [P, QS, 512], F32R)
            qklo = sb("qklo", [P, QS, 512], F32R)
            afull = sb("afull", [P, 2, 512])
            b1c = sb("b1c", [P, HID])

        T = [ps("T0"), ps("T1")]
        S = [ps("S0"), ps("S1")]
        PB = [ps("P0"), ps("P1")]
        V = [ps("V0"), ps("V1")]

        raw_in, raw_hi, raw_lo = [sem("raw_in0"), sem("raw_in1")], sem("raw_hi"), sem("raw_lo")
        const_in, mod_in, s_init, s_ident, s_sel = sem("const_in"), [sem("mod_in0"), sem("mod_in1")], sem("init"), sem("ident_m"), sem("selm")
        mod_mm, mod_row, mod_T, mod_ab, mod_silu, gates_out, mod_chain = (
            sem("mod_mm"), sem("mod_row"), sem("mod_T"), sem("mod_ab"), sem("mod_silu"), sem("gates_out"), sem("mod_chain"))
        trig_in, trig_red, trig_sin, trig_done = sem("trig_in"), sem("trig_red"), sem("trig_sin"), sem("trig_done")
        t_full = [sem("t_full0"), sem("t_full1")]

        def sig(name, per):
            return Signal(sem(name), per)

        x_loaded, xb_loaded = sig("x_loaded", 16), sig("xb_loaded", 16)
        par1, par2 = sig("par1", 32 if L == 0 else 16), sig("par2", 32)
        ms1, rstd1, xn_ok = sig("ms1", 1), sig("rstd1", 1), sig("xn_ok", TT)
        ms2, rs2, xn2_ok = sig("ms2", 1), sig("rs2", 1), sig("xn2_ok", TT)
        h_full, h_hi, h_lo = sig("h_full", FT), sig("h_hi", FT), sig("h_lo", FT)
        h2_full, h2_hi, h2_lo = sig("h2_full", FT), sig("h2_hi", FT), sig("h2_lo", FT)
        xr_ok, x2_ok, y_ok, y_stored = sig("xr_ok", 1), sig("x2_ok", TT), sig("y_ok", TT), sig("y_stored", 16)
        w2_gated = sig("w2_gated", TT)
        v_ok = sig("v_ok", 2 if L == 0 else 4)
        s_full, max_ok, m_ok, mT_ok = sig("s_full", 16), sig("max_ok", 8), sig("m_ok", 8), sig("mT_ok", 8)
        stat1, stat2s = sig("stat1", 3 - L), sig("stat2", 3 - L)
        p_full, p_ok, av_full, o_ok = sig("p_full", 16), sig("p_ok", 16), sig("av_full", 16), sig("o_ok", 8)
        mh_ok, rd_ok, sw_ok = sig("mh_ok", 16), sig("rd_ok", 8), sig("sw_ok", HID)
        ot_hi, ot_lo = sig("ot_hi", 2 if L == 0 else 4), sig("ot_lo", 2 if L == 0 else 4)
        pj_gated = sig("pj_gated", TT)
        a_full, a_hi, a_lo = sig("a_full", HID), sig("a_hi", HID), sig("a_lo", HID)
        if L == 1:
            x2b_ok = sig("x2b_ok", 1)
        if L == 0:
            sq_ok, hsum_ok, m2_ok = sig("sq_ok", TT), sig("hsum_ok", TT), sig("m2_ok", TT)
            qraw_ok, hss_ok, hr_ok, qn_ok, m1_ok, qf_ok = (
                sig("qraw_ok", TT), sig("hss_ok", TT), sig("hr_ok", TT), sig("qn_ok", TT), sig("m1_ok", TT), sig("qf_ok", TT))
            st_hi, st_lo, qkT_ok, tanh_ok = (
                sig("st_hi", 2 * TT), sig("st_lo", 2 * TT), sig("qkT_ok", 8), sig("tanh_ok", HID))
        else:
            qk_hi, qk_lo = sig("qk_hi", 8), sig("qk_lo", 8)

        last_read = {f"xnT{i}": (h_full, i + 1) for i in range(FT)}
        last_read |= {f"h2T{i}": (h2_full, i + 1) for i in range(FT)}
        last_read |= {f"oT{i}": (ot_lo, i + 1) for i in range(ot_lo.per)}
        last_read |= {f"pj{i}": (pj_gated, i + 1) for i in range(TT)}
        last_read |= {f"w2{i}": (w2_gated, i + 1) for i in range(TT)}
        last_read |= {f"m{i}": (mT_ok, i + 1) for i in range(UNITS)}
        v_order = [0, 1] if L == 0 else [0, 2, 1, 3]
        last_read |= {f"v{i}": (v_ok, j + 1) for j, i in enumerate(v_order)}
        if L == 0:
            last_read |= {f"qk{i}": (qraw_ok, i + 1) for i in range(TT)}
            last_read |= {f"qkT{i}": (qkT_ok, i + 1) for i in range(8)}
            last_read |= {f"hid{i}": (a_full, i + 1) for i in range(HID)}
            hh_read = v_ok
        else:
            last_read |= {f"qk{i}": (qk_lo, i + 1) for i in range(UNITS)}
            last_read |= {f"hid{i}": (a_full, 2 * i + 2) for i in range(HID // 2)}
            hh_read = qk_lo

        uses = {n: dense_uses(L, *parts_of(n)) for n in range(-1, NB + 1)}
        per_body = len(uses[2])
        assert per_body % 2 == 0

        def uses_before(n):
            if isinstance(n, int):
                return sum(len(uses[i]) for i in range(-1, n)), 0
            return sum(len(uses[i]) for i in range(-1, 2)), n - 2

        def bank_of(n, name):
            names = [x for x, _ in uses[n if isinstance(n, int) else 2]]
            pos = names.index(name)
            return pos, (uses_before(n)[0] + pos) % 2

        def t_claim(eng, n, name):
            pos, bank = bank_of(n, name)
            if pos >= 2:
                at, (former, part) = n, uses[n if isinstance(n, int) else 2][pos - 2]
            elif uses_before(n)[0] + pos < 2:
                return T[bank], t_full[bank]
            else:
                at = n - 1
                former, part = uses[n - 1 if isinstance(n, int) else 2][pos - 2]
            s_, k = last_read[former]
            s_.wait(eng, at + {"U": 0, "F": 1, "B": -1}[part], k)
            return T[bank], t_full[bank]

        def t_read(eng, n, name):
            pos, bank = bank_of(n, name)
            const, more = uses_before(n)
            first = const + pos
            eng.wait_ge(t_full[bank], first // 2 + 1 + more * (per_body // 2))
            return T[bank]

        cT = sb("cT", [P, FT, NB])
        cact = sb("cact", [P, FT, NB])
        modr = sb("modr", [NB, NMOD]) if L == 0 else o_tok[0:NB, :, :].rearrange("p t c -> p (t c)")
        bmod = pt[0:NB, :, :].rearrange("p s c -> p (s c)")[:, 0:NMOD]
        grow = (qn if L == 0 else afull)[0:NB, :, :].rearrange("p a (b c) -> p (a b) c", b=2)
        bo8 = sb("bo8", [NB, 2, D])
        wn = sb("wn", [P, 4])
        abT = sb("abT", [P, 8, NB])
        ab_all = sb("ab_all", [P, NB, 8])
        if L == 0:
            pos = sb("pos", [P, NB * TT, 3])
            ang = sb("ang", [P, 2, NB * TT, 6])
            kk = sb("kk", [P, 2, NB * TT, 6])
            trig = sb("trig", [P, 2, NB * TT, 6])
            wqk = sb("wqk", [P, 2, 16])
            cs_all = sb("cs_all", [P, NB * TT, 2, 2, 16])

        block = ctx.enter_context(nc.Block())

        def bodies(eng, body):
            for n in (-1, 0, 1):
                body(n, *parts_of(n))
            with eng.Fori(2, NB - 1) as n:
                body(n, *parts_of(n))
            for n in (NB - 1, NB):
                body(n, *parts_of(n))

        def units_at(n, v, U, F, B):
            if v < 0:
                return (n - 1, v + UNITS) if B else None
            if v >= UNITS:
                return (n + 1, v - UNITS) if F else None
            return (n, v) if U else None

        @block.sync
        def _(sp):
            sp.dma_start(cT[:, :, :], w["cT"]).then_inc(const_in, 16)
            sp.dma_start(bmod[:, :], w["bmod"].partition_broadcast(NB)).then_inc(const_in, 16)
            sp.dma_start(bo8[:, 0, :], w["bo"].partition_broadcast(NB)).then_inc(const_in, 16)
            if L == 0:
                sp.dma_start(wn[:, 0:2], w["n1"]).then_inc(const_in, 16)
                sp.dma_start(wn[:, 2:4], w["n2"]).then_inc(const_in, 16)
                sp.dma_start(pos[:, :, :], w["pos"]).then_inc(trig_in, 16)
                sp.dma_start(wqk[:, 0, :], w["qn"].partition_broadcast(P)).then_inc(trig_in, 16)
                sp.dma_start(wqk[:, 1, :], w["kn"].partition_broadcast(P)).then_inc(trig_in, 16)
            else:
                sp.dma_start(bo8[:, 1, :], w["b2"].partition_broadcast(NB)).then_inc(const_in, 16)
                sp.dma_start(b1c[:, :], w["b1"]).then_inc(const_in, 16)
            for h in range(2):
                sp.dma_start(raw[:, h, :].rearrange("p (k n) -> p k n", k=FT), w["wmod"].rearrange("p (k n) -> p k n", k=FT)[:, :, h * 768:(h + 1) * 768]).then_inc(mod_in[h], 16)
            for n, (k, c, m) in enumerate(chunks):
                if n >= 2:
                    sp.wait_ge(raw_lo, n - 1)
                else:
                    sp.wait_ge(mod_mm, n + 1)
                src = w[k][:, c:c + m]
                sp.dma_start(raw[:, n % 2, 0:m], src).then_inc(raw_in[n % 2], 16)
            sp.wait_ge(mod_row, 1)
            sp.dma_start(scratch["gates"], grow[:, :, :].rearrange("b g d -> b (g d)")).then_inc(gates_out, 16)
            sp.wait_ge(gates_out, 16)
            sp.wait_ge(mod_ab, 1)
            if L == 0:
                sp.wait_ge(trig_done, 1)

            def load_front(b):
                xn_ok.wait(sp, b, 0)
                sp.dma_start(x_in[:, :, :], x_src[b]).then_inc(x_loaded.sem, 16)
                h_full.wait(sp, b, 0)
                if L == 0:
                    qf_ok.wait(sp, b, 0)
                sp.dma_start(ab1[:, :], ab_all[:, b, 0:4]).then_inc(par1.sem, 16)
                if L == 0:
                    sp.dma_start(cs[:, :, :, :, :].rearrange("p t c q d -> p t (c q d)"), cs_all[:, :, :, :, :].rearrange("p (n t) c q d -> p n t (c q d)", t=TT)[:, b]).then_inc(par1.sem, 16)

            def load_back(b):
                xr_ok.wait(sp, b, 0)
                sp.dma_start(x_back[:, :, :], x_src[b]).then_inc(xb_loaded.sem, 16)
                h2_full.wait(sp, b, 0)
                y_ok.wait(sp, b, 0)
                sp.dma_start(ab2[:, :], ab_all[:, b, 4:8]).then_inc(par2.sem, 16)
                sp.dma_start(gates[:, :, :], scratch["gates"][b].partition_broadcast(P)).then_inc(par2.sem, 16)

            def store(b):
                y_ok.wait(sp, b, TT)
                sp.dma_start(y_dst[b], yo[:, :, :]).then_inc(y_stored.sem, 16)

            def body(n, U, F, B):
                if B and not (isinstance(n, int) and n == 1):
                    store(n - 2)
                if F:
                    load_front(n + 1)
                if B:
                    load_back(n - 1)

            bodies(sp, body)
            store(NB - 1)
            y_stored.wait(sp, NB, 0)

        @block.gpsimd
        def _(pool):
            g = nc.gpsimd
            g.memset(ident[:, :], 0.0).then_inc(s_ident, 1)
            pool.wait_ge(s_ident, 1)
            g.affine_select(out=ident[:, :], in_=ident[:, :], compare_op=ALU.not_equal, fill=1.0,
                            base=0, pattern=[[-1, P]], channel_multiplier=1).then_inc(s_ident, 1)
            g.memset(mhalf[:, :], -0.5).then_inc(s_init, 1)
            g.memset(vaug[:, :, :, DH:DHA], 1.0).then_inc(s_init, 1)
            g.memset(negm[:, :, :], 0.0).then_inc(s_init, 1)
            if L == 0:
                g.memset(stack[:, :, :, :, 48:64].bitcast(F32), 0.0).then_inc(s_init, 1)
            else:
                g.memset(rden[:, :, :], 0.0).then_inc(s_init, 1)
            pool.wait_ge(s_init, 4)

            def power(out, in_, ok, ms, b, k):
                ms.wait(pool, b, k)
                g.tensor_tensor(out, in_, mhalf[:, 0:in_.shape[-1]], ALU.pow).then_inc(ok.sem, 1)

            def low(out, full, hi_, ok, hi_ok, b, k, read, rk):
                read.wait(pool, b, rk)
                hi_ok.wait(pool, b, k)
                g.tensor_tensor(out, full, hi_.bitcast(F32), ALU.subtract).then_inc(ok.sem, 1)

            def residual(n):
                xb_loaded.wait(pool, n, 16)
                par2.wait(pool, n, par2.per)
                x2_ok.wait(pool, n, 0)
                g.tensor_tensor(xr[:, :, :], x_back[:, :, :], bcast(gates[:, 0, :], 1, TT), ALU.add).then_inc(xr_ok.sem, 1)

            def h_low(n):
                for ft in range(FT):
                    low(hlo[:, ft, :], hfull[:, ft, :], hhi[:, ft, :], h_lo, h_hi, n, ft + 1, hh_read, 0)

            def h2_low(b):
                for ft in range(FT):
                    low(h2lo[:, ft, :], h2full[:, ft, :], h2hi[:, ft, :], h2_lo, h2_hi, b, ft + 1, a_full, 0)

            def head_norm(n, t):
                power(hr[:, t, :], hss[:, t, :], hr_ok, hss_ok, n, t + 1)

            def cos_part(n, t):
                st_lo.wait(pool, n - 1, 2 * t + 2)
                qn_ok.wait(pool, n, t + 1)
                o4 = m1[:, t, :].rearrange("p (q h d) -> p q h d", q=2, h=HEADS)
                i4 = qn[:, t, :].rearrange("p (q h d) -> p q h d", q=2, h=HEADS)
                g.tensor_tensor(o4, i4, bcast(cs[:, t, 0, :, :], 2, HEADS), ALU.mult).then_inc(m1_ok.sem, 1)

            def a_low(b, i):
                if L == 0:
                    low(alo[:, i, :], afull[:, i % 2, :], ahi[:, i, :], a_lo, a_hi, b, i + 1, pj_gated, TT)
                else:
                    j = i // 2
                    if i % 2 == 0:
                        low(alo[:, i, :], afull[:, j % 2, 0:256], ahi[:, i, :], a_lo, a_hi, b, i + 1, pj_gated, TT)
                    else:
                        low(alo[:, i, :], afull[:, j % 2, 256:512], ahi[:, i, :], a_lo, a_hi, b, i + 1, pj_gated, TT)

            def norm1_n(n):
                power(rstd[:, :], msq[:, :], rstd1, ms1, n, 1)

            def norm2_b(b):
                power(rstd2[:, :], msq2[:, :], rs2, ms2, b, 1)

            def body(n, U, F, B):
                f, b = n + 1, n - 1
                if L == 0:
                    if F:
                        norm1_n(f)
                    if B:
                        residual(b)
                    if F:
                        h_low(f)
                        head_norm(f, 0)
                        head_norm(f, 1)
                    if B:
                        norm2_b(b)
                    if F:
                        cos_part(f, 0)
                    if B:
                        h2_low(b)
                    if F:
                        cos_part(f, 1)
                else:
                    if B:
                        residual(b)
                    if F:
                        norm1_n(f)
                    if B:
                        norm2_b(b)
                    if F:
                        h_low(f)
                    if B:
                        h2_low(b)
                if B:
                    for i in range(HID):
                        a_low(b, i)

            bodies(pool, body)

        @block.scalar
        def _(act):
            a = nc.scalar
            if L == 0:
                act.wait_ge(trig_red, 1)
                a.activation(trig[:, :, :, :], ang[:, :, :, :], ACT.Sin).then_inc(trig_sin, 1)
            else:
                act.wait_ge(const_in, 16 * 5)
                a.activation(cact[:, :, :], cT[:, :, :], ACT.Tanh, scale=0.5).then_inc(mod_silu, 1)
            for n, (k, c, m) in enumerate(chunks):
                act.wait_ge(raw_in[n % 2], 16 * (n // 2 + 1))
                dst = hi[k][:, :, :].rearrange("p a b -> p (a b)")[:, c:c + m]
                a.copy(dst, raw[:, n % 2, 0:m]).then_inc(raw_hi, 1)

            def high(out, full, ok, full_ok, b, k, read, rk):
                read.wait(act, b, rk)
                full_ok.wait(act, b, k)
                a.copy(out, full).then_inc(ok.sem, 1)

            def h_high(n):
                for ft in range(FT):
                    high(hhi[:, ft, :], hfull[:, ft, :], h_hi, h_full, n, ft + 1, hh_read, 0)

            def h2_high(b):
                for ft in range(FT):
                    high(h2hi[:, ft, :], h2full[:, ft, :], h2_hi, h2_full, b, ft + 1, a_full, 0)

            def ot_high(n, b):
                for i in range(ot_hi.per):
                    bank = t_read(act, n, f"oT{i}")
                    w2_gated.wait(act, b, 0)
                    a.copy(othi[:, 2 * i:2 * i + 2, :].rearrange("p a b -> p (a b)") if L else othi[:, i, :],
                           bank[:, 0:512] if L else bank[:, 0:256]).then_inc(ot_hi.sem, 1)

            def qkv_raw(n, b, t):
                bank = t_read(act, n, f"qk{t}")
                qn_ok.wait(act, b - 1, t + 1)
                a.copy(qraw[:, t, :], bank[:, :]).then_inc(qraw_ok.sem, 1)

            def v_evac(n, b, i):
                bank = t_read(act, n, f"v{i}")
                if L == 0:
                    av_full.wait(act, b, 0)
                    out = vaug[:, i, :, 0:DH]
                    src = bank[:, 0:256].rearrange("p (h d) -> p h d", d=DH)
                else:
                    av_full.wait(act, b - 1, 8 + 8 * (i % 2))
                    out = vaug[:, i // 2, (i % 2) * 8:(i % 2) * 8 + 8, 0:DH]
                    src = bank[:, :].rearrange("p (h d) -> p h d", d=DH)
                a.copy(out, src).then_inc(v_ok.sem, 1)

            def stack_high(n, t):
                qkT_ok.wait(act, n, 0)
                qf_ok.wait(act, n, t + 1)
                f = m1[:, t, :].rearrange("p (q h d) -> p q h d", q=2, h=HEADS)
                a.copy(stack[:, t, 0, :, 0:32].rearrange("p h (r d) -> p h r d", r=2),
                       bcast(f[:, 0], 2, 2)).then_inc(st_hi.sem, 1)
                a.copy(stack[:, t, 1, :, 0:64].rearrange("p h (r d) -> p h r d", r=2)[:, :, :, 0:16],
                       bcast(f[:, 1], 2, 2)).then_inc(st_hi.sem, 1)

            def qkT_evac(n, b, i):
                half, t, q = i // 4, (i // 2) % 2, i % 2
                bank = t_read(act, n, f"qkT{i}")
                p_full.wait(act, b - 1, 8 + 8 * half)
                a.copy(qkT[:, q, 4 * half:4 * half + 4, t * P:(t + 1) * P],
                       bank[:, :].rearrange("p (u c) -> p u c", u=4)).then_inc(qkT_ok.sem, 1)

            def qk_high(n, b, u):
                bank = t_read(act, n, f"qk{u}")
                p_full.wait(act, b, 2 * (u - QS + 1))
                a.copy(qkhi[:, u % QS, :], bank[:, :]).then_inc(qk_hi.sem, 1)

            def m_evac(n, b, u):
                bank = t_read(act, n, f"m{u}")
                p_full.wait(act, b, 2 * (u - 1))
                a.copy(mT[0:4, u % 2, :], bank[0:4, 0:NTOK]).then_inc(mT_ok.sem, 1)

            def exps(b, u):
                for hh in range(2):
                    k = 2 * u + hh
                    p_full.wait(act, b, k + 1)
                    av_full.wait(act, b, k - 3)
                    a.activation(pt[:, k % 4, :], PB[hh][:, :], ACT.Exp, scale=cfg["scale"]).then_inc(p_ok.sem, 1)

            def hid_act(n, b, i):
                if L == 0:
                    bank = t_read(act, n, f"hid{i}")
                    a_full.wait(act, b, i - 1)
                    a.activation(th[:, i % 2, :], bank[:, 0:256], ACT.Tanh, scale=0.5).then_inc(tanh_ok.sem, 1)
                else:
                    bank = t_read(act, n, f"hid{i}")
                    a_lo.wait(act, b, 2 * i - 2)
                    for j in range(2):
                        ins = a.activation(afull[:, i % 2, 256 * j:256 * j + 256], bank[:, 256 * j:256 * j + 256],
                                           ACT.Gelu, bias=b1c[:, 2 * i + j:2 * i + j + 1])
                        ins.then_inc(a_full.sem, 1)
                    a_full.wait(act, b, 2 * i + 2)
                    pj_gated.wait(act, b, TT)
                    for j in range(2):
                        ins = a.copy(ahi[:, 2 * i + j, :], afull[:, i % 2, 256 * j:256 * j + 256])
                        ins.then_inc(a_hi.sem, 1)

            def a_high(b, i):
                high(ahi[:, i, :], afull[:, i % 2, :], a_hi, a_full, b, i + 1, pj_gated, TT)

            def body(n, U, F, B):
                f, b = n + 1, n - 1
                for u in range(UNITS):
                    if L == 0 and F and u == 6:
                        for i in range(4):
                            qkT_evac(n, f, i)
                    if w1_ := units_at(n, u + 1, U, F, False):
                        m_evac(n, *w1_)
                    if U:
                        exps(n, u)
                    if L == 0:
                        if U and u == 0:
                            v_evac(n, n, 0)
                            v_evac(n, n, 1)
                            for i in range(4, 8):
                                qkT_evac(n, n, i)
                        if F and u == 1:
                            h_high(f)
                        if B and u == 1:
                            ot_high(n, b)
                        if F and u == 2:
                            qkv_raw(n, f, 0)
                            qkv_raw(n, f, 1)
                        if F and u == 4:
                            stack_high(f, 0)
                        if B and u == 4:
                            h2_high(b)
                        if F and u == 5:
                            stack_high(f, 1)
                        if B and u >= 5:
                            for i in (2 * u - 10, 2 * u - 9):
                                hid_act(n, b, i)
                                a_high(b, i)
                    else:
                        if U and u in (1, 2):
                            v_evac(n, n, 2 * u - 1)
                        if w3_ := units_at(n, u + 3, U, F, False):
                            qk_high(n, *w3_)
                        if B and u == 1:
                            ot_high(n, b)
                        if F and u == 4:
                            h_high(f)
                        if B and u == 4:
                            h2_high(b)
                        if B and u == 5:
                            for i in range(4):
                                hid_act(n, b, i)
                        if F and u >= 6:
                            v_evac(n, f, 2 * u - 12)

            bodies(act, body)

        @block.vector
        def _(dve):
            v = nc.vector
            setup_steps = []

            def done(ins):
                ins.then_inc(mod_chain, 1)
                setup_steps.append(ins)
                dve.wait_ge(mod_chain, len(setup_steps))

            dve.wait_ge(s_ident, 2)
            for hh in range(2):
                v.tensor_tensor(sel[:, hh, :], ident[:, 2 * hh:2 * hh + 1].to_broadcast([P, P]),
                                ident[:, 2 * hh + 1:2 * hh + 2].to_broadcast([P, P]), ALU.add).then_inc(s_sel, 1)
            if L == 0:
                dve.wait_ge(trig_in, 48)
                freq = [1.0, 0.01]
                a_v = ang[:, 1, :, :].rearrange("p n (a h) -> p n a h", h=2)
                for h in range(2):
                    done(v.tensor_scalar(a_v[:, :, :, h], pos[:, :, :], freq[h], None, ALU.mult))
                magic = 1.5 * 2 ** 23
                c1 = 6.28125
                c2 = round((2 * math.pi - c1) * 2 ** 21) / 2 ** 21
                c3 = 2 * math.pi - c1 - c2
                sa, ca, kt = ang[:, 1, :, :], ang[:, 0, :, :], kk[:, 0, :, :]
                done(v.tensor_scalar(kt, sa, 1 / (2 * math.pi), magic, ALU.mult, ALU.add))
                done(v.tensor_scalar(kt, kt, magic, None, ALU.subtract))
                for c in (c1, c2, c3):
                    done(v.scalar_tensor_tensor(out=sa, in0=kt, scalar=-c, in1=sa, op0=ALU.mult, op1=ALU.add))
                pi = 3.1415925
                done(v.tensor_scalar(sa, sa, pi, -pi, ALU.min, ALU.max))
                done(v.tensor_scalar(ca, sa, math.pi / 2, None, ALU.add))
                done(v.tensor_scalar(kt, ca, pi, -2 * math.pi, ALU.is_gt, ALU.mult))
                done(v.tensor_tensor(ca, ca, kt, ALU.add))
                v.tensor_scalar(ca, ca, pi, -pi, ALU.min, ALU.max).then_inc(trig_red, 1)
                dve.wait_ge(trig_sin, 1)
                done(v.tensor_scalar(kk[:, 1, :, :], trig[:, 1, :, :], -1.0, None, ALU.mult))
                N16 = NB * TT
                for q in range(2):
                    w2_ = wqk[:, q, 0:12].rearrange("p (j e) -> p j e", e=2)
                    c_o = cs_all[:, :, 0, q, 0:12].rearrange("p n (j e) -> p n j e", e=2)
                    s_o = cs_all[:, :, 1, q, 0:12].rearrange("p n (j e) -> p n j e", e=2)
                    done(v.tensor_tensor(c_o, bcast(trig[:, 0, :, :], 3, 2), bcast(w2_, 1, N16), ALU.mult))
                    done(v.tensor_copy(cs_all[:, :, 0, q, 12:16], bcast(wqk[:, q, 12:16], 1, N16)))
                    done(v.tensor_tensor(s_o[:, :, :, 0], kk[:, 1, :, :], bcast(w2_[:, :, 1], 1, N16), ALU.mult))
                    done(v.tensor_tensor(s_o[:, :, :, 1], trig[:, 1, :, :], bcast(w2_[:, :, 0], 1, N16), ALU.mult))
                    done(v.memset(cs_all[:, :, 1, q, 12:16], 0.0))
                v.memset(grow[:, 3, :], 0.0).then_inc(trig_done, 1)
                dve.wait_ge(trig_done, 1)
            dve.wait_ge(s_init, 4)
            dve.wait_ge(const_in, 16 * 5)
            if L == 1:
                dve.wait_ge(mod_silu, 1)
                done(v.scalar_tensor_tensor(out=cact[:, :, :], in0=cact[:, :, :], scalar=1.0, in1=cT[:, :, :], op0=ALU.add, op1=ALU.mult))
                v.tensor_scalar(cact[:, :, :], cact[:, :, :], 0.5, None, ALU.mult).then_inc(mod_silu, 1)
            else:
                v.tensor_copy(cact[:, :, :], cT[:, :, :]).then_inc(mod_silu, 2)
            for q in range(4):
                dve.wait_ge(mod_mm, 1 + q // 2)
                src = [T[0], T[1], S[0], S[1]][q]
                done(v.tensor_tensor(modr[:, 384 * q:384 * q + 384], src[0:NB, 0:384], bmod[:, 384 * q:384 * q + 384], ALU.add))
            done(v.tensor_copy(grow[:, 1, :], modr[:, 512:768]))
            done(v.tensor_tensor(grow[:, 0, :], modr[:, 512:768], bo8[:, 0, :], ALU.mult))
            if L == 1:
                done(v.tensor_tensor(grow[:, 3, :], modr[:, 1280:1536], bo8[:, 1, :], ALU.mult))
            v.tensor_copy(grow[:, 2, :], modr[:, 1280:1536]).then_inc(mod_row, 1)
            dve.wait_ge(mod_T, 1)
            for j in range(8):
                src = V[0][:, 8 * j:8 * j + 8]
                out = ab_all[:, :, j]
                if j % 4 < 2:
                    if L == 0:
                        k = (j // 4) * 2 + j % 2
                        ins = v.tensor_scalar(out, src, 1.0, wn[:, k:k + 1], ALU.add, ALU.mult)
                    else:
                        ins = v.tensor_scalar(out, src, 1.0, None, ALU.add)
                else:
                    ins = v.tensor_copy(out, src)
            ins.then_inc(mod_ab, 1)
            for n, (k, c, m) in enumerate(chunks):
                dve.wait_ge(raw_hi, n + 1)
                cols = [x[k][:, :, :].rearrange("p a b -> p (a b)")[:, c:c + m] for x in (hi, lo)]
                v.tensor_tensor(cols[1], raw[:, n % 2, 0:m], cols[0].bitcast(F32), ALU.subtract).then_inc(raw_lo, 1)

            def norm_stats(st_ok, b, x, st, ag, ms, ms_ok):
                for t in range(TT):
                    ins = v.bn_stats(st[:, t, :], x[:, t, :])
                ins.then_inc(st_ok.sem, 1)
                st_ok.wait(dve, b, 1)
                v.tensor_copy(held[:, :], mhalf[:, 0:1])
                for t in range(TT):
                    ins = v.bn_aggr(ag[:, t, :], st[:, t, :])
                ins.then_inc(st_ok.sem, 1)
                st_ok.wait(dve, b, 2)
                if L == 0:
                    v.tensor_tensor(ms, ag[:, :, 0], ag[:, :, 0], ALU.mult).then_inc(st_ok.sem, 1)
                    st_ok.wait(dve, b, 3)
                    v.scalar_tensor_tensor(out=ms, in0=ms, scalar=cfg["eps"], in1=ag[:, :, 1], op0=ALU.add, op1=ALU.add).then_inc(ms_ok.sem, 1)
                else:
                    v.tensor_scalar(ms, ag[:, :, 1], cfg["eps"], None, ALU.add).then_inc(ms_ok.sem, 1)

            def normed(out, x, ag, rs, out_ok):
                for t in range(TT):
                    if L == 0:
                        ins = v.tensor_scalar(out[:, t, :], x[:, t, :], rs[:, t:t + 1], None, ALU.mult)
                    else:
                        ins = v.tensor_scalar(out[:, t, :], x[:, t, :], ag[:, t, 0:1], rs[:, t:t + 1], ALU.subtract, ALU.mult)
                    ins.then_inc(out_ok.sem, 1)

            def norm1(n):
                x_loaded.wait(dve, n, 16)
                norm_stats(stat1, n, x_in, stat, aggr, msq[:, :], ms1)
                rstd1.wait(dve, n, 1)
                h_full.wait(dve, n, 0)
                normed(xn, x_in, aggr, rstd, xn_ok)

            def norm2(b):
                x2_ok.wait(dve, b, TT)
                norm_stats(stat2s, b, x2, stat2, aggr2, msq2[:, :], ms2)
                rs2.wait(dve, b, 1)
                h2_full.wait(dve, b, 0)
                normed(xn2, x2, aggr2, rstd2, xn2_ok)

            def modulated(n, b, name, out, ab, ok, hi_read, lo_read):
                for ft in range(FT):
                    bank = t_read(dve, n, f"{name}{ft}")
                    hi_read.wait(dve, b, 0)
                    lo_read.wait(dve, b, 0)
                    v.tensor_scalar(out[:, ft, :], bank[:, 0:NTOK], ab[:, ft:ft + 1], ab[:, 2 + ft:3 + ft],
                                    ALU.mult, ALU.add).then_inc(ok.sem, 1)

            def ot_low(n, b):
                for i in range(ot_lo.per):
                    bank = T[bank_of(n, f"oT{i}")[1]]
                    ot_hi.wait(dve, b, i + 1)
                    w2_gated.wait(dve, b, 0)
                    sl = slice(2 * i, 2 * i + 2) if L else slice(i, i + 1)
                    flat = lambda x: x[:, sl, :].rearrange("p a b -> p (a b)")
                    v.tensor_tensor(flat(otlo), bank[:, 0:512 if L else 256], flat(othi).bitcast(F32), ALU.subtract).then_inc(ot_lo.sem, 1)

            def residual1(n, b):
                par2.wait(dve, b, 32)
                xr_ok.wait(dve, b, 1)
                y_ok.wait(dve, b, 0)
                for t in range(TT):
                    bank = t_read(dve, n, f"pj{t}")
                    v.tensor_tensor(x2[:, t, :], bank[:, 0:D], gates[:, 1, :], ALU.mult).then_inc(pj_gated.sem, 1)
                    pj_gated.wait(dve, b, t + 1)
                    v.tensor_tensor(x2[:, t, :], x2[:, t, :], xr[:, t, :], ALU.add).then_inc(x2_ok.sem, 1)

            def add_bias2(b):
                xn2_ok.wait(dve, b, TT)
                v.tensor_tensor(x2[:, :, :], x2[:, :, :], bcast(gates[:, 3, :], 1, TT), ALU.add).then_inc(x2b_ok.sem, 1)

            def residual2(n, b, t):
                y_stored.wait(dve, b, 0)
                if L == 1:
                    x2b_ok.wait(dve, b, 1)
                bank = t_read(dve, n, f"w2{t}")
                v.tensor_tensor(yo[:, t, :], bank[:, 0:D], gates[:, 2, :], ALU.mult).then_inc(w2_gated.sem, 1)
                w2_gated.wait(dve, b, t + 1)
                v.tensor_tensor(yo[:, t, :], yo[:, t, :], x2[:, t, :], ALU.add).then_inc(y_ok.sem, 1)

            def head_squares(n, t):
                qraw_ok.wait(dve, n, t + 1)
                hss_ok.wait(dve, n, t)
                v.tensor_tensor(sq[:, :], qraw[:, t, :], qraw[:, t, :], ALU.mult).then_inc(sq_ok.sem, 1)
                sq_ok.wait(dve, n, t + 1)
                v.tensor_reduce(hss[:, t, :], sq[:, :].rearrange("p (h d) -> p h d", d=16), AX.X, ALU.add).then_inc(hsum_ok.sem, 1)
                hsum_ok.wait(dve, n, t + 1)
                v.tensor_scalar(hss[:, t, :], hss[:, t, :], 1.0 / 16, cfg["eps"], ALU.mult, ALU.add).then_inc(hss_ok.sem, 1)

            def head_rotate(n, t):
                hr_ok.wait(dve, n, t + 1)
                m1_ok.wait(dve, n - 1, t + 1)
                i3 = qraw[:, t, :].rearrange("p (h d) -> p h d", d=16)
                n3 = qn[:, t, :].rearrange("p (h d) -> p h d", d=16)
                v.tensor_tensor(n3, i3, bcast(hr[:, t, :], 2, 16), ALU.mult).then_inc(qn_ok.sem, 1)
                qn_ok.wait(dve, n, t + 1)
                par1.wait(dve, n, par1.per)
                qf_ok.wait(dve, n, t)
                n5 = qn[:, t, :].rearrange("p (q h j e) -> p q h j e", q=2, h=HEADS, e=2)
                m5 = m2[:, :, :].rearrange("p (q h) (j e) -> p q h j e", q=2, e=2)
                s5 = cs[:, t, 1, :, :].rearrange("p q (j e) -> p q j e", e=2)
                for e in range(2):
                    for q in range(2):
                        ins = v.tensor_tensor(m5[:, q, :, :, e], n5[:, q, :, 0:6, 1 - e],
                                              bcast(s5[:, q, 0:6, e], 1, HEADS), ALU.mult)
                ins.then_inc(m2_ok.sem, 1)
                m2_ok.wait(dve, n, t + 1)
                m1_ok.wait(dve, n, t + 1)
                f3 = m1[:, t, :].rearrange("p (h d) -> p h d", d=16)[:, :, 0:12]
                v.tensor_tensor(f3, f3, m2[:, :, :], ALU.add).then_inc(qf_ok.sem, 1)

            def stack_low(n, t):
                qf_ok.wait(dve, n, t + 1)
                f = m1[:, t, :].rearrange("p (q h d) -> p q h d", q=2, h=HEADS)
                for q in range(2):
                    st_hi.wait(dve, n, 2 * t + q + 1)
                    at = 32 if q == 0 else 16
                    v.tensor_tensor(stack[:, t, q, :, at:at + 16], f[:, q], stack[:, t, q, :, 0:16].bitcast(F32), ALU.subtract).then_inc(st_lo.sem, 1)

            def qk_low(n, b, u):
                bank = T[bank_of(n, f"qk{u}")[1]]
                qk_hi.wait(dve, b, u + 1)
                p_full.wait(dve, b, 2 * (u - QS + 1))
                v.tensor_tensor(qklo[:, u % QS, :], bank[:, :], qkhi[:, u % QS, :].bitcast(F32), ALU.subtract).then_inc(qk_lo.sem, 1)

            def maxima(b, u):
                m_ok.wait(dve, b, u)
                for hh in range(2):
                    s_full.wait(dve, b, 2 * u + hh + 1)
                    ins = v.tensor_reduce(negm[:, hh, :], S[hh][:, :].rearrange("p (t k) -> p t k", t=TT), AX.X, ALU.max, negate=True)
                ins.then_inc(max_ok.sem, 1)
                max_ok.wait(dve, b, u + 1)
                mT_ok.wait(dve, b, u)
                by_tile = lambda x: x[:, :, :].rearrange("p h t -> p t h")
                v.tensor_copy(mhi[:, :, :], negm[:, :, :]).then_inc(mh_ok.sem, 1)
                mh_ok.wait(dve, b, 2 * u + 1)
                v.tensor_copy(mcols[:, :, :, 0], by_tile(mhi).bitcast(F32)).then_inc(mh_ok.sem, 1)
                v.tensor_tensor(mcols[:, :, :, 1], by_tile(negm), by_tile(mhi).bitcast(F32), ALU.subtract).then_inc(m_ok.sem, 1)

            def outputs(n, u):
                av_full.wait(dve, n, 2 * u + 2)
                ot_lo.wait(dve, n - 1, u // 2 + 1 if L else ot_lo.per)
                o_ok.wait(dve, n, u)
                vb = V[u % 2][:, 0:4 * DHA].rearrange("p (t h d) -> p t h d", t=TT, d=DHA)
                v.reciprocal(rden[:, :, :], vb[:, :, :, DH]).then_inc(rd_ok.sem, 1)
                rd_ok.wait(dve, n, u + 1)
                out = o_tok[:, :, 2 * u * DH:(2 * u + 2) * DH].rearrange("p t (h d) -> p t h d", h=2)
                v.tensor_tensor(out, vb[:, :, :, 0:DH], bcast(rden[:, :, :], 3, DH), ALU.mult).then_inc(o_ok.sem, 1)

            def body(n, U, F, B):
                f, b = n + 1, n - 1
                for u in range(UNITS):
                    if w2_ := units_at(n, u + 2, U, F, False):
                        maxima(*w2_)
                    if L == 1 and B and u == 4:
                        norm2(b)
                        add_bias2(b)
                    if w_2 := units_at(n, u - 2, U, False, B):
                        outputs(*w_2)
                    if L == 0:
                        if F and u == 0:
                            norm1(f)
                        if F and u == 1:
                            par1.wait(dve, f, par1.per)
                            modulated(n, f, "xnT", hfull, ab1, h_full, h_hi, h_lo)
                        if B and u == 1:
                            ot_low(n, b)
                        if F and u == 2:
                            head_squares(f, 0)
                            head_squares(f, 1)
                        if B and u == 2:
                            residual1(n, b)
                        if B and u == 3:
                            norm2(b)
                        if F and u == 3:
                            head_rotate(f, 0)
                        if B and u == 4:
                            modulated(n, b, "h2T", h2full, ab2, h2_full, h2_hi, h2_lo)
                        if F and u == 4:
                            stack_low(f, 0)
                            head_rotate(f, 1)
                        if F and u == 5:
                            stack_low(f, 1)
                        if B and u >= 5:
                            swiglu(n, b, 2 * u - 10)
                            swiglu(n, b, 2 * u - 9)
                        if B and u == 7:
                            residual2(n, b, 0)
                            residual2(n, b, 1)
                    else:
                        if w3_ := units_at(n, u + 3, U, F, False):
                            qk_low(n, *w3_)
                        if B and u == 1:
                            ot_low(n, b)
                        if F and u == 2:
                            norm1(f)
                        if B and u == 3:
                            residual1(n, b)
                        if F and u == 4:
                            par1.wait(dve, f, par1.per)
                            modulated(n, f, "xnT", hfull, ab1, h_full, h_hi, h_lo)
                        if B and u == 4:
                            modulated(n, b, "h2T", h2full, ab2, h2_full, h2_hi, h2_lo)
                        if B and u >= 6:
                            residual2(n, b, u - 6)

            def swiglu(n, b, i):
                bank = T[bank_of(n, f"hid{i}")[1]]
                tanh_ok.wait(dve, b, i + 1)
                v.scalar_tensor_tensor(out=t1[:, i % 2, :], in0=th[:, i % 2, :], scalar=1.0, in1=bank[:, 0:256],
                                       op0=ALU.add, op1=ALU.mult).then_inc(sw_ok.sem, 1)
                sw_ok.wait(dve, b, i + 1)
                a_lo.wait(dve, b, i - 1)
                v.scalar_tensor_tensor(out=afull[:, i % 2, :], in0=bank[:, 256:512], scalar=0.5, in1=t1[:, i % 2, :],
                                       op0=ALU.mult, op1=ALU.mult).then_inc(a_full.sem, 1)

            bodies(dve, body)

        @block.tensor
        def _(pe):
            mm = nc.tensor.matmul
            pe.wait_ge(mod_silu, 2)
            pe.wait_ge(s_ident, 2)
            for h in range(2):
                pe.wait_ge(mod_in[h], 16)
                for j in range(2):
                    bank = (T, S)[h][j]
                    modw = raw[:, h, :].rearrange("p (k n) -> p k n", k=FT)
                    for k in range(FT):
                        ins = mm(bank[0:NB, 0:384], cact[:, k, :], modw[:, k, j * 384:(j + 1) * 384], start=(k == 0), stop=(k == FT - 1))
                ins.then_inc(mod_mm, 1)
            pe.wait_ge(mod_row, 1)
            comps = [256, 384, 0, 128, 1024, 1152, 768, 896]
            for j, c in enumerate(comps):
                ins = nc.tensor.transpose(V[0][:, 8 * j:8 * j + 8], modr[:, c:c + P], ident[0:NB, 0:NB])
            ins.then_inc(mod_T, 1)
            pe.wait_ge(mod_ab, 1)
            pe.wait_ge(s_init, 4)
            pe.wait_ge(s_sel, 2)
            pe.wait_ge(raw_lo, len(chunks))

            def split_mm(out, wts, mov, first, last):
                parts = [(0, 0), (1, 0), (0, 1)]
                for j, (a_, b_) in enumerate(parts):
                    ins = mm(out, wts[a_], mov[b_], start=first and j == 0, stop=last and j == 2)
                return ins

            def xnT(n, name, src, ok, b):
                ok.wait(pe, b, TT)
                for ft in range(FT):
                    bank, full = t_claim(pe, n, f"{name}{ft}")
                    for t in range(TT):
                        ins = nc.tensor.transpose(bank[:, t * P:(t + 1) * P], src[:, t, ft * P:(ft + 1) * P], ident[:, :])
                    ins.then_inc(full, 1)

            def tok_major(bank, xs, ws, t, c0, c1, kt):
                for k in range(kt):
                    ins = split_mm(bank[:, 0:c1 - c0], [x[:, k, t * P:(t + 1) * P] for x in xs],
                                   [y[:, k, c0:c1] for y in ws], k == 0, k == kt - 1)
                return ins

            wp = {k: (hi[k], lo[k]) for k in shapes}

            def qk0(n, b, t):
                h_lo.wait(pe, b, FT)
                h_hi.wait(pe, b, FT)
                bank, full = t_claim(pe, n, f"qk{t}")
                tok_major(bank, (hhi, hlo), wp["wqkv"], t, 0, 512, FT).then_inc(full, 1)

            def values(n, b, i):
                h_lo.wait(pe, b, FT)
                h_hi.wait(pe, b, FT)
                bank, full = t_claim(pe, n, f"v{i}")
                t, c, m = (i, 512, 256) if L == 0 else (i // 2, 2048 + 512 * (i % 2), 512)
                tok_major(bank, (hhi, hlo), wp["wqkv"], t, c, c + m, FT).then_inc(full, 1)

            def qk1(n, b, u):
                h_lo.wait(pe, b, FT)
                h_hi.wait(pe, b, FT)
                bank, full = t_claim(pe, n, f"qk{u}")
                for q in range(2):
                    c = q * 1024 + u * P
                    for k in range(FT):
                        ins = split_mm(bank[:, q * 256:(q + 1) * 256], [x[:, k, c:c + P] for x in wp["wqkv"]],
                                       [x[:, k, :] for x in (hhi, hlo)], k == 0, k == FT - 1)
                ins.then_inc(full, 1)

            def oT(n, b):
                per = INNER // P // ot_lo.per
                for i in range(ot_lo.per):
                    o_ok.wait(pe, b, UNITS if L == 0 else 2 * i + 2)
                    bank, full = t_claim(pe, n, f"oT{i}")
                    for j in range(per):
                        for t in range(TT):
                            c = (i * per + j) * P
                            ins = nc.tensor.transpose(bank[:, j * 256 + t * P:j * 256 + (t + 1) * P], o_tok[:, t, c:c + P], ident[:, :])
                    ins.then_inc(full, 1)

            def project(n, b):
                ot_lo.wait(pe, b, ot_lo.per)
                ot_hi.wait(pe, b, ot_hi.per)
                for t in range(TT):
                    bank, full = t_claim(pe, n, f"pj{t}")
                    tok_major(bank, (othi, otlo), wp["wo"], t, 0, D, KO).then_inc(full, 1)

            def hidden(n, b, tiles_):
                h2_lo.wait(pe, b, FT)
                h2_hi.wait(pe, b, FT)
                for i in tiles_:
                    bank, full = t_claim(pe, n, f"hid{i}")
                    for j in range(2):
                        ws, c = (wp["w3" if j else "w1"], i * P) if L == 0 else (wp["w1"], (2 * i + j) * P)
                        for k in range(FT):
                            ins = split_mm(bank[:, j * 256:(j + 1) * 256], [x[:, k, c:c + P] for x in ws],
                                           [x[:, k, :] for x in (h2hi, h2lo)], k == 0, k == FT - 1)
                    ins.then_inc(full, 1)

            def down(n, b, t):
                a_lo.wait(pe, b, HID)
                a_hi.wait(pe, b, HID)
                bank, full = t_claim(pe, n, f"w2{t}")
                tok_major(bank, (ahi, alo), wp["w2"], t, 0, D, HID).then_inc(full, 1)

            def qkT0(n, b, i):
                half, t, q = i // 4, (i // 2) % 2, i % 2
                st_lo.wait(pe, b, 2 * t + 2)
                bank, full = t_claim(pe, n, f"qkT{i}")
                for j in range(4):
                    u = 4 * half + j
                    ins = nc.tensor.transpose(bank[:, j * P:(j + 1) * P],
                                              stack[:, t, q, 2 * u:2 * u + 2, :].rearrange("p h r -> p (h r)").bitcast(F32), ident[:, :])
                ins.then_inc(full, 1)

            def head_rows(u, hh):
                if L == 0:
                    r = slice(64 * hh, 64 * hh + QK_ROWS)
                    return [(qkT[r, 0, u, :], qkT[r, 1, u, :])]
                r = slice(64 * hh, 64 * hh + 64)
                q = [x[r, u % QS, 0:256] for x in (qkhi, qklo)]
                k = [x[r, u % QS, 256:512] for x in (qkhi, qklo)]
                return [(q[0], k[0]), (q[1], k[0]), (q[0], k[1])]

            def scores(n, u):
                if L == 0:
                    qkT_ok.wait(pe, n, 4 if u < 4 else 8)
                else:
                    qk_lo.wait(pe, n, u + 1)
                max_ok.wait(pe, n, u)
                for hh in range(2):
                    prods = head_rows(u, hh)
                    for t in range(TT):
                        for j, (q, k) in enumerate(prods):
                            ins = mm(S[hh][:, t * 256:(t + 1) * 256], q[:, t * P:(t + 1) * P], k, start=(j == 0), stop=(j == len(prods) - 1))
                    ins.then_inc(s_full.sem, 1)

            def maxT(n, b, u):
                m_ok.wait(pe, b, u + 1)
                bank, full = t_claim(pe, n, f"m{u}")
                for t in range(TT):
                    ins = nc.tensor.transpose(bank[0:4, t * P:(t + 1) * P], mcols[:, t, :, :].rearrange("p h s -> p (h s)"), ident[:, :])
                ins.then_inc(full, 1)

            def scores_T(n, u):
                mT_ok.wait(pe, n, u + 1)
                for hh in range(2):
                    p_ok.wait(pe, n, 2 * u + hh - 1)
                    prods = head_rows(u, hh)
                    for kt in range(TT):
                        out = PB[hh][:, kt * 256:(kt + 1) * 256]
                        mm(out, sel[0:4, hh, :], mT[0:4, u % 2, :], start=True, stop=False)
                        for j, (q, k) in enumerate(prods):
                            ins = mm(out, k[:, kt * P:(kt + 1) * P], q, start=False, stop=(j == len(prods) - 1))
                    ins.then_inc(p_full.sem, 1)

            def weigh(n, u, hh):
                if hh == 0:
                    v_ok.wait(pe, n, 2 if L == 0 or u < 4 else 4)
                    o_ok.wait(pe, n, u - 1)
                p_ok.wait(pe, n, 2 * u + hh + 1)
                for t in range(TT):
                    c = (2 * t + hh) * DHA
                    for kt in range(TT):
                        ins = mm(V[u % 2][:, c:c + DHA], pt[:, (2 * u + hh) % 4, kt * 256 + t * P:kt * 256 + (t + 1) * P],
                                 vaug[:, kt, 2 * u + hh, :], start=(kt == 0), stop=(kt == 1))
                ins.then_inc(av_full.sem, 1)

            def body(n, U, F, B):
                f, b = n + 1, n - 1
                for u in range(UNITS):
                    if L == 0 and F and u == 6:
                        for i in range(4):
                            qkT0(n, f, i)
                    if w2_ := units_at(n, u + 2, U, F, False):
                        scores(*w2_)
                    if w1_ := units_at(n, u + 1, U, F, False):
                        maxT(n, *w1_)
                    if U:
                        scores_T(n, u)
                    if w_1 := units_at(n, u - 1, U, False, B):
                        weigh(*w_1, 0)
                        weigh(*w_1, 1)
                    if L == 0:
                        if U and u == 0:
                            values(n, n, 0)
                            values(n, n, 1)
                            for i in range(4, 8):
                                qkT0(n, n, i)
                        if F and u == 1:
                            xnT(n, "xnT", xn, xn_ok, f)
                        if B and u == 1:
                            oT(n, b)
                        if F and u == 2:
                            qk0(n, f, 0)
                            qk0(n, f, 1)
                        if B and u == 2:
                            project(n, b)
                        if B and u == 4:
                            xnT(n, "h2T", xn2, xn2_ok, b)
                        if B and u >= 5:
                            hidden(n, b, (2 * u - 10, 2 * u - 9))
                        if B and u == 7:
                            down(n, b, 0)
                            down(n, b, 1)
                    else:
                        if U and u in (1, 2):
                            values(n, n, 2 * u - 1)
                        if w3_ := units_at(n, u + 3, U, F, False):
                            qk1(n, *w3_)
                        if B and u == 1:
                            oT(n, b)
                        if B and u == 3:
                            project(n, b)
                        if F and u == 4:
                            xnT(n, "xnT", xn, xn_ok, f)
                        if B and u == 4:
                            xnT(n, "h2T", xn2, xn2_ok, b)
                        if B and u == 5:
                            hidden(n, b, range(4))
                        if F and u >= 6:
                            values(n, f, 2 * u - 12)
                        if B and u >= 6:
                            down(n, b, u - 6)

            bodies(pe, body)


def build(nc, ins, out):
    x = ins["x"].rearrange("b (t p) d -> b p t d", p=P)
    y = out.rearrange("b (t p) d -> b p t d", p=P)
    mid = nc.dram_tensor("tokens_between", [NB, NTOK, D], F32, kind="Internal").ap().rearrange("b (t p) d -> b p t d", p=P)
    layers = []
    for L, names in enumerate([
        dict(wqkv="qkvT0", wo="projT0", w1="w1T0", w3="w3T0", w2="w2T0", wmod="adaT0"),
        dict(wqkv="W_qkv", wo="W_out", w1="W1", w2="W2", wmod="W_mod"),
    ]):
        w = {k: ins[v] for k, v in names.items()}
        w["cT"] = ins["cT"].rearrange("p (k b) -> p k b", k=FT)
        layers.append(w)
    layers[0] |= dict(bmod=ins["ada_b"], bo=ins["proj_b"], n1=ins["norm1"], n2=ins["norm2"], pos=ins["pos"],
                      qn=ins["q_norm"], kn=ins["k_norm"])
    layers[1] |= dict(bmod=ins["b_mod"], bo=ins["b_out"], b2=ins["b2"], b1=ins["b1"])
    for L in range(2):
        gates = nc.dram_tensor(f"gates{L}", [NB, 4 * D], F32, kind="Internal").ap()
        scratch = dict(gates=gates, g3=gates[:, D:4 * D])
        build_layer(nc, L, (x, mid)[L], (mid, y)[L], layers[L], scratch)


def kernel(**inputs):
    import numpy as _np
    import concourse.bacc as _bacc
    from concourse import mybir as _mybir
    from concourse.bass_utils import run_bass_kernel_spmd as _run

    def arr(name):
        return _np.asarray(inputs[name])

    def tiles(a):
        return a.reshape(-1, P, a.shape[1]).transpose(1, 0, 2).reshape(P, -1)

    def pad(a, n, axis):
        w = [(0, 0)] * a.ndim
        w[axis] = (0, n - a.shape[axis])
        return _np.pad(a, w)

    L0, L1 = "L0_cond_", "L1_cond_"
    host = dict(
        x=arr("x"),
        cT=tiles(arr("cond_1024").T),
        pos=arr("fside_BxSx3_0").reshape(NB * TT, P, 3).transpose(1, 0, 2),
        qkvT0=tiles(arr(L0 + "qkv_w").T), projT0=tiles(arr(L0 + "proj_w").T),
        w1T0=tiles(pad(arr(L0 + "w1").T, FF0P, 1)), w3T0=tiles(pad(arr(L0 + "w3").T, FF0P, 1)),
        w2T0=tiles(pad(arr(L0 + "w2").T, FF0P, 0)), adaT0=tiles(arr(L0 + "ada_w").T),
        ada_b=arr(L0 + "ada_b"), proj_b=arr(L0 + "proj_b"),
        norm1=arr(L0 + "norm1_w").reshape(FT, P).T, norm2=arr(L0 + "norm2_w").reshape(FT, P).T,
        q_norm=arr(L0 + "q_norm_w"), k_norm=arr(L0 + "k_norm_w"),
        W_mod=tiles(arr(L1 + "W_mod")), b_mod=arr(L1 + "b_mod"), W_qkv=tiles(arr(L1 + "W_qkv")), W_out=tiles(arr(L1 + "W_out")),
        b_out=arr(L1 + "b_out"), W1=tiles(arr(L1 + "W1")), b1=arr(L1 + "b1").reshape(8, P).T, W2=tiles(arr(L1 + "W2")), b2=arr(L1 + "b2"),
    )
    nc = _bacc.Bacc("TRN2", target_bir_lowering=False, num_devices=1)
    arrays, ins = {}, {}
    for name, a in host.items():
        a = _np.ascontiguousarray(a)
        arrays[f"in_{name}"] = a
        ins[name] = nc.dram_tensor(f"in_{name}", a.shape, _mybir.dt.from_np(a.dtype), kind="ExternalInput").ap()
    out = nc.dram_tensor("out", (NB, NTOK, D), F32, kind="ExternalOutput").ap()
    build(nc, ins, out)
    r = _run(nc, [arrays], core_ids=[0])
    return r.results[0]["out"]
```

```python
from contextlib import ExitStack
import math

import numpy as np
import concourse.bass as bass
from concourse import mybir

F32 = mybir.dt.float32
F32R = mybir.dt.float32r
ALU = mybir.AluOpType
ACT = mybir.ActivationFunctionType
AX = mybir.AxisListType

P = 128
NB = 8
NTOK = 256
TT = NTOK // P
D = 256
FT = D // P
HEADS = 16
UNITS = HEADS // 2
FF0P = 768
QK_ROWS = 64

LAYERS = [
    dict(dh=16, eps=1e-6, hid=FF0P // P, inner=256, qkv=768, scale=16 ** -0.5),
    dict(dh=64, eps=1e-5, hid=1024 // P, inner=1024, qkv=3072, scale=64 ** -0.5),
]


class Signal:

    def __init__(self, sem, per):
        self.sem, self.per = sem, per

    def at(self, b, k):
        v = b * self.per + k
        return max(v, 0) if isinstance(v, int) else v


def bcast(ap, axis, n):
    a = ap.unsqueeze(axis)
    shape = list(a.shape)
    shape[axis] = n
    return a.to_broadcast(shape)


def at(n, off):
    m = n + off
    return [] if isinstance(m, int) and not 0 <= m < NB else [m]


def unit_at(n, v):
    return [(m, v % UNITS) for m in at(n, v // UNITS)]


FIRST, LOOP, LAST = -2, [(3, NB - 2), (3, NB - 1)], NB + 1

DENSE = [
    ["qk0 +1", "qk1 +1",
     "v +1", "pj -1",
     "w2 -2",
     "qkT0 +1", "qkT1 +1", "h2T -1",
     "qkT2 +1", "qkT3 +1", "hid0 -1", "hid1 -1",
     "qkT4 +1", "qkT5 +1", "hid2 -1", "hid3 -1",
     "qkT6 +1", "qkT7 +1", "xnT +2", "hid4 -1", "hid5 -1"],
    ["qk3 +0", "v1 +0", "v3 +0",
     "qk4 +0", "w2 -2",
     "qk5 +0", "pj -1",
     "qk6 +0", "xnT +1",
     "qk7 +0", "h2T -1",
     "qk0 +1", "v0 +1",
     "qk1 +1", "hid0 -1", "hid1 -1",
     "qk2 +1", "v2 +1", "hid2 -1", "hid3 -1"],
]


def dense_uses(L, n):
    pairs = [(x.split()[0], int(x.split()[1])) for x in DENSE[L]]
    return [(name, off) for name, off in pairs if at(n, off)]


def build_layer(nc, L, x_src, y_dst, w, scratch):
    cfg = LAYERS[L]
    DH, HID, INNER, QKV = cfg["dh"], cfg["hid"], cfg["inner"], cfg["qkv"]
    KO = INNER // P
    QS = 2
    NMOD = 6 * D

    ctx = ExitStack()
    with ctx:
        def sb(name, shape, dt=F32):
            return ctx.enter_context(nc.sbuf_tensor(f"{name}_{L}", shape, dt))

        def ps(name):
            return ctx.enter_context(nc.psum_tensor(f"{name}_{L}", [P, 512], F32))

        def sem(name):
            return ctx.enter_context(nc.semaphore(f"{name}_{L}"))

        shapes = dict(wqkv=[P, FT, QKV], wo=[P, KO, D], w1=[P, FT, HID * P], w2=[P, HID, D])
        if L == 0:
            shapes["w3"] = [P, FT, HID * P]
        hi = {k: sb(f"{k}_hi", s, F32R) for k, s in shapes.items()}
        lo = {k: sb(f"{k}_lo", s, F32R) for k, s in shapes.items()}
        CH = 2048
        chunks = []
        for k in ["wqkv", "wo", "w1", "w3", "w2"]:
            if k in shapes:
                n = shapes[k][1] * shapes[k][2]
                chunks += [(k, c, min(CH, n - c)) for c in range(0, n, CH)]

        ident = sb("ident", [P, P])
        arena = sb("arena", [P, 11, 512])

        def buf(i, n=1):
            return arena[:, i:i + n, :].rearrange("p a b -> p (a b)")

        x_back, xr, x2, yo, xn2, h2full = (buf(i).rearrange("p (t d) -> p t d", t=TT) for i in range(6))
        gates1 = buf(6).rearrange("p (g d) -> p g d", g=2)
        gates2 = buf(7).rearrange("p (g d) -> p g d", g=2)
        xn, hfull = (buf(i).rearrange("p (t d) -> p t d", t=TT) for i in (8, 9))
        x_in = buf(10).rearrange("p (t d) -> p t d", t=TT)
        pq = sb("pq", [P, 4, 512])
        raw = [buf(0, 4), buf(4, 4)]
        hhi = sb("hhi", [P, FT, NTOK], F32R)
        hlo = sb("hlo", [P, FT, NTOK], F32R)
        h2hi = sb("h2hi", [P, FT, NTOK], F32R)
        h2lo = sb("h2lo", [P, FT, NTOK], F32R)
        ab1 = sb("ab1", [P, 4])
        ab2 = sb("ab2", [P, 4])
        held = sb("held", [P, 1])
        stat = sb("stat", [P, TT, 6])
        aggr = sb("aggr", [P, TT, 2])
        msq = sb("msq", [P, TT])
        rstd = sb("rstd", [P, TT])
        stat2 = sb("stat2", [P, TT, 6])
        aggr2 = sb("aggr2", [P, TT, 2])
        msq2 = sb("msq2", [P, TT])
        rstd2 = sb("rstd2", [P, TT])
        mhalf = sb("mhalf", [P, 32])
        negm = sb("negm", [P, 2, TT])
        negb = sb("negb", [P, 2, 2, TT])
        rsum = sb("rsum", [P, 2, 2, TT])
        rinv = sb("rinv", [P, 2, 2, TT])
        pt = [sb("pt_hi", [P, 2, 512], F32R), sb("pt_lo", [P, 2, 512], F32R)] if L else [sb("pt", [P, 2, 512])]
        if L == 0:
            vs = sb("vs", [P, TT, 256])
            vz = sb("vz", [P, TT, HEADS, 32])
        else:
            vhi, vlo = sb("vhi", [P, TT, HEADS, DH], F32R), sb("vlo", [P, TT, HEADS, DH], F32R)
        othi = sb("othi", [P, KO, NTOK], F32R)
        otlo = sb("otlo", [P, KO, NTOK], F32R)
        ahi = sb("ahi", [P, HID, NTOK], F32R)
        alo = sb("alo", [P, HID, NTOK], F32R)
        if L == 0:
            cs = sb("cs", [P, TT, 2, 2, 16])
            qraw = sb("qraw", [P, TT, 512])
            ff = sb("ff", [P, TT, D])
            sq = sb("sq", [P, TT, 512])
            hss = sb("hss", [P, TT, 32])
            hr = sb("hr", [P, TT, 32])
            qn = sb("qn", [P, TT, 512])
            m1 = sb("m1", [P, TT, 512])
            m2 = sb("m2", [P, 32, 12])
            stack = sb("stack", [P, TT, 2, HEADS, 64], F32R)
            qkT = sb("qkT", [P, 2, UNITS, NTOK], F32R)
            th = sb("th", [P, 2, NTOK])
            t1 = sb("t1", [P, 2, NTOK])
            afull = sb("afull", [P, 2, NTOK])
        else:
            qkhi = sb("qkhi", [P, QS, 512], F32R)
            qklo = sb("qklo", [P, QS, 512], F32R)
            afull = sb("afull", [P, 2, 512])
            b1c = sb("b1c", [P, HID])

        S = [ps("S0"), ps("S1")]
        PB = [ps("P0"), ps("P1")]
        T = [ps(f"T{i}") for i in range(3 - L)]
        if L == 0:
            ov = ps("V0")
            V = [ov[:, 0:256], ov[:, 256:512]]
        else:
            V = [ps("V0"), ps("V1")]

        raw_in, raw_hi, raw_lo = [sem("raw_in0"), sem("raw_in1")], sem("raw_hi"), sem("raw_lo")
        const_in, mod_in, s_init, s_ident = sem("const_in"), [sem("mod_in0"), sem("mod_in1")], sem("init"), sem("ident_m")
        mod_mm, mod_row, mod_T, mod_ab, mod_silu, gates_out, mod_chain = (
            sem("mod_mm"), sem("mod_row"), sem("mod_T"), sem("mod_ab"), sem("mod_silu"), sem("gates_out"), sem("mod_chain"))
        trig_in, trig_red, trig_sin, trig_done = sem("trig_in"), sem("trig_red"), sem("trig_sin"), sem("trig_done")
        t_full = [sem(f"t_full{i}") for i in range(len(T))]

        def sig(name, per):
            return Signal(sem(name), per)

        x_loaded, xb_loaded = sig("x_loaded", 16), sig("xb_loaded", 16)
        par1, par2, par3 = sig("par1", 32 if L == 0 else 16), sig("par2", 32), sig("par3", 16)
        ms1, rstd1, xn_ok = sig("ms1", 1), sig("rstd1", 1), sig("xn_ok", TT)
        ms2, rs2, xn2_ok = sig("ms2", 1), sig("rs2", 1), sig("xn2_ok", TT)
        h_full, h_hi, h_lo = sig("h_full", FT), sig("h_hi", FT), sig("h_lo", FT)
        h2_full, h2_hi, h2_lo = sig("h2_full", FT), sig("h2_hi", FT), sig("h2_lo", FT)
        xr_ok, x2_ok, y_ok, y_stored = sig("xr_ok", 1), sig("x2_ok", TT), sig("y_ok", TT), sig("y_stored", 16)
        w2_gated = sig("w2_gated", TT)
        v_hi, v_lo = (sig("v_ok", 2), None) if L == 0 else (sig("v_hi", 4), sig("v_lo", 4))
        v_ok = v_lo or v_hi
        vs_ok = sig("vs_ok", 2)
        s_full, max_ok, bias_ok, ex_ok = sig("s_full", 16), sig("max_ok", 8), sig("bias_ok", 8), sig("ex_ok", 16)
        stat1, stat2s = sig("stat1", 3 - L), sig("stat2", 3 - L)
        rd_ok, pn_ok, p_full, av_full = sig("rd_ok", 8), sig("pn_ok", 16), sig("p_full", 16), sig("av_full", 8)
        p_hi, p_lo = (sig("p_ok", 16), None) if L == 0 else (sig("p_hi", 16), sig("p_lo", 16))
        p_ok = p_lo or p_hi
        sw_ok = sig("sw_ok", HID)
        ot_hi, ot_lo = sig("ot_hi", KO), sig("ot_lo", KO)
        pj_gated = sig("pj_gated", TT)
        a_full, a_hi, a_lo = sig("a_full", HID), sig("a_hi", HID), sig("a_lo", HID)
        x2b_ok = sig("x2b_ok", 1)
        y0_ok = sig("y0_ok", 1)
        if L == 0:
            sq_ok, hsum_ok, m2_ok = sig("sq_ok", TT), sig("hsum_ok", TT), sig("m2_ok", TT)
            qraw_ok, hss_ok, hr_ok, qn_ok, m1_ok, qf_ok = (
                sig("qraw_ok", TT), sig("hss_ok", TT), sig("hr_ok", TT), sig("qn_ok", TT), sig("m1_ok", TT), sig("qf_ok", TT))
            st_hi, st_lo, qkT_ok, tanh_ok = (
                sig("st_hi", 2 * TT), sig("st_lo", 2 * TT), sig("qkT_ok", 8), sig("tanh_ok", HID))
        else:
            qk_hi, qk_lo = sig("qk_hi", 8), sig("qk_lo", 8)

        last_read = dict(xnT=(h_full, FT), h2T=(h2_full, FT), pj=(pj_gated, TT), w2=(w2_gated, TT))
        v_order = [0, 1] if L == 0 else [0, 2, 1, 3]
        last_read |= {f"v{i}": (v_lo, j + 1) for j, i in enumerate(v_order)} if L else dict(v=(vs_ok, TT))
        if L == 0:
            last_read |= {f"qk{i}": (qraw_ok, i + 1) for i in range(TT)}
            last_read |= {f"qkT{i}": (qkT_ok, i + 1) for i in range(8)}
            last_read |= {f"hid{i}": (a_full, i + 1) for i in range(HID)}
            hh_read = vs_ok
        else:
            last_read |= {f"qk{i}": (qk_lo, i + 1) for i in range(UNITS)}
            last_read |= {f"hid{i}": (a_full, 2 * i + 2) for i in range(HID // 2)}
            hh_read = qk_hi

        loop_from, loop_to = LOOP[L]
        uses = {n: dense_uses(L, n) for n in range(FIRST, LAST + 1)}
        per_body = len(uses[loop_from])
        assert per_body == len(DENSE[L]) and per_body % len(T) == 0

        def uses_of(n):
            return uses[n if isinstance(n, int) else loop_from]

        def uses_before(n):
            if isinstance(n, int):
                return sum(len(uses[i]) for i in range(FIRST, n)), 0
            return sum(len(uses[i]) for i in range(FIRST, loop_from)), n - loop_from

        def bank_of(n, name):
            pos = [x for x, _ in uses_of(n)].index(name)
            return pos, (uses_before(n)[0] + pos) % len(T)

        def t_claim(eng, n, name):
            pos, bank = bank_of(n, name)
            before = [(n, x) for x in uses_of(n)[:pos]]
            m = n - 1
            while len(before) < len(T) and not (isinstance(m, int) and m < FIRST):
                before = [(m, x) for x in uses_of(m)] + before
                m = m - 1
            if len(before) >= len(T):
                body_, (former, off) = before[-len(T)]
                s_, k = last_read[former]
                eng.wait_ge(s_.sem, s_.at(body_ + off, k))
            return T[bank], t_full[bank]

        def t_read(eng, n, name):
            pos, bank = bank_of(n, name)
            const, more = uses_before(n)
            eng.wait_ge(t_full[bank], (const + pos) // len(T) + 1 + more * (per_body // len(T)))
            return T[bank]

        cT = sb("cT", [P, FT, NB])
        cact = sb("cact", [P, FT, NB])
        modr = pq[0:NB, :, :].rearrange("p a b -> p (a b)")[:, 0:NMOD]
        bmod = buf(8, 3)[0:NB, :]
        grow = (qn if L == 0 else afull)[0:NB, :, :].rearrange("p a (b c) -> p (a b) c", b=2)
        bo8 = sb("bo8", [NB, 2, D])
        wn = sb("wn", [P, 4])
        ab_all = sb("ab_all", [P, NB, 8])
        if L == 0:
            pos = sb("pos", [P, NB * TT, 3])
            ang = sb("ang", [P, 2, NB * TT, 6])
            kk = sb("kk", [P, 2, NB * TT, 6])
            trig = sb("trig", [P, 2, NB * TT, 6])
            wqk = sb("wqk", [P, 2, 16])
            cs_all = sb("cs_all", [P, NB * TT, 2, 2, 16])

        block = ctx.enter_context(nc.Block())

        early = sum(k == "wqkv" for k, _, _ in chunks)
        late = {-1: range(early, early + 2), 0: range(early + 2, len(chunks))}

        def bodies(eng, body, split=None):
            for n in range(FIRST, loop_from):
                body(n)
                for c in late.get(n, ()) if split else ():
                    split(c)
            with eng.Fori(loop_from, loop_to) as n:
                body(n)
            for n in range(loop_to, LAST + 1):
                body(n)

        @block.sync
        def _(sp):
            sp.dma_start(cT[:, :, :], w["cT"]).then_inc(const_in, 16)
            sp.dma_start(bmod[:, :], w["bmod"].partition_broadcast(NB)).then_inc(const_in, 16)
            sp.dma_start(bo8[:, 0, :], w["bo"].partition_broadcast(NB)).then_inc(const_in, 16)
            if L == 0:
                sp.dma_start(wn[:, 0:2], w["n1"]).then_inc(const_in, 16)
                sp.dma_start(wn[:, 2:4], w["n2"]).then_inc(const_in, 16)
                sp.dma_start(pos[:, :, :], w["pos"]).then_inc(trig_in, 16)
                sp.dma_start(wqk[:, 0, :], w["qn"].partition_broadcast(P)).then_inc(trig_in, 16)
                sp.dma_start(wqk[:, 1, :], w["kn"].partition_broadcast(P)).then_inc(trig_in, 16)
            else:
                sp.dma_start(bo8[:, 1, :], w["b2"].partition_broadcast(NB)).then_inc(const_in, 16)
                sp.dma_start(b1c[:, :], w["b1"]).then_inc(const_in, 16)
            for h in range(2):
                sp.dma_start(raw[h][:, 0:NMOD].rearrange("p (k n) -> p k n", k=FT), w["wmod"].rearrange("p (k n) -> p k n", k=FT)[:, :, h * 768:(h + 1) * 768]).then_inc(mod_in[h], 16)
            def load_chunk(i):
                k, c, m = chunks[i]
                if i >= 2:
                    sp.wait_ge(raw_lo, i - 1)
                else:
                    sp.wait_ge(mod_mm, i + 1)
                sp.dma_start(raw[i % 2][:, 0:m], w[k][:, c:c + m]).then_inc(raw_in[i % 2], 16)

            for i in range(early):
                load_chunk(i)
            sp.wait_ge(mod_row, 1)
            sp.dma_start(scratch["gates"], grow[:, :, :].rearrange("b g d -> b (g d)")).then_inc(gates_out, 16)
            sp.wait_ge(gates_out, 16)
            sp.wait_ge(mod_ab, 1)
            if L == 0:
                sp.wait_ge(trig_done, 1)

            def load_tokens(b):
                sp.wait_ge(xn_ok.sem, xn_ok.at(b, 0))
                sp.dma_start(x_in[:, :, :], x_src[b]).then_inc(x_loaded.sem, 16)

            def load_scales(b):
                sp.wait_ge(h_full.sem, h_full.at(b, 0))
                if L == 0:
                    sp.wait_ge(qf_ok.sem, qf_ok.at(b, 0))
                sp.dma_start(ab1[:, :], ab_all[:, b, 0:4]).then_inc(par1.sem, 16)
                if L == 0:
                    sp.dma_start(cs[:, :, :, :, :].rearrange("p t c q d -> p t (c q d)"), cs_all[:, :, :, :, :].rearrange("p (n t) c q d -> p n t (c q d)", t=TT)[:, b]).then_inc(par1.sem, 16)

            def load_back(b):
                if isinstance(b, int) and b == 0:
                    sp.wait_ge(raw_lo, len(chunks))
                sp.wait_ge(xr_ok.sem, xr_ok.at(b, 0))
                sp.dma_start(x_back[:, :, :], x_src[b]).then_inc(xb_loaded.sem, 16)
                sp.wait_ge(h2_full.sem, h2_full.at(b, 0))
                sp.wait_ge(x2_ok.sem, x2_ok.at(b, 0))
                sp.dma_start(ab2[:, :], ab_all[:, b, 4:8]).then_inc(par2.sem, 16)
                sp.dma_start(gates1[:, :, :], scratch["gates"][b, 0:2 * D].partition_broadcast(P)).then_inc(par2.sem, 16)

            def load_gates2(b):
                sp.wait_ge(y_ok.sem, y_ok.at(b, 0))
                sp.dma_start(gates2[:, :, :], scratch["gates"][b, 2 * D:4 * D].partition_broadcast(P)).then_inc(par3.sem, 16)

            def store(b):
                sp.wait_ge(y_ok.sem, y_ok.at(b, TT))
                sp.dma_start(y_dst[b], yo[:, :, :]).then_inc(y_stored.sem, 16)

            def body(n):
                for f in at(n, 2 if L == 0 else 1):
                    load_tokens(f)
                for b in at(n, -1):
                    load_back(b)
                for d in at(n, -2):
                    store(d)
                for b in at(n, -1):
                    load_gates2(b)
                for f in at(n, 2 if L == 0 else 1):
                    load_scales(f)

            bodies(sp, body, load_chunk)
            sp.wait_ge(y_stored.sem, y_stored.at(NB, 0))

        @block.gpsimd
        def _(pool):
            g = nc.gpsimd
            g.memset(ident[:, :], 0.0).then_inc(s_ident, 1)
            pool.wait_ge(s_ident, 1)
            g.affine_select(out=ident[:, :], in_=ident[:, :], compare_op=ALU.not_equal, fill=1.0,
                            base=0, pattern=[[-1, P]], channel_multiplier=1).then_inc(s_ident, 1)
            g.memset(mhalf[:, :], -0.5).then_inc(s_init, 1)
            if L == 0:
                g.memset(vz[:, :, :, :], 0.0).then_inc(s_init, 1)
                g.memset(stack[:, :, :, :, 48:64].bitcast(F32), 0.0).then_inc(s_init, 1)
            pool.wait_ge(s_init, 3 - 2 * L)

            def power(out, in_, ok, ms, b, k):
                pool.wait_ge(ms.sem, ms.at(b, k))
                g.tensor_tensor(out, in_, mhalf[:, 0:in_.shape[-1]], ALU.pow).then_inc(ok.sem, 1)

            def low(out, full, hi_, ok, hi_ok, b, k, read, rk):
                pool.wait_ge(read.sem, read.at(b, rk))
                pool.wait_ge(hi_ok.sem, hi_ok.at(b, k))
                g.tensor_tensor(out, full, hi_.bitcast(F32), ALU.subtract).then_inc(ok.sem, 1)

            def residual(n):
                pool.wait_ge(xb_loaded.sem, xb_loaded.at(n, 16))
                pool.wait_ge(par2.sem, par2.at(n, par2.per))
                pool.wait_ge(x2_ok.sem, x2_ok.at(n, 0))
                g.tensor_tensor(xr[:, :, :], x_back[:, :, :], bcast(gates1[:, 0, :], 1, TT), ALU.add).then_inc(xr_ok.sem, 1)

            def h_low(n):
                for ft in range(FT):
                    low(hlo[:, ft, :], hfull[:, ft, :], hhi[:, ft, :], h_lo, h_hi, n, ft + 1, hh_read, 0)

            def h2_low(b):
                for ft in range(FT):
                    low(h2lo[:, ft, :], h2full[:, ft, :], h2hi[:, ft, :], h2_lo, h2_hi, b, ft + 1, a_full, 0)

            def head_norm(n, t):
                power(hr[:, t, :], hss[:, t, :], hr_ok, hss_ok, n, t + 1)

            def cos_part(n, t):
                pool.wait_ge(st_lo.sem, st_lo.at(n - 1, 2 * t + 2))
                pool.wait_ge(qn_ok.sem, qn_ok.at(n, t + 1))
                o4 = m1[:, t, :].rearrange("p (q h d) -> p q h d", q=2, h=HEADS)
                i4 = qn[:, t, :].rearrange("p (q h d) -> p q h d", q=2, h=HEADS)
                g.tensor_tensor(o4, i4, bcast(cs[:, t, 0, :, :], 2, HEADS), ALU.mult).then_inc(m1_ok.sem, 1)

            def a_low(b, i):
                if L == 0:
                    low(alo[:, i, :], afull[:, i % 2, :], ahi[:, i, :], a_lo, a_hi, b, i + 1, w2_gated, 0)
                else:
                    j = i // 2
                    if i % 2 == 0:
                        low(alo[:, i, :], afull[:, j % 2, 0:256], ahi[:, i, :], a_lo, a_hi, b, i + 1, w2_gated, 0)
                    else:
                        low(alo[:, i, :], afull[:, j % 2, 256:512], ahi[:, i, :], a_lo, a_hi, b, i + 1, w2_gated, 0)

            def norm1_n(n):
                power(rstd[:, :], msq[:, :], rstd1, ms1, n, 1)

            def norm2_b(b):
                power(rstd2[:, :], msq2[:, :], rs2, ms2, b, 1)

            def body(n):
                if L == 0:
                    for f in at(n, 1):
                        h_low(f)
                    for d in at(n, -2):
                        a_low(d, 4)
                        a_low(d, 5)
                    for b in at(n, -1):
                        residual(b)
                    for f in at(n, 1):
                        head_norm(f, 0)
                        head_norm(f, 1)
                        cos_part(f, 0)
                    for b in at(n, -1):
                        norm2_b(b)
                    for f in at(n, 1):
                        cos_part(f, 1)
                    for b in at(n, -1):
                        h2_low(b)
                        a_low(b, 0)
                        a_low(b, 1)
                    for e in at(n, 2):
                        norm1_n(e)
                    for b in at(n, -1):
                        a_low(b, 2)
                        a_low(b, 3)
                else:
                    for d in at(n, -2):
                        for i in range(4, 8):
                            a_low(d, i)
                    for b in at(n, -1):
                        residual(b)
                    for f in at(n, 1):
                        norm1_n(f)
                    for b in at(n, -1):
                        norm2_b(b)
                    for f in at(n, 1):
                        h_low(f)
                    for b in at(n, -1):
                        h2_low(b)
                        for i in range(4):
                            a_low(b, i)

            bodies(pool, body)

        @block.scalar
        def _(act):
            a = nc.scalar
            if L == 0:
                act.wait_ge(trig_red, 1)
                a.activation(trig[:, :, :, :], ang[:, :, :, :], ACT.Sin).then_inc(trig_sin, 1)
            else:
                act.wait_ge(const_in, 16 * 5)
                a.activation(cact[:, :, :], cT[:, :, :], ACT.Tanh, scale=0.5).then_inc(mod_silu, 1)
            def chunk_high(i):
                k, c, m = chunks[i]
                act.wait_ge(raw_in[i % 2], 16 * (i // 2 + 1))
                dst = hi[k][:, :, :].rearrange("p a b -> p (a b)")[:, c:c + m]
                a.copy(dst, raw[i % 2][:, 0:m]).then_inc(raw_hi, 1)

            for i in range(early):
                chunk_high(i)

            def high(out, full, ok, full_ok, b, k, read, rk):
                act.wait_ge(read.sem, read.at(b, rk))
                act.wait_ge(full_ok.sem, full_ok.at(b, k))
                a.copy(out, full).then_inc(ok.sem, 1)

            def h_high(n):
                for ft in range(FT):
                    high(hhi[:, ft, :], hfull[:, ft, :], h_hi, h_full, n, ft + 1, hh_read, 0)

            def h2_high(b):
                for ft in range(FT):
                    high(h2hi[:, ft, :], h2full[:, ft, :], h2_hi, h2_full, b, ft + 1, a_full, 0)

            def ot_high(n, i):
                act.wait_ge(av_full.sem, av_full.at(n, 4 * i + 4 if L == 0 else i + 1))
                act.wait_ge(pj_gated.sem, pj_gated.at(n, 0))
                if L == 0:
                    a.copy(othi[:, i, :], V[i % 2][:, 0:NTOK]).then_inc(ot_hi.sem, 1)
                else:
                    for hh in range(2):
                        r = slice(64 * hh, 64 * hh + 64)
                        ins = a.copy(othi[r, i, :], V[i % 2][r, 256 * hh:256 * hh + 256])
                    ins.then_inc(ot_hi.sem, 1)

            def qkv_raw(n, b, t):
                bank = t_read(act, n, f"qk{t}")
                act.wait_ge(qn_ok.sem, qn_ok.at(b - 1, t + 1))
                a.activation(sq[:, t, :], bank[:, :], ACT.Square).then_inc(sq_ok.sem, 1)
                a.copy(qraw[:, t, :], bank[:, :]).then_inc(qraw_ok.sem, 1)

            def v_evac(n, b, i):
                bank = t_read(act, n, "v" if L == 0 else f"v{i}")
                if L == 0:
                    act.wait_ge(v_hi.sem, v_hi.at(b, 0))
                    a.copy(vs[:, i, :], bank[:, i * 256:(i + 1) * 256]).then_inc(vs_ok.sem, 1)
                else:
                    act.wait_ge(av_full.sem, av_full.at(b - 1, 4 + 4 * (i % 2)))
                    a.copy(vhi[:, i // 2, (i % 2) * 8:(i % 2) * 8 + 8, :].rearrange("p h d -> p (h d)"), bank[:, :]).then_inc(v_hi.sem, 1)

            def v_place(b):
                act.wait_ge(av_full.sem, av_full.at(b, 0))
                act.wait_ge(vs_ok.sem, vs_ok.at(b, TT))
                for t in range(TT):
                    for hh in range(2):
                        ins = a.copy(vz[:, t, :, :].rearrange("p (u h) c -> p u h c", h=2)[:, :, hh, 16 * hh:16 * hh + 16],
                                     vs[:, t, :].rearrange("p (u h d) -> p u h d", h=2, d=DH)[:, :, hh, :])
                    ins.then_inc(v_hi.sem, 1)

            def keep_x2(b):
                act.wait_ge(x2_ok.sem, x2_ok.at(b, TT))
                act.wait_ge(y_stored.sem, y_stored.at(b, 0))
                a.copy(yo[:, :, :], x2[:, :, :]).then_inc(y0_ok.sem, 1)

            def stack_high(n, t):
                act.wait_ge(qkT_ok.sem, qkT_ok.at(n, 0))
                act.wait_ge(qf_ok.sem, qf_ok.at(n, t + 1))
                f = m1[:, t, :].rearrange("p (q h d) -> p q h d", q=2, h=HEADS)
                a.copy(stack[:, t, 0, :, 0:32].rearrange("p h (r d) -> p h r d", r=2),
                       bcast(f[:, 0], 2, 2)).then_inc(st_hi.sem, 1)
                a.copy(stack[:, t, 1, :, 0:64].rearrange("p h (r d) -> p h r d", r=2)[:, :, :, 0:16],
                       bcast(f[:, 1], 2, 2)).then_inc(st_hi.sem, 1)

            def qkT_evac(n, b, i):
                half, t, q = i // 4, (i // 2) % 2, i % 2
                bank = t_read(act, n, f"qkT{i}")
                act.wait_ge(s_full.sem, s_full.at(b - 1, 8 + 8 * half))
                a.copy(qkT[:, q, 4 * half:4 * half + 4, t * P:(t + 1) * P],
                       bank[:, :].rearrange("p (u c) -> p u c", u=4)).then_inc(qkT_ok.sem, 1)

            def qk_high(n, b, u):
                bank = t_read(act, n, f"qk{u}")
                act.wait_ge(s_full.sem, s_full.at(b, 2 * (u - QS + 1)))
                a.copy(qkhi[:, u % QS, :], bank[:, :]).then_inc(qk_hi.sem, 1)

            def exps(b, u):
                act.wait_ge(bias_ok.sem, bias_ok.at(b, u + 1))
                for hh in range(2):
                    k = 2 * u + hh
                    act.wait_ge(p_full.sem, p_full.at(b, k - 3))
                    for t in range(TT):
                        ins = a.activation(pq[:, k % 4, t * 256:(t + 1) * 256], S[hh][:, t * 256:(t + 1) * 256], ACT.Exp,
                                           bias=negb[:, u % 2, hh, t:t + 1], scale=cfg["scale"],
                                           accum_out=rsum[:, u % 2, hh, t:t + 1])
                    ins.then_inc(ex_ok.sem, 1)

            def pt_high(b, u):
                act.wait_ge(av_full.sem, av_full.at(b, u))
                for hh in range(2):
                    act.wait_ge(p_full.sem, p_full.at(b, 2 * u + hh + 1))
                    a.copy(pt[0][:, hh, :], PB[hh][:, :]).then_inc(p_hi.sem, 1)

            def hid_act(n, b, i):
                if L == 0:
                    bank = t_read(act, n, f"hid{i}")
                    act.wait_ge(a_full.sem, a_full.at(b, i - 1))
                    a.activation(th[:, i % 2, :], bank[:, 0:256], ACT.Tanh, scale=0.5).then_inc(tanh_ok.sem, 1)
                else:
                    bank = t_read(act, n, f"hid{i}")
                    act.wait_ge(a_lo.sem, a_lo.at(b, 2 * i - 2))
                    for j in range(2):
                        ins = a.activation(afull[:, i % 2, 256 * j:256 * j + 256], bank[:, 256 * j:256 * j + 256],
                                           ACT.Gelu, bias=b1c[:, 2 * i + j:2 * i + j + 1])
                        ins.then_inc(a_full.sem, 1)

            def hid_high(b, i):
                act.wait_ge(a_full.sem, a_full.at(b, 2 * i + 2))
                act.wait_ge(w2_gated.sem, w2_gated.at(b, 0))
                for j in range(2):
                    ins = a.copy(ahi[:, 2 * i + j, :], afull[:, i % 2, 256 * j:256 * j + 256])
                    ins.then_inc(a_hi.sem, 1)

            def a_high(b, i):
                high(ahi[:, i, :], afull[:, i % 2, :], a_hi, a_full, b, i + 1, w2_gated, 0)

            def body(n):
                for u in range(UNITS):
                    if L == 0:
                        if u == 0:
                            for f in at(n, 1):
                                h_high(f)
                        if u == 1:
                            for f in at(n, 1):
                                qkv_raw(n, f, 0)
                                qkv_raw(n, f, 1)
                        if u == 2:
                            for f in at(n, 1):
                                v_evac(n, f, 0)
                                v_evac(n, f, 1)
                        if u == 5:
                            for b in at(n, -1):
                                h2_high(b)
                        if u == 0:
                            for d in at(n, -2):
                                hid_act(n - 1, d, 4)
                                hid_act(n - 1, d, 5)
                            for m in at(n, 0):
                                v_place(m)
                        if u >= 6:
                            for b in at(n, -1):
                                hid_act(n, b, 2 * u - 12)
                                hid_act(n, b, 2 * u - 11)
                    else:
                        if u != 2:
                            for m, v_ in unit_at(n, u - 2):
                                if u == 3:
                                    ot_high(m, 0)
                                ot_high(m, v_)
                        if u == 0:
                            for d in at(n, -2):
                                hid_act(n - 1, d, 2)
                                hid_act(n - 1, d, 3)
                        if u == 7:
                            for b in at(n, -1):
                                hid_act(n, b, 0)
                                hid_act(n, b, 1)
                    if L == 1:
                        for m, v_ in unit_at(n, u + 3):
                            qk_high(n, m, v_)
                        if u == 4:
                            for f in at(n, 1):
                                h_high(f)
                    for m, v_ in unit_at(n, u + 2):
                        exps(m, v_)
                    for m, v_ in unit_at(n, u):
                        pt_high(m, v_)
                    if L == 0:
                        if u == 0:
                            for b in at(n, -1):
                                ot_high(b, 1)
                            for d in at(n, -2):
                                keep_x2(d)
                        if u == 3:
                            for f in at(n, 1):
                                stack_high(f, 0)
                        if u == 4:
                            for m in at(n, 0):
                                ot_high(m, 0)
                        if u >= 4:
                            for f in at(n, 1):
                                qkT_evac(n, f, 2 * u - 8)
                                qkT_evac(n, f, 2 * u - 7)
                        if u == 4:
                            for f in at(n, 1):
                                stack_high(f, 1)
                        if u == 0:
                            for d in at(n, -2):
                                a_high(d, 4)
                                a_high(d, 5)
                        if u >= 6:
                            for b in at(n, -1):
                                a_high(b, 2 * u - 12)
                                a_high(b, 2 * u - 11)
                    else:
                        if u == 0:
                            for m in at(n, 0):
                                v_evac(n, m, 1)
                                v_evac(n, m, 3)
                            for d in at(n, -2):
                                hid_high(d, 2)
                                hid_high(d, 3)
                        if u == 5:
                            for f in at(n, 1):
                                v_evac(n, f, 0)
                            for b in at(n, -1):
                                h2_high(b)
                        if u == 7:
                            for f in at(n, 1):
                                v_evac(n, f, 2)
                            for b in at(n, -1):
                                hid_high(b, 0)
                                hid_high(b, 1)

            bodies(act, body, chunk_high)

        @block.vector
        def _(dve):
            v = nc.vector
            steps_done = 0

            def done(ins):
                nonlocal steps_done
                steps_done += 1
                ins.then_inc(mod_chain, 1)
                dve.wait_ge(mod_chain, steps_done)

            dve.wait_ge(s_ident, 2)
            if L == 0:
                dve.wait_ge(trig_in, 48)
                freq = [1.0, 0.01]
                a_v = ang[:, 1, :, :].rearrange("p n (a h) -> p n a h", h=2)
                for h in range(2):
                    done(v.tensor_scalar(a_v[:, :, :, h], pos[:, :, :], freq[h], None, ALU.mult))
                magic = 1.5 * 2 ** 23
                c1 = 6.28125
                c2 = round((2 * math.pi - c1) * 2 ** 21) / 2 ** 21
                c3 = 2 * math.pi - c1 - c2
                sa, ca, kt = ang[:, 1, :, :], ang[:, 0, :, :], kk[:, 0, :, :]
                done(v.tensor_scalar(kt, sa, 1 / (2 * math.pi), magic, ALU.mult, ALU.add))
                done(v.tensor_scalar(kt, kt, magic, None, ALU.subtract))
                for c in (c1, c2, c3):
                    done(v.scalar_tensor_tensor(out=sa, in0=kt, scalar=-c, in1=sa, op0=ALU.mult, op1=ALU.add))
                pi = 3.1415925
                done(v.tensor_scalar(sa, sa, pi, -pi, ALU.min, ALU.max))
                done(v.tensor_scalar(ca, sa, math.pi / 2, None, ALU.add))
                done(v.tensor_scalar(kt, ca, pi, -2 * math.pi, ALU.is_gt, ALU.mult))
                done(v.tensor_tensor(ca, ca, kt, ALU.add))
                v.tensor_scalar(ca, ca, pi, -pi, ALU.min, ALU.max).then_inc(trig_red, 1)
                dve.wait_ge(trig_sin, 1)
                done(v.tensor_scalar(kk[:, 1, :, :], trig[:, 1, :, :], -1.0, None, ALU.mult))
                N16 = NB * TT
                for q in range(2):
                    w2_ = wqk[:, q, 0:12].rearrange("p (j e) -> p j e", e=2)
                    c_o = cs_all[:, :, 0, q, 0:12].rearrange("p n (j e) -> p n j e", e=2)
                    s_o = cs_all[:, :, 1, q, 0:12].rearrange("p n (j e) -> p n j e", e=2)
                    done(v.tensor_tensor(c_o, bcast(trig[:, 0, :, :], 3, 2), bcast(w2_, 1, N16), ALU.mult))
                    done(v.tensor_copy(cs_all[:, :, 0, q, 12:16], bcast(wqk[:, q, 12:16], 1, N16)))
                    done(v.tensor_tensor(s_o[:, :, :, 0], kk[:, 1, :, :], bcast(w2_[:, :, 1], 1, N16), ALU.mult))
                    done(v.tensor_tensor(s_o[:, :, :, 1], trig[:, 1, :, :], bcast(w2_[:, :, 0], 1, N16), ALU.mult))
                    done(v.memset(cs_all[:, :, 1, q, 12:16], 0.0))
                v.memset(grow[:, 3, :], 0.0).then_inc(trig_done, 1)
                dve.wait_ge(trig_done, 1)
            dve.wait_ge(s_init, 3 - 2 * L)
            dve.wait_ge(const_in, 16 * 5)
            if L == 1:
                dve.wait_ge(mod_silu, 1)
                done(v.scalar_tensor_tensor(out=cact[:, :, :], in0=cact[:, :, :], scalar=1.0, in1=cT[:, :, :], op0=ALU.add, op1=ALU.mult))
                v.tensor_scalar(cact[:, :, :], cact[:, :, :], 0.5, None, ALU.mult).then_inc(mod_silu, 1)
            else:
                v.tensor_copy(cact[:, :, :], cT[:, :, :]).then_inc(mod_silu, 2)
            for q in range(4):
                dve.wait_ge(mod_mm, 1 + q // 2)
                src = [T[0], T[1], S[0], S[1]][q]
                done(v.tensor_tensor(modr[:, 384 * q:384 * q + 384], src[0:NB, 0:384], bmod[:, 384 * q:384 * q + 384], ALU.add))
            done(v.tensor_copy(grow[:, 1, :], modr[:, 512:768]))
            done(v.tensor_tensor(grow[:, 0, :], modr[:, 512:768], bo8[:, 0, :], ALU.mult))
            if L == 1:
                done(v.tensor_tensor(grow[:, 3, :], modr[:, 1280:1536], bo8[:, 1, :], ALU.mult))
            v.tensor_copy(grow[:, 2, :], modr[:, 1280:1536]).then_inc(mod_row, 1)
            dve.wait_ge(mod_T, 1)
            for j in range(8):
                src = V[0][:, 8 * j:8 * j + 8]
                out = ab_all[:, :, j]
                if j % 4 < 2:
                    if L == 0:
                        k = (j // 4) * 2 + j % 2
                        ins = v.tensor_scalar(out, src, 1.0, wn[:, k:k + 1], ALU.add, ALU.mult)
                    else:
                        ins = v.tensor_scalar(out, src, 1.0, None, ALU.add)
                else:
                    ins = v.tensor_copy(out, src)
            ins.then_inc(mod_ab, 1)
            def chunk_low(i):
                k, c, m = chunks[i]
                dve.wait_ge(raw_hi, i + 1)
                cols = [x[k][:, :, :].rearrange("p a b -> p (a b)")[:, c:c + m] for x in (hi, lo)]
                v.tensor_tensor(cols[1], raw[i % 2][:, 0:m], cols[0].bitcast(F32), ALU.subtract).then_inc(raw_lo, 1)

            for i in range(early):
                chunk_low(i)

            def norm_stats(st_ok, b, x, st, ag, ms, ms_ok):
                for t in range(TT):
                    ins = v.bn_stats(st[:, t, :], x[:, t, :])
                ins.then_inc(st_ok.sem, 1)
                dve.wait_ge(st_ok.sem, st_ok.at(b, 1))
                v.tensor_copy(held[:, :], mhalf[:, 0:1])
                for t in range(TT):
                    ins = v.bn_aggr(ag[:, t, :], st[:, t, :])
                ins.then_inc(st_ok.sem, 1)
                dve.wait_ge(st_ok.sem, st_ok.at(b, 2))
                if L == 0:
                    v.tensor_tensor(ms, ag[:, :, 0], ag[:, :, 0], ALU.mult).then_inc(st_ok.sem, 1)
                    dve.wait_ge(st_ok.sem, st_ok.at(b, 3))
                    v.scalar_tensor_tensor(out=ms, in0=ms, scalar=cfg["eps"], in1=ag[:, :, 1], op0=ALU.add, op1=ALU.add).then_inc(ms_ok.sem, 1)
                else:
                    v.tensor_scalar(ms, ag[:, :, 1], cfg["eps"], None, ALU.add).then_inc(ms_ok.sem, 1)

            def normed(out, x, ag, rs, out_ok):
                for t in range(TT):
                    if L == 0:
                        ins = v.tensor_scalar(out[:, t, :], x[:, t, :], rs[:, t:t + 1], None, ALU.mult)
                    else:
                        ins = v.tensor_scalar(out[:, t, :], x[:, t, :], ag[:, t, 0:1], rs[:, t:t + 1], ALU.subtract, ALU.mult)
                    ins.then_inc(out_ok.sem, 1)

            def norm1_stats(n):
                dve.wait_ge(x_loaded.sem, x_loaded.at(n, 16))
                norm_stats(stat1, n, x_in, stat, aggr, msq[:, :], ms1)

            def norm1(n):
                dve.wait_ge(rstd1.sem, rstd1.at(n, 1))
                dve.wait_ge(h_full.sem, h_full.at(n, 0))
                normed(xn, x_in, aggr, rstd, xn_ok)

            def norm2_stats(b):
                dve.wait_ge(x2_ok.sem, x2_ok.at(b, TT))
                norm_stats(stat2s, b, x2, stat2, aggr2, msq2[:, :], ms2)

            def norm2(b):
                dve.wait_ge(rs2.sem, rs2.at(b, 1))
                dve.wait_ge(h2_full.sem, h2_full.at(b, 0))
                normed(xn2, x2, aggr2, rstd2, xn2_ok)

            def modulated(n, b, name, out, ab, ok, hi_read, lo_read):
                bank = t_read(dve, n, name)
                dve.wait_ge(hi_read.sem, hi_read.at(b, 0))
                dve.wait_ge(lo_read.sem, lo_read.at(b, 0))
                for ft in range(FT):
                    v.tensor_scalar(out[:, ft, :], bank[:, ft * NTOK:(ft + 1) * NTOK], ab[:, ft:ft + 1], ab[:, 2 + ft:3 + ft],
                                    ALU.mult, ALU.add).then_inc(ok.sem, 1)

            def ot_low(n, i):
                dve.wait_ge(ot_hi.sem, ot_hi.at(n, i + 1))
                dve.wait_ge(pj_gated.sem, pj_gated.at(n, 0))
                for r, c in [(slice(0, P), 0)] if L == 0 else [(slice(0, 64), 0), (slice(64, P), 256)]:
                    ins = v.tensor_tensor(otlo[r, i, :], V[i % 2][r, c:c + NTOK], othi[r, i, :].bitcast(F32), ALU.subtract)
                ins.then_inc(ot_lo.sem, 1)

            def residual1(n, b):
                dve.wait_ge(par2.sem, par2.at(b, 32))
                dve.wait_ge(xr_ok.sem, xr_ok.at(b, 1))
                if L == 0:
                    dve.wait_ge(y0_ok.sem, y0_ok.at(b, 0))
                    dve.wait_ge(xn2_ok.sem, xn2_ok.at(b, 0))
                else:
                    dve.wait_ge(y_ok.sem, y_ok.at(b, 0))
                bank = t_read(dve, n, "pj")
                for t in range(TT):
                    v.tensor_tensor(x2[:, t, :], bank[:, t * D:(t + 1) * D], gates1[:, 1, :], ALU.mult).then_inc(pj_gated.sem, 1)
                for t in range(TT):
                    dve.wait_ge(pj_gated.sem, pj_gated.at(b, t + 1))
                    v.tensor_tensor(x2[:, t, :], x2[:, t, :], xr[:, t, :], ALU.add).then_inc(x2_ok.sem, 1)

            def add_bias2(b):
                dve.wait_ge(par3.sem, par3.at(b, 16))
                dve.wait_ge(xn2_ok.sem, xn2_ok.at(b, TT))
                v.tensor_tensor(x2[:, :, :], x2[:, :, :], bcast(gates2[:, 1, :], 1, TT), ALU.add).then_inc(x2b_ok.sem, 1)

            def residual2(n, b):
                dve.wait_ge(y_stored.sem, y_stored.at(b, 0))
                dve.wait_ge(par3.sem, par3.at(b, 16))
                bank = t_read(dve, n, "w2")
                if L == 0:
                    dve.wait_ge(y0_ok.sem, y0_ok.at(b, 1))
                    part, to = ff, yo
                else:
                    dve.wait_ge(x2b_ok.sem, x2b_ok.at(b, 1))
                    part, to = yo, x2
                for t in range(TT):
                    v.tensor_tensor(part[:, t, :], bank[:, t * D:(t + 1) * D], gates2[:, 0, :], ALU.mult).then_inc(w2_gated.sem, 1)
                for t in range(TT):
                    dve.wait_ge(w2_gated.sem, w2_gated.at(b, t + 1))
                    v.tensor_tensor(yo[:, t, :], part[:, t, :], to[:, t, :], ALU.add).then_inc(y_ok.sem, 1)

            def head_sums(n, t):
                dve.wait_ge(sq_ok.sem, sq_ok.at(n, t + 1))
                v.tensor_reduce(hss[:, t, :], sq[:, t, :].rearrange("p (h d) -> p h d", d=16), AX.X, ALU.add).then_inc(hsum_ok.sem, 1)
                dve.wait_ge(hsum_ok.sem, hsum_ok.at(n, t + 1))
                v.tensor_scalar(hss[:, t, :], hss[:, t, :], 1.0 / 16, cfg["eps"], ALU.mult, ALU.add).then_inc(hss_ok.sem, 1)

            def head_rotate(n, t):
                dve.wait_ge(hr_ok.sem, hr_ok.at(n, t + 1))
                dve.wait_ge(m1_ok.sem, m1_ok.at(n - 1, t + 1))
                dve.wait_ge(qraw_ok.sem, qraw_ok.at(n, t + 1))
                i3 = qraw[:, t, :].rearrange("p (h d) -> p h d", d=16)
                n3 = qn[:, t, :].rearrange("p (h d) -> p h d", d=16)
                v.tensor_tensor(n3, i3, bcast(hr[:, t, :], 2, 16), ALU.mult).then_inc(qn_ok.sem, 1)
                dve.wait_ge(qn_ok.sem, qn_ok.at(n, t + 1))
                dve.wait_ge(par1.sem, par1.at(n, par1.per))
                dve.wait_ge(qf_ok.sem, qf_ok.at(n, t))
                n5 = qn[:, t, :].rearrange("p (q h j e) -> p q h j e", q=2, h=HEADS, e=2)
                m5 = m2[:, :, :].rearrange("p (q h) (j e) -> p q h j e", q=2, e=2)
                s5 = cs[:, t, 1, :, :].rearrange("p q (j e) -> p q j e", e=2)
                for e in range(2):
                    for q in range(2):
                        ins = v.tensor_tensor(m5[:, q, :, :, e], n5[:, q, :, 0:6, 1 - e],
                                              bcast(s5[:, q, 0:6, e], 1, HEADS), ALU.mult)
                ins.then_inc(m2_ok.sem, 1)

            def head_add(n, t):
                dve.wait_ge(m2_ok.sem, m2_ok.at(n, t + 1))
                dve.wait_ge(m1_ok.sem, m1_ok.at(n, t + 1))
                f3 = m1[:, t, :].rearrange("p (h d) -> p h d", d=16)[:, :, 0:12]
                v.tensor_tensor(f3, f3, m2[:, :, :], ALU.add).then_inc(qf_ok.sem, 1)

            def stack_low(n, t):
                dve.wait_ge(qf_ok.sem, qf_ok.at(n, t + 1))
                f = m1[:, t, :].rearrange("p (q h d) -> p q h d", q=2, h=HEADS)
                for q in range(2):
                    dve.wait_ge(st_hi.sem, st_hi.at(n, 2 * t + q + 1))
                    at = 32 if q == 0 else 16
                    v.tensor_tensor(stack[:, t, q, :, at:at + 16], f[:, q], stack[:, t, q, :, 0:16].bitcast(F32), ALU.subtract).then_inc(st_lo.sem, 1)

            def qk_low(n, b, u):
                bank = T[bank_of(n, f"qk{u}")[1]]
                dve.wait_ge(qk_hi.sem, qk_hi.at(b, u + 1))
                dve.wait_ge(s_full.sem, s_full.at(b, 2 * (u - QS + 1)))
                v.tensor_tensor(qklo[:, u % QS, :], bank[:, :], qkhi[:, u % QS, :].bitcast(F32), ALU.subtract).then_inc(qk_lo.sem, 1)

            def maxima(b, u):
                dve.wait_ge(bias_ok.sem, bias_ok.at(b, u))
                for hh in range(2):
                    dve.wait_ge(s_full.sem, s_full.at(b, 2 * u + hh + 1))
                    ins = v.tensor_reduce(negm[:, hh, :], S[hh][:, :].rearrange("p (t k) -> p t k", t=TT), AX.X, ALU.max, negate=True)
                ins.then_inc(max_ok.sem, 1)
                dve.wait_ge(max_ok.sem, max_ok.at(b, u + 1))
                v.tensor_scalar(negb[:, u % 2, :, :], negm[:, :, :], cfg["scale"], None, ALU.mult).then_inc(bias_ok.sem, 1)

            def normalise(b, u):
                dve.wait_ge(ex_ok.sem, ex_ok.at(b, 2 * u + 2))
                v.reciprocal(rinv[:, u % 2, :, :], rsum[:, u % 2, :, :]).then_inc(rd_ok.sem, 1)
                dve.wait_ge(rd_ok.sem, rd_ok.at(b, u + 1))
                for hh in range(2):
                    for t in range(TT):
                        x = pq[:, (2 * u + hh) % 4, t * 256:(t + 1) * 256]
                        ins = v.tensor_scalar(x, x, rinv[:, u % 2, hh, t:t + 1], None, ALU.mult)
                    ins.then_inc(pn_ok.sem, 1)

            def pt_low(b, u):
                dve.wait_ge(av_full.sem, av_full.at(b, u))
                for hh in range(2):
                    dve.wait_ge(p_hi.sem, p_hi.at(b, 2 * u + hh + 1))
                    v.tensor_tensor(pt[1][:, hh, :], PB[hh][:, :], pt[0][:, hh, :].bitcast(F32), ALU.subtract).then_inc(p_lo.sem, 1)

            def v_low(n, b, i):
                bank = T[bank_of(n, f"v{i}")[1]]
                dve.wait_ge(v_hi.sem, v_hi.at(b, v_order.index(i) + 1))
                dve.wait_ge(av_full.sem, av_full.at(b - 1, 4 + 4 * (i % 2)))
                sl = lambda x: x[:, i // 2, (i % 2) * 8:(i % 2) * 8 + 8, :].rearrange("p h d -> p (h d)")
                v.tensor_tensor(sl(vlo), bank[:, :], sl(vhi).bitcast(F32), ALU.subtract).then_inc(v_lo.sem, 1)

            def body(n):
                for u in range(UNITS):
                    if L == 0:
                        if u == 0:
                            for f in at(n, 1):
                                dve.wait_ge(par1.sem, par1.at(f, par1.per))
                                modulated(n - 1, f, "xnT", hfull, ab1, h_full, h_hi, h_lo)
                        if u == 4:
                            for f in at(n, 1):
                                stack_low(f, 0)
                        if u == 5:
                            for f in at(n, 1):
                                stack_low(f, 1)
                            for b in at(n, -1):
                                modulated(n, b, "h2T", h2full, ab2, h2_full, h2_hi, h2_lo)
                    else:
                        for m, v_ in unit_at(n, u - 1):
                            pt_low(m, v_)
                        if u == 3:
                            for b in at(n, -1):
                                residual1(n, b)
                        if u != 2:
                            for m, v_ in unit_at(n, u - 2):
                                if u == 3:
                                    ot_low(m, 0)
                                ot_low(m, v_)
                        if u == 2:
                            for d in at(n, -2):
                                residual2(n, d)
                        if u == 4:
                            for f in at(n, 1):
                                dve.wait_ge(par1.sem, par1.at(f, par1.per))
                                modulated(n, f, "xnT", hfull, ab1, h_full, h_hi, h_lo)
                            for b in at(n, -1):
                                norm2(b)
                        if u == 5:
                            for b in at(n, -1):
                                modulated(n, b, "h2T", h2full, ab2, h2_full, h2_hi, h2_lo)
                    for m, v_ in unit_at(n, u + 2):
                        maxima(m, v_)
                    if L == 0 and u == 0:
                        for d in at(n, -2):
                            swiglu(n - 1, d, 4)
                    if L == 0 and u >= 6:
                        for b in at(n, -1):
                            swiglu(n, b, 2 * u - 12)
                    for m, v_ in unit_at(n, u + 1):
                        normalise(m, v_)
                    if L == 0 and u == 3:
                        for f in at(n, 1):
                            head_rotate(f, 0)
                    if L == 0:
                        if u == 1:
                            for f in at(n, 1):
                                head_sums(f, 0)
                                head_sums(f, 1)
                        if u == 2:
                            for b in at(n, -1):
                                residual1(n, b)
                                norm2_stats(b)
                        if u == 3:
                            for f in at(n, 1):
                                head_add(f, 0)
                                head_rotate(f, 1)
                            for b in at(n, -1):
                                norm2(b)
                            for d in at(n, -2):
                                residual2(n, d)
                        if u == 4:
                            for f in at(n, 1):
                                head_add(f, 1)
                            for m in at(n, 0):
                                ot_low(m, 0)
                        if u == 0:
                            for b in at(n, -1):
                                ot_low(b, 1)
                            for e in at(n, 2):
                                norm1_stats(e)
                        if u == 7:
                            for e in at(n, 2):
                                norm1(e)
                    else:
                        for m, v_ in unit_at(n, u + 3):
                            qk_low(n, m, v_)
                        if u == 0:
                            for m in at(n, 0):
                                v_low(n, m, 1)
                                v_low(n, m, 3)
                        if u == 1:
                            for f in at(n, 1):
                                norm1_stats(f)
                        if u == 2:
                            for f in at(n, 1):
                                norm1(f)
                        if u == 3:
                            for b in at(n, -1):
                                norm2_stats(b)
                        if u == 4:
                            for b in at(n, -1):
                                add_bias2(b)
                        if u == 5:
                            for f in at(n, 1):
                                v_low(n, f, 0)
                        if u == 7:
                            for f in at(n, 1):
                                v_low(n, f, 2)

            def swiglu(n, b, i):
                for j in (i, i + 1):
                    bank = T[bank_of(n, f"hid{j}")[1]]
                    dve.wait_ge(tanh_ok.sem, tanh_ok.at(b, j + 1))
                    v.scalar_tensor_tensor(out=t1[:, j % 2, :], in0=th[:, j % 2, :], scalar=1.0, in1=bank[:, 0:256],
                                           op0=ALU.add, op1=ALU.mult).then_inc(sw_ok.sem, 1)
                for j in (i, i + 1):
                    bank = T[bank_of(n, f"hid{j}")[1]]
                    dve.wait_ge(sw_ok.sem, sw_ok.at(b, j + 1))
                    dve.wait_ge(a_lo.sem, a_lo.at(b, j - 1))
                    v.scalar_tensor_tensor(out=afull[:, j % 2, :], in0=bank[:, 256:512], scalar=0.5, in1=t1[:, j % 2, :],
                                           op0=ALU.mult, op1=ALU.mult).then_inc(a_full.sem, 1)

            bodies(dve, body, chunk_low)

        @block.tensor
        def _(pe):
            mm = nc.tensor.matmul
            pe.wait_ge(mod_silu, 2)
            pe.wait_ge(s_ident, 2)
            for h in range(2):
                pe.wait_ge(mod_in[h], 16)
                for j in range(2):
                    bank = (T, S)[h][j]
                    modw = raw[h][:, 0:NMOD].rearrange("p (k n) -> p k n", k=FT)
                    for k in range(FT):
                        ins = mm(bank[0:NB, 0:384], cact[:, k, :], modw[:, k, j * 384:(j + 1) * 384], start=(k == 0), stop=(k == FT - 1))
                ins.then_inc(mod_mm, 1)
            pe.wait_ge(mod_row, 1)
            comps = [256, 384, 0, 128, 1024, 1152, 768, 896]
            for j, c in enumerate(comps):
                ins = nc.tensor.transpose(V[0][:, 8 * j:8 * j + 8], modr[:, c:c + P], ident[0:NB, 0:NB])
            ins.then_inc(mod_T, 1)
            pe.wait_ge(mod_ab, 1)
            pe.wait_ge(s_init, 3 - 2 * L)
            pe.wait_ge(raw_lo, early)

            def split_mm(out, wts, mov, first, last):
                parts = [(0, 0), (1, 0), (0, 1)]
                for j, (a_, b_) in enumerate(parts):
                    ins = mm(out, wts[a_], mov[b_], start=first and j == 0, stop=last and j == 2)
                return ins

            def xnT(n, name, src, ok, b):
                pe.wait_ge(ok.sem, ok.at(b, TT))
                bank, full = t_claim(pe, n, name)
                for ft in range(FT):
                    for t in range(TT):
                        c = ft * NTOK + t * P
                        ins = nc.tensor.transpose(bank[:, c:c + P], src[:, t, ft * P:(ft + 1) * P], ident[:, :])
                ins.then_inc(full, 1)

            def tok_major(out, xs, ws, t, c0, c1, kt):
                for k in range(kt):
                    ins = split_mm(out, [x[:, k, t * P:(t + 1) * P] for x in xs],
                                   [y[:, k, c0:c1] for y in ws], k == 0, k == kt - 1)
                return ins

            wp = {k: (hi[k], lo[k]) for k in shapes}

            def qk0(n, b, t):
                pe.wait_ge(h_lo.sem, h_lo.at(b, FT))
                pe.wait_ge(h_hi.sem, h_hi.at(b, FT))
                bank, full = t_claim(pe, n, f"qk{t}")
                tok_major(bank[:, :], (hhi, hlo), wp["wqkv"], t, 0, 512, FT).then_inc(full, 1)

            def values(n, b, i):
                pe.wait_ge(h_lo.sem, h_lo.at(b, FT))
                pe.wait_ge(h_hi.sem, h_hi.at(b, FT))
                if L == 0:
                    bank, full = t_claim(pe, n, "v")
                    for t in range(TT):
                        ins = tok_major(bank[:, t * D:(t + 1) * D], (hhi, hlo), wp["wqkv"], t, 512, 768, FT)
                    ins.then_inc(full, 1)
                else:
                    bank, full = t_claim(pe, n, f"v{i}")
                    c = 2048 + 512 * (i % 2)
                    tok_major(bank[:, :], (hhi, hlo), wp["wqkv"], i // 2, c, c + 512, FT).then_inc(full, 1)

            def qk1(n, b, u):
                pe.wait_ge(h_lo.sem, h_lo.at(b, FT))
                pe.wait_ge(h_hi.sem, h_hi.at(b, FT))
                bank, full = t_claim(pe, n, f"qk{u}")
                for q in range(2):
                    c = q * 1024 + u * P
                    for k in range(FT):
                        ins = split_mm(bank[:, q * 256:(q + 1) * 256], [x[:, k, c:c + P] for x in wp["wqkv"]],
                                       [x[:, k, :] for x in (hhi, hlo)], k == 0, k == FT - 1)
                ins.then_inc(full, 1)

            def project(n, b):
                if isinstance(b, int) and b == 0:
                    pe.wait_ge(raw_lo, len(chunks))
                pe.wait_ge(ot_lo.sem, ot_lo.at(b, ot_lo.per))
                pe.wait_ge(ot_hi.sem, ot_hi.at(b, ot_hi.per))
                bank, full = t_claim(pe, n, "pj")
                for t in range(TT):
                    ins = tok_major(bank[:, t * D:(t + 1) * D], (othi, otlo), wp["wo"], t, 0, D, KO)
                ins.then_inc(full, 1)

            def hidden(n, b, tiles_):
                pe.wait_ge(h2_lo.sem, h2_lo.at(b, FT))
                pe.wait_ge(h2_hi.sem, h2_hi.at(b, FT))
                for i in tiles_:
                    bank, full = t_claim(pe, n, f"hid{i}")
                    for j in range(2):
                        ws, c = (wp["w3" if j else "w1"], i * P) if L == 0 else (wp["w1"], (2 * i + j) * P)
                        for k in range(FT):
                            ins = split_mm(bank[:, j * 256:(j + 1) * 256], [x[:, k, c:c + P] for x in ws],
                                           [x[:, k, :] for x in (h2hi, h2lo)], k == 0, k == FT - 1)
                    ins.then_inc(full, 1)

            def down(n, b):
                pe.wait_ge(a_lo.sem, a_lo.at(b, HID))
                pe.wait_ge(a_hi.sem, a_hi.at(b, HID))
                bank, full = t_claim(pe, n, "w2")
                for t in range(TT):
                    ins = tok_major(bank[:, t * D:(t + 1) * D], (ahi, alo), wp["w2"], t, 0, D, HID)
                ins.then_inc(full, 1)

            def qkT0(n, b, i):
                half, t, q = i // 4, (i // 2) % 2, i % 2
                pe.wait_ge(st_lo.sem, st_lo.at(b, 2 * t + 2))
                bank, full = t_claim(pe, n, f"qkT{i}")
                for j in range(4):
                    u = 4 * half + j
                    ins = nc.tensor.transpose(bank[:, j * P:(j + 1) * P],
                                              stack[:, t, q, 2 * u:2 * u + 2, :].rearrange("p h r -> p (h r)").bitcast(F32), ident[:, :])
                ins.then_inc(full, 1)

            def head_rows(u, hh):
                if L == 0:
                    r = slice(64 * hh, 64 * hh + QK_ROWS)
                    return [(qkT[r, 0, u, :], qkT[r, 1, u, :])]
                r = slice(64 * hh, 64 * hh + 64)
                q = [x[r, u % QS, 0:256] for x in (qkhi, qklo)]
                k = [x[r, u % QS, 256:512] for x in (qkhi, qklo)]
                return [(q[0], k[0]), (q[1], k[0]), (q[0], k[1])]

            def scores(n, u):
                if L == 0:
                    pe.wait_ge(qkT_ok.sem, qkT_ok.at(n, 4 if u < 4 else 8))
                else:
                    pe.wait_ge(qk_lo.sem, qk_lo.at(n, u + 1))
                for hh in range(2):
                    pe.wait_ge(ex_ok.sem, ex_ok.at(n, 2 * u + hh - 1))
                    prods = head_rows(u, hh)
                    for t in range(TT):
                        for j, (q, k) in enumerate(prods):
                            ins = mm(S[hh][:, t * 256:(t + 1) * 256], q[:, t * P:(t + 1) * P], k, start=(j == 0), stop=(j == len(prods) - 1))
                    ins.then_inc(s_full.sem, 1)

            def transposes(n, u):
                for hh in range(2):
                    pe.wait_ge(pn_ok.sem, pn_ok.at(n, 2 * u + hh + 1))
                    pe.wait_ge(p_ok.sem, p_ok.at(n, 2 * u + hh - 1))
                    for kt in range(TT):
                        for t in range(TT):
                            ins = nc.tensor.transpose(PB[hh][:, kt * 256 + t * P:kt * 256 + (t + 1) * P],
                                                      pq[:, (2 * u + hh) % 4, t * 256 + kt * P:t * 256 + (kt + 1) * P], ident[:, :])
                    ins.then_inc(p_full.sem, 1)

            def weigh(n, u):
                pe.wait_ge(v_ok.sem, v_ok.at(n, 2 if L == 0 or u < 4 else 4))
                if L == 0:
                    pe.wait_ge(ot_lo.sem, ot_lo.at(n - (u < 4), 2 if u < 4 else 1))
                else:
                    pe.wait_ge(ot_lo.sem, ot_lo.at(n, u - 1))
                for hh in range(2):
                    pe.wait_ge(p_ok.sem, p_ok.at(n, 2 * u + hh + 1))
                    h = 2 * u + hh
                    for kt in range(TT):
                        ks = slice(kt * 256, (kt + 1) * 256)
                        if L == 0:
                            r = 32 * (u % 4)
                            ins = mm(V[u // 4][r:r + 32, 0:NTOK], vz[:, kt, h, :], pt[0][:, hh, ks], start=(hh + kt == 0), stop=(hh + kt == 2))
                        else:
                            out = V[u % 2][:, 256 * hh:256 * hh + 256]
                            ins = split_mm(out, [x[:, kt, 2 * u:2 * u + 2, :].rearrange("p h d -> p (h d)") for x in (vhi, vlo)], [x[:, hh, ks] for x in pt], kt == 0, kt == TT - 1)
                ins.then_inc(av_full.sem, 1)

            def body(n):
                for u in range(UNITS):
                    for m, v_ in unit_at(n, u + 2):
                        scores(m, v_)
                    if L == 1:
                        for m, v_ in unit_at(n, u + 3):
                            qk1(n, m, v_)
                    for m, v_ in unit_at(n, u - 1):
                        weigh(m, v_)
                    for m, v_ in unit_at(n, u):
                        transposes(m, v_)
                    if L == 0:
                        if u == 0:
                            for f in at(n, 1):
                                qk0(n, f, 0)
                                qk0(n, f, 1)
                        if u == 1:
                            for f in at(n, 1):
                                values(n, f, None)
                            for b in at(n, -1):
                                project(n, b)
                        if u == 2:
                            for d in at(n, -2):
                                down(n, d)
                        if u >= 4:
                            for f in at(n, 1):
                                qkT0(n, f, 2 * u - 8)
                                qkT0(n, f, 2 * u - 7)
                        if u == 4:
                            for b in at(n, -1):
                                xnT(n, "h2T", xn2, xn2_ok, b)
                        if u == 7:
                            for g in at(n, 2):
                                xnT(n, "xnT", xn, xn_ok, g)
                        if u >= 5:
                            for b in at(n, -1):
                                hidden(n, b, (2 * u - 10, 2 * u - 9))
                    else:
                        if u == 0:
                            for m in at(n, 0):
                                values(n, m, 1)
                                values(n, m, 3)
                        if u == 1:
                            for d in at(n, -2):
                                down(n, d)
                        if u == 2:
                            for b in at(n, -1):
                                project(n, b)
                        if u == 3:
                            for f in at(n, 1):
                                xnT(n, "xnT", xn, xn_ok, f)
                        if u == 4:
                            for b in at(n, -1):
                                xnT(n, "h2T", xn2, xn2_ok, b)
                        if u == 5:
                            for f in at(n, 1):
                                values(n, f, 0)
                        if u == 7:
                            for f in at(n, 1):
                                values(n, f, 2)
                        if u >= 6:
                            for b in at(n, -1):
                                hidden(n, b, (2 * u - 12, 2 * u - 11))

            bodies(pe, body)


def build(nc, ins, out):
    x = ins["x"].rearrange("b (t p) d -> b p t d", p=P)
    y = out.rearrange("b (t p) d -> b p t d", p=P)
    mid = nc.dram_tensor("tokens_between", [NB, NTOK, D], F32, kind="Internal").ap().rearrange("b (t p) d -> b p t d", p=P)
    layers = []
    for L, names in enumerate([
        dict(wqkv="qkvT0", wo="projT0", w1="w1T0", w3="w3T0", w2="w2T0", wmod="adaT0"),
        dict(wqkv="W_qkv", wo="W_out", w1="W1", w2="W2", wmod="W_mod"),
    ]):
        w = {k: ins[v] for k, v in names.items()}
        w["cT"] = ins["cT"].rearrange("p (k b) -> p k b", k=FT)
        layers.append(w)
    layers[0] |= dict(bmod=ins["ada_b"], bo=ins["proj_b"], n1=ins["norm1"], n2=ins["norm2"], pos=ins["pos"],
                      qn=ins["q_norm"], kn=ins["k_norm"])
    layers[1] |= dict(bmod=ins["b_mod"], bo=ins["b_out"], b2=ins["b2"], b1=ins["b1"])
    for L in range(2):
        gates = nc.dram_tensor(f"gates{L}", [NB, 4 * D], F32, kind="Internal").ap()
        scratch = dict(gates=gates)
        build_layer(nc, L, (x, mid)[L], (mid, y)[L], layers[L], scratch)


def kernel(**inputs):
    import numpy as _np
    import concourse.bacc as _bacc
    from concourse import mybir as _mybir
    from concourse.bass_utils import run_bass_kernel_spmd as _run

    def arr(name):
        return _np.asarray(inputs[name])

    def tiles(a):
        return a.reshape(-1, P, a.shape[1]).transpose(1, 0, 2).reshape(P, -1)

    def pad(a, n, axis):
        w = [(0, 0)] * a.ndim
        w[axis] = (0, n - a.shape[axis])
        return _np.pad(a, w)

    L0, L1 = "L0_cond_", "L1_cond_"
    host = dict(
        x=arr("x"),
        cT=tiles(arr("cond_1024").T),
        pos=arr("fside_BxSx3_0").reshape(NB * TT, P, 3).transpose(1, 0, 2),
        qkvT0=tiles(arr(L0 + "qkv_w").T), projT0=tiles(arr(L0 + "proj_w").T),
        w1T0=tiles(pad(arr(L0 + "w1").T, FF0P, 1)), w3T0=tiles(pad(arr(L0 + "w3").T, FF0P, 1)),
        w2T0=tiles(pad(arr(L0 + "w2").T, FF0P, 0)), adaT0=tiles(arr(L0 + "ada_w").T),
        ada_b=arr(L0 + "ada_b"), proj_b=arr(L0 + "proj_b"),
        norm1=arr(L0 + "norm1_w").reshape(FT, P).T, norm2=arr(L0 + "norm2_w").reshape(FT, P).T,
        q_norm=arr(L0 + "q_norm_w"), k_norm=arr(L0 + "k_norm_w"),
        W_mod=tiles(arr(L1 + "W_mod")), b_mod=arr(L1 + "b_mod"), W_qkv=tiles(arr(L1 + "W_qkv")), W_out=tiles(arr(L1 + "W_out")),
        b_out=arr(L1 + "b_out"), W1=tiles(arr(L1 + "W1")), b1=arr(L1 + "b1").reshape(8, P).T, W2=tiles(arr(L1 + "W2")), b2=arr(L1 + "b2"),
    )
    nc = _bacc.Bacc("TRN2", target_bir_lowering=False, num_devices=1)
    arrays, ins = {}, {}
    for name, a in host.items():
        a = _np.ascontiguousarray(a)
        arrays[f"in_{name}"] = a
        ins[name] = nc.dram_tensor(f"in_{name}", a.shape, _mybir.dt.from_np(a.dtype), kind="ExternalInput").ap()
    out = nc.dram_tensor("out", (NB, NTOK, D), F32, kind="ExternalOutput").ap()
    build(nc, ins, out)
    r = _run(nc, [arrays], core_ids=[0])
    return r.results[0]["out"]
```
